# Optimizing a Trainium2 kernel written in Bass

```python
import numpy as np
import jax
import jax.numpy as jnp

def _softmax(x, axis=-1):
    return jax.nn.softmax(x, axis=axis)

def _gelu(x):
    return jax.nn.gelu(x, approximate=True)

def _silu(x):
    return jax.nn.silu(x)

def _sigmoid(x):
    return jax.nn.sigmoid(x)

def _layernorm(x, axis=-1, eps=1e-05):
    m = jnp.mean(x, axis=axis, keepdims=True)
    v = jnp.var(x, axis=axis, keepdims=True)
    return (x - m) / jnp.sqrt(v + eps)

def _scatter_add(tgt, idx, src, axis=0):
    return tgt.at[idx].add(src)

def _segment_sum(src, seg, n):
    return jax.ops.segment_sum(src, seg, n)
kernel_name = 'mk_macaron_d1_jaxref_r2_a7ff87'

def setup_inputs(seed: int=0):
    np.random.seed(seed)
    _w = jnp.asarray

    def _L0_attn_setup():
        import jax, jax.numpy as jnp
        import numpy as np
        D_MODEL = 1024
        D_STATE = 16
        KER = 4
        DT_RANK = D_MODEL // 16
        B_SZ = 2
        SEQ = 512

        def _mamba(x, W_in, conv_w, conv_b, W_xproj, W_dt, b_dt, A_log, Dskip, W_out):
            Bsz, L, dm = x.shape
            d_state = A_log.shape[1]
            dt_rank = W_dt.shape[1]
            K = conv_w.shape[1]
            xz = x @ W_in.T
            u, z = jnp.split(xz, 2, axis=-1)
            up = jnp.pad(u, ((0, 0), (K - 1, 0), (0, 0)))
            conv = conv_b + sum((conv_w[:, k] * up[:, k:k + L, :] for k in range(K)))
            u = jax.nn.silu(conv)
            x_dbl = u @ W_xproj.T
            dt_r = x_dbl[..., :dt_rank]
            Bm = x_dbl[..., dt_rank:dt_rank + d_state]
            Cm = x_dbl[..., dt_rank + d_state:]
            dt = jax.nn.softplus(dt_r @ W_dt.T + b_dt)
            A = -jnp.exp(A_log)
            dA = jnp.exp(dt[..., None] * A)
            dBu = dt[..., None] * Bm[:, :, None, :] * u[..., None]

            def step(h, inp):
                dA_t, dBu_t, C_t = inp
                h = dA_t * h + dBu_t
                y_t = jnp.einsum('bdn,bn->bd', h, C_t)
                return (h, y_t)
            h0 = jnp.zeros((Bsz, dm, d_state), dtype=x.dtype)
            _, ys = jax.lax.scan(step, h0, (dA.swapaxes(0, 1), dBu.swapaxes(0, 1), Cm.swapaxes(0, 1)))
            y = ys.swapaxes(0, 1) + u * Dskip
            y = y * jax.nn.silu(z)
            return y @ W_out.T
        key = jax.random.key(seed)
        ks = jax.random.split(key, 8)
        s = 0.02
        return {'x': jax.random.normal(ks[0], (B_SZ, SEQ, D_MODEL), jnp.float32), 'W_in': jax.random.normal(ks[1], (2 * D_MODEL, D_MODEL), jnp.float32) * s, 'conv_w': jax.random.normal(ks[2], (D_MODEL, KER), jnp.float32) * s, 'conv_b': jnp.zeros((D_MODEL,), jnp.float32), 'W_xproj': jax.random.normal(ks[3], (DT_RANK + 2 * D_STATE, D_MODEL), jnp.float32) * s, 'W_dt': jax.random.normal(ks[4], (D_MODEL, DT_RANK), jnp.float32) * s, 'b_dt': jax.random.uniform(ks[5], (D_MODEL,), jnp.float32, -4.0, -2.0), 'A_log': jnp.log(jnp.broadcast_to(jnp.arange(1, D_STATE + 1, dtype=jnp.float32), (D_MODEL, D_STATE))), 'Dskip': jnp.ones((D_MODEL,), jnp.float32), 'W_out': jax.random.normal(ks[6], (D_MODEL, D_MODEL), jnp.float32) * s}
    _L0_attn_in = _L0_attn_setup()

    def _L0_ffn_setup():
        import jax, jax.numpy as jnp
        import numpy as np
        B, S, D_IN, D_OUT = (4, 1024, 1024, 1024)
        EPS = 1e-10
        key = jax.random.key(seed)
        kx, kw, kb = jax.random.split(key, 3)
        x = jax.random.normal(kx, (B, S, D_IN), dtype=jnp.float32)
        weight = jax.random.normal(kw, (D_OUT, D_IN), dtype=jnp.float32) * 0.02
        bias = jax.random.normal(kb, (D_OUT,), dtype=jnp.float32) * 0.02
        return {'x': x, 'weight': weight, 'bias': bias}
    _L0_ffn_in = _L0_ffn_setup()
    _d = {'L0_attn_x': _L0_attn_in['x'], 'L0_attn_W_in': _L0_attn_in['W_in'], 'L0_attn_conv_w': _L0_attn_in['conv_w'], 'L0_attn_conv_b': _L0_attn_in['conv_b'], 'L0_attn_W_xproj': _L0_attn_in['W_xproj'], 'L0_attn_W_dt': _L0_attn_in['W_dt'], 'L0_attn_b_dt': _L0_attn_in['b_dt'], 'L0_attn_A_log': _L0_attn_in['A_log'], 'L0_attn_Dskip': _L0_attn_in['Dskip'], 'L0_attn_W_out': _L0_attn_in['W_out'], 'L0_ffn_weight': _L0_ffn_in['weight'], 'L0_ffn_bias': _L0_ffn_in['bias']}
    _x0 = _d['L0_attn_x']
    _d['L0_attn_x'] = jax.random.normal(jax.random.fold_in(jax.random.key(seed), 1), (1, 4096, 1024), dtype=_x0.dtype)
    del _x0
    return _d

def reference(L0_attn_x, L0_attn_W_in, L0_attn_conv_w, L0_attn_conv_b, L0_attn_W_xproj, L0_attn_W_dt, L0_attn_b_dt, L0_attn_A_log, L0_attn_Dskip, L0_attn_W_out, L0_ffn_weight, L0_ffn_bias):

    def _L0_attn_ref(x, W_in, conv_w, conv_b, W_xproj, W_dt, b_dt, A_log, Dskip, W_out):
        import jax, jax.numpy as jnp
        import numpy as np
        D_MODEL = 1024
        D_STATE = 16
        KER = 4
        DT_RANK = D_MODEL // 16
        B_SZ = 2
        SEQ = 512

        def _mamba(x, W_in, conv_w, conv_b, W_xproj, W_dt, b_dt, A_log, Dskip, W_out):
            Bsz, L, dm = x.shape
            d_state = A_log.shape[1]
            dt_rank = W_dt.shape[1]
            K = conv_w.shape[1]
            xz = x @ W_in.T
            u, z = jnp.split(xz, 2, axis=-1)
            up = jnp.pad(u, ((0, 0), (K - 1, 0), (0, 0)))
            conv = conv_b + sum((conv_w[:, k] * up[:, k:k + L, :] for k in range(K)))
            u = jax.nn.silu(conv)
            x_dbl = u @ W_xproj.T
            dt_r = x_dbl[..., :dt_rank]
            Bm = x_dbl[..., dt_rank:dt_rank + d_state]
            Cm = x_dbl[..., dt_rank + d_state:]
            dt = jax.nn.softplus(dt_r @ W_dt.T + b_dt)
            A = -jnp.exp(A_log)
            dA = jnp.exp(dt[..., None] * A)
            dBu = dt[..., None] * Bm[:, :, None, :] * u[..., None]

            def step(h, inp):
                dA_t, dBu_t, C_t = inp
                h = dA_t * h + dBu_t
                y_t = jnp.einsum('bdn,bn->bd', h, C_t)
                return (h, y_t)
            h0 = jnp.zeros((Bsz, dm, d_state), dtype=x.dtype)
            _, ys = jax.lax.scan(step, h0, (dA.swapaxes(0, 1), dBu.swapaxes(0, 1), Cm.swapaxes(0, 1)))
            y = ys.swapaxes(0, 1) + u * Dskip
            y = y * jax.nn.silu(z)
            return y @ W_out.T
        return _mamba(x, W_in, conv_w, conv_b, W_xproj, W_dt, b_dt, A_log, Dskip, W_out)

    def _L0_ffn_ref(x, weight, bias):
        import jax, jax.numpy as jnp
        import numpy as np
        B, S, D_IN, D_OUT = (4, 1024, 1024, 1024)
        EPS = 1e-10
        scale = jnp.mean(jnp.abs(weight))
        w_t = jnp.clip(jnp.round(weight / (scale + EPS)), -1.0, 1.0)
        w_ste = weight + jax.lax.stop_gradient(w_t * scale - weight)
        return jnp.einsum('bsi,oi->bso', x, w_ste) + bias
    x = L0_attn_x
    x = x + 0.5 * _L0_ffn_ref(_layernorm(x, axis=-1), L0_ffn_weight, L0_ffn_bias)
    x = x + _L0_attn_ref(_layernorm(x, axis=-1), L0_attn_W_in, L0_attn_conv_w, L0_attn_conv_b, L0_attn_W_xproj, L0_attn_W_dt, L0_attn_b_dt, L0_attn_A_log, L0_attn_Dskip, L0_attn_W_out)
    x = x + 0.5 * _L0_ffn_ref(_layernorm(x, axis=-1), L0_ffn_weight, L0_ffn_bias)
    return x

_drawn_inputs = setup_inputs


def setup_inputs(seed=0):
    import zlib

    import numpy as np

    out = dict(_drawn_inputs(seed))
    spreads = {'L0_attn_conv_b': (0.0, 0.528), 'L0_attn_Dskip': (1.0, 0.6)}
    factors = {'L0_attn_W_in': 4.196,
     'L0_attn_conv_w': 8.0,
     'L0_attn_W_xproj': 8.0,
     'L0_attn_W_dt': 8.0,
     'L0_attn_b_dt': 8.0,
     'L0_attn_A_log': 8.0,
     'L0_attn_W_out': 3.609,
     'L0_ffn_bias': 3.042}
    for name, (base, spread) in spreads.items():
        noise = np.random.default_rng([zlib.crc32(name.encode()), seed]).standard_normal(out[name].shape)
        drawn = base * np.exp(spread * noise) if base else spread * noise
        out[name] = jnp.asarray(drawn.astype(out[name].dtype))
    for name, factor in factors.items():
        out[name] = (out[name] * factor).astype(out[name].dtype)
    return out
```

```python
from contextlib import ExitStack

import concourse.bass as bass
from concourse import mybir

ALU = mybir.AluOpType
ACT = mybir.ActivationFunctionType
AX_X = mybir.AxisListType.X
F32 = mybir.dt.float32
F16 = mybir.dt.float16
I32 = mybir.dt.int32
RADD = bass.bass_isa.ReduceOp.add
RABSMAX = bass.bass_isa.ReduceOp.absmax

P = 128
L, D = 4096, 1024
NS = 16
R = 64
G = D // P
HALF = 512
T1 = 512
C1 = L // T1
TT1 = T1 // P
T2 = 256
C2 = L // T2
TT2 = T2 // P
XS = 512.0
WS = 8192.0
EXPONENT = 0x7F800000
TINY = 1e-30
EPS = 1e-5
EPS_FFN = 1e-10
ROUND = 1.5 * 2.0 ** 23


def wait(eng, sem, count):
    if isinstance(count, int) and count <= 0:
        return
    eng.wait_ge(sem, count)


def wait_alone(eng, sem, count):
    if not isinstance(count, int):
        eng.wait_ge(sem, 1)
    wait(eng, sem, count)


def prepare_weights(nc, sem, w_ffn, w_in, w_out, tern, wu, consts, ident, ident16, split_dram):
    srcs = [w_ffn.rearrange("(k p) m -> p k m", p=P),
            w_in.rearrange("(k p) m -> p k m", p=P)[:, :, 0:D],
            w_in.rearrange("(k p) m -> p k m", p=P)[:, :, D:2 * D],
            w_out.rearrange("(k p) m -> p k m", p=P)]
    with ExitStack() as ctx:
        def sb(name, shape, dt):
            return ctx.enter_context(nc.sbuf_tensor(name, shape, dt))

        stage = [sb(f"stage{i}", [P, G, D], F32) for i in range(2)]
        parts = sb("parts", [P, 2, G, D], F16)
        part = sb("part", [P, 4], F32)
        total = sb("total", [P, 4], F32)
        tmp = sb("tmp", [P, 4, 4], F32)

        w_loaded = [sem(f"w_loaded{i}") for i in range(4)]
        part_done, total_done, small = sem("w_part_done"), sem("w_total_done"), sem("w_small")
        factor_done, hi_done, lo_done = sem("w_factor_done"), sem("w_hi_done"), sem("w_lo_done")
        tern_step, parts_stored, ident_step = sem("tern_step"), sem("w_parts_stored"), sem("ident_step")

        with nc.Block() as block:
            @block.sync
            def _(sp):
                for m in range(4):
                    if m == 2:
                        sp.wait_ge(tern_step, 3)
                    if m == 3:
                        sp.wait_ge(hi_done, 1)
                        sp.wait_ge(lo_done, 1)
                    sp.dma_start(stage[m % 2][:], srcs[m]).then_inc(w_loaded[m], 16)
                for m in (2, 3):
                    sp.wait_ge(hi_done, m)
                    sp.wait_ge(lo_done, m)
                    sp.dma_start(split_dram[m - 2], parts[:].rearrange("p a k m -> p (a k m)")).then_inc(parts_stored, 16)
                sp.wait_ge(parts_stored, 32)

            @block.gpsimd
            def _(pool):
                nc.gpsimd.memset(consts["minus_half"], -0.5)
                nc.gpsimd.memset(consts["one"], 1.0)
                nc.gpsimd.memset(ident[:], 0.0).then_inc(ident_step, 1)
                pool.wait_ge(ident_step, 1)
                nc.gpsimd.affine_select(out=ident[:], in_=ident[:], compare_op=ALU.not_equal, fill=1.0, base=0,
                                        pattern=[[-1, P]], channel_multiplier=1).then_inc(ident_step, 1)
                pool.wait_ge(ident_step, 2)
                nc.gpsimd.tensor_copy(ident16[:], ident[:]).then_inc(ident_step, 1)
                for m in range(4):
                    pool.wait_ge(part_done, m + 1)
                    nc.gpsimd.partition_all_reduce(total[:, m:m + 1], part[:, m:m + 1], P,
                                                   RADD if m == 0 else RABSMAX).then_inc(total_done, 1)

            @block.scalar
            def _(act):
                for m in range(1, 4):
                    hi = wu[0] if m == 1 else parts[:, 0]
                    act.wait_ge(factor_done, m)
                    if m == 3:
                        act.wait_ge(parts_stored, 16)
                    nc.scalar.activation(hi, stage[m % 2][:], ACT.Copy, scale=tmp[:, m, 2:3]).then_inc(hi_done, 1)

            @block.vector
            def _(dve):
                steps = [0]

                def link(ins):
                    steps[0] += 1
                    ins.then_inc(small, 1)
                    dve.wait_ge(small, steps[0])

                def reduce(m):
                    dve.wait_ge(w_loaded[m], 16)
                    nc.vector.tensor_reduce(part[:, m:m + 1], stage[m % 2][:].rearrange("p k m -> p (k m)"), AX_X,
                                            ALU.add if m == 0 else ALU.max,
                                            apply_absolute_value=True).then_inc(part_done, 1)

                def ternary():
                    dve.wait_ge(total_done, 1)
                    link(nc.vector.tensor_scalar(tmp[:, 0, 0:1], total[:, 0:1], 1.0 / (D * D), None, ALU.mult))
                    link(nc.vector.tensor_scalar(tmp[:, 0, 1:2], tmp[:, 0, 0:1], EPS_FFN, None, ALU.add))
                    link(nc.vector.reciprocal(tmp[:, 0, 2:3], tmp[:, 0, 1:2]))
                    link(nc.vector.tensor_scalar(consts["ffn_scale"], tmp[:, 0, 0:1], 0.5 / XS, None, ALU.mult))
                    w = stage[0][:].rearrange("p k m -> p (k m)")
                    nc.vector.tensor_scalar(w, w, tmp[:, 0, 2:3], -1.0, ALU.mult, ALU.max).then_inc(tern_step, 1)
                    dve.wait_ge(tern_step, 1)
                    nc.vector.tensor_scalar(w, w, 1.0, ROUND, ALU.min, ALU.add).then_inc(tern_step, 1)
                    dve.wait_ge(tern_step, 2)
                    nc.vector.tensor_scalar(tern[:].rearrange("p k m -> p (k m)"), w, -ROUND, None,
                                            ALU.add).then_inc(tern_step, 1)

                def factor(m):
                    dve.wait_ge(total_done, m + 1)
                    link(nc.vector.tensor_scalar(tmp[:, m, 0:1], total[:, m:m + 1], TINY, None, ALU.max))
                    link(nc.vector.tensor_scalar(tmp[:, m, 1:2].bitcast(I32), tmp[:, m, 0:1].bitcast(I32),
                                                 EXPONENT, None, ALU.bitwise_and))
                    link(nc.vector.reciprocal(tmp[:, m, 3:4], tmp[:, m, 1:2]))
                    nc.vector.tensor_scalar(tmp[:, m, 2:3], tmp[:, m, 3:4], WS, None, ALU.mult).then_inc(factor_done, 1)
                    dve.wait_ge(factor_done, m)

                def low(m):
                    hi, lo = (wu[0], wu[1]) if m == 1 else (parts[:, 0], parts[:, 1])
                    dve.wait_ge(hi_done, m)
                    nc.vector.scalar_tensor_tensor(out=lo.rearrange("p k m -> p (k m)"),
                                                   in0=stage[m % 2][:].rearrange("p k m -> p (k m)"),
                                                   scalar=tmp[:, m, 2:3], in1=hi.rearrange("p k m -> p (k m)"),
                                                   op0=ALU.mult, op1=ALU.subtract).then_inc(lo_done, 1)

                reduce(0)
                reduce(1)
                ternary()
                factor(1)
                low(1)
                for m in (2, 3):
                    reduce(m)
                    factor(m)
                    if m == 3:
                        dve.wait_ge(parts_stored, 16)
                    low(m)
                link(nc.vector.tensor_scalar(consts["u_scale"], tmp[:, 1, 1:2], 1.0 / (WS * XS), None, ALU.mult))
                link(nc.vector.tensor_scalar(consts["half_z"], tmp[:, 2, 1:2], 0.5 / (WS * XS), None, ALU.mult))
                link(nc.vector.tensor_scalar(consts["out_scale"], tmp[:, 3, 1:2], consts["half_z"], 1.0 / WS,
                                             ALU.mult, ALU.mult))


def row_stats(dve, nc, row, stats, mv, vn, idle, chain, ready, read, k):
    for h in range(2):
        ins = nc.vector.bn_stats(stats[:, 6 * h:6 * h + 6], row[:, h * HALF:(h + 1) * HALF])
    ins.then_inc(chain, 1)
    wait(dve, chain, k * 2 + 1)
    nc.vector.memset(idle, 0.0)
    nc.vector.bn_aggr(mv[:, 0:2], stats[:, 0:12]).then_inc(chain, 1)
    wait(dve, chain, k * 2 + 2)
    wait(dve, read, k)
    nc.vector.tensor_scalar(vn[:, 0:1], mv[:, 1:2], EPS, 1.0 / (XS * XS), ALU.add, ALU.mult)
    nc.vector.tensor_scalar(vn[:, 1:2], mv[:, 0:1], -1.0, None, ALU.mult).then_inc(ready, 1)


def row_scale(pool, nc, vn, minus_half, sn, ready, chain, done, used, k):
    wait(pool, ready, k + 1)
    wait(pool, used, k)
    nc.gpsimd.tensor_tensor(sn[:, 0:1], vn[:, 0:1], minus_half, ALU.pow).then_inc(chain, 1)
    wait(pool, chain, k + 1)
    nc.gpsimd.tensor_tensor(sn[:, 1:2], vn[:, 1:2], sn[:, 0:1], ALU.mult).then_inc(done, 1)


def first_pass(nc, sem, ins, tern, wu, consts, ident, dram):
    with ExitStack() as ctx:
        def sb(name, shape, dt=F32):
            return ctx.enter_context(nc.sbuf_tensor(name, shape, dt))

        wx = sb("wx", [P, G, R + 2 * NS])
        wdt = sb("wdt", [R, D])
        half_bias = sb("half_bias", [P, D])
        conv_w = sb("conv_w", [P, G, 4])
        conv_b = sb("conv_b", [P, G])
        dt_b = sb("dt_b", [P, G])
        dskip = sb("dskip", [P, G])
        xin = [sb(f"xin{i}", [P, D]) for i in range(2)]
        x1 = [sb(f"x1_{i}", [P, D]) for i in range(2)]
        xn = [sb(f"xn{i}", [P, D]) for i in range(2)]
        xt = sb("xt", [P, 2, G, P], F16)
        xz = [sb(f"xz{i}", [P, 2, 2, G, T2], F16) for i in range(2)]
        up = [sb(f"up{i}", [P, T1 + 3]) for i in range(2)]
        acc = [sb(f"acc{i}", [P, T1]) for i in range(2)]
        halo = sb("halo", [P, G, 3])
        u = [sb(f"u{i}", [P, G, T1]) for i in range(2)]
        ud = [sb(f"ud{i}", [P, T1]) for i in range(2)]
        y0 = [sb(f"y0_{i}", [P, TT1, 2 * P]) for i in range(2)]
        xdbl = sb("xdbl", [R + 2 * NS, T1])
        ct = sb("ct", [P, TT1, NS])
        rel = [sb(f"rel{i}", [P, T1]) for i in range(2)]
        ex = [sb(f"ex{i}", [P, T1]) for i in range(2)]
        lg = [sb(f"lg{i}", [P, T1]) for i in range(2)]
        res = sb("res", [P, T1])
        dt = [sb(f"dt{i}", [P, T1]) for i in range(2)]
        dtu = [sb(f"dtu{i}", [P, T1]) for i in range(2)]
        small = sb("small1", [P, 64])
        stats = [small[:, 0:12], small[:, 12:24]]
        mv = [small[:, 24:26], small[:, 26:28]]
        vn = [small[:, 28:30], small[:, 30:32]]
        sn = [small[:, 32:34], small[:, 34:36]]
        minus_half = consts["minus_half"]

        def bank(name, shape=(P, HALF)):
            return ctx.enter_context(nc.psum_tensor(name, list(shape), F32))

        p_tr = [bank(f"p_tr{i}") for i in range(2)]
        p_ffn = [bank(f"p_ffn{i}") for i in range(2)]
        p_u = [bank(f"p_u{i}") for i in range(2)]
        p_s = [bank(f"p_s{i}") for i in range(2)]

        const_loaded, const_done = sem("const_loaded1"), sem("const_done1")
        x_loaded = [sem(f"x_loaded{i}") for i in range(2)]
        xb_done, x1_done = sem("xb_done"), sem("x1_done")
        x1_stored = [sem(f"x1_stored{i}") for i in range(2)]
        ln_chain = [sem(f"ln{i}_chain") for i in range(2)]
        stats_ready = [sem(f"stats{i}_ready") for i in range(2)]
        pow_done = [sem(f"pow{i}_done") for i in range(2)]
        scale_ready = [sem(f"scale{i}_ready") for i in range(2)]
        xn_done = [sem(f"xn{i}_done") for i in range(2)]
        tr_full = [sem(f"tr_full{i}") for i in range(2)]
        hi_done = [sem(f"hi_done{i}") for i in range(2)]
        tr_split = [sem(f"tr_split{i}") for i in range(2)]
        ffn_full = sem("ffn_full")
        xz_stored = [sem(f"xz_stored{i}") for i in range(2)]
        u_full, up_done, conv_chain, conv_done = sem("u_full"), sem("up_done"), sem("conv_chain"), sem("conv_done")
        silu_done = sem("silu_done")
        s_full = [sem(f"s_full{i}") for i in range(2)]
        s_free = [sem(f"s_free{i}") for i in range(2)]
        ud_done, y0_stored = sem("ud_done"), [sem(f"y0_stored{i}") for i in range(2)]
        b_stored, ct_stored = sem("b_stored"), sem("ct_stored")
        abs_done, exp_done, ln_done = sem("abs_done"), sem("exp_done"), sem("ln_done")
        sp_chain, dt_done, dtu_done = sem("softplus_chain"), sem("dt_done"), sem("dtu_done")
        dt_stored = [sem(f"dt_stored{i}") for i in range(2)]

        units = [("x", 0), ("y", 0), ("y", 1), ("c", 0), ("d", 0), ("d", 1), ("y", 2), ("y", 3), ("d", 2), ("d", 3),
                 ("y", 4), ("y", 5), ("d", 4), ("d", 5), ("y", 6), ("y", 7), ("d", 6), ("d", 7)]
        place = {(0, 0): (0, 2), (0, 1): (2, 4), (1, 0): (4, 6), (1, 1): (6, 9), (2, 0): (9, 11), (2, 1): (11, 14),
                 (3, 0): (14, 16), (3, 1): (16, 18)}
        NU = len(units) // 2

        def last(k):
            return isinstance(k, int) and k + 1 >= L // P

        def s_units(j, part):
            a, b = place[j, part]
            return [(v, *units[v]) for v in range(a, b)]

        def drive(eng, step, prologue=None):
            if prologue:
                prologue()
            for j in range(TT1):
                step(-1, 1, j, True, False, False)
            for j in range(TT1):
                step(0, 0, j, True, True, False)
            for j in range(TT1):
                step(1, 1, j, True, True, True)
            with eng.Fori(0, (C1 - 4) // 2) as turn:
                for o in range(2):
                    for j in range(TT1):
                        step(turn * 2 + 2 + o, o, j, True, True, True)
            for j in range(TT1):
                step(C1 - 2, C1 % 2, j, True, True, True)
            for j in range(TT1):
                step(C1 - 1, (C1 - 1) % 2, j, False, True, True)
            for j in range(TT1):
                step(C1, C1 % 2, j, False, False, True)

        with nc.Block() as block:
            @block.sync
            def _(sp):
                loads = [(wx[:], ins["W_xproj"].rearrange("(g p) m -> p g m", p=P)), (wdt[:], ins["W_dt"]),
                         (half_bias[:], ins["bias"].partition_broadcast(P)),
                         (conv_w[:], ins["conv_w"].rearrange("(g p) k -> p g k", p=P)),
                         (conv_b[:], ins["conv_b"].rearrange("(g p) -> p g", p=P)),
                         (dt_b[:], ins["b_dt"].rearrange("(g p) -> p g", p=P)),
                         (dskip[:], ins["Dskip"].rearrange("(g p) -> p g", p=P))]

                def load_x(k, b, row):
                    wait_alone(sp, xn_done[0], k - 1)
                    wait_alone(sp, xb_done, k - 1)
                    sp.dma_start(xin[b][:], ins["x"][bass.ds(row, P), :]).then_inc(x_loaded[b], 16)

                load_x(0, 0, 0)
                load_x(1, 1, P)
                with nc.allow_non_contiguous_dma(reason="small constants"):
                    for dst, src in loads:
                        sp.dma_start(dst, src).then_inc(const_loaded, 16)

                def s_stores(d, j, part):
                    for v, kind, g in s_units(j, part):
                        if kind == "x":
                            wait_alone(sp, s_free[v % 2], d * NU + v // 2 + 1)
                            sp.dma_start(dram["b"][bass.ds(d * 2, 2)].rearrange("h n t -> n h t"),
                                         xdbl[R:R + NS, :].rearrange("n (h t) -> n h t", h=2)).then_inc(b_stored, 16)
                        if kind == "c":
                            wait_alone(sp, s_free[v % 2], d * NU + v // 2 + 1)
                            with nc.allow_non_contiguous_dma(reason="64 bytes a token"):
                                sp.dma_start(dram["ct"][bass.ds(d * T1, T1), :].rearrange("(t p) n -> p t n", p=P),
                                             ct[:]).then_inc(ct_stored, 16)
                        if kind == "y" and g % 2:
                            for w in (v - 1, v):
                                wait_alone(sp, s_free[w % 2], d * NU + w // 2 + 1)
                            sp.dma_start(dram["y0"][bass.ds(d * T1, T1), (g - 1) * P:(g + 1) * P].rearrange(
                                "(t p) n -> p t n", p=P), y0[g // 2 % 2][:]).then_inc(y0_stored[g // 2 % 2], 16)
                        if kind == "d":
                            wait_alone(sp, dt_done, d * G + g + 1)
                            wait_alone(sp, dtu_done, d * G + g + 1)
                            for name, tile in (("dt", dt), ("dtu", dtu)):
                                sp.dma_start(dram[name][bass.ds(d * 2, 2), :, g].rearrange("h p t -> p h t"),
                                             tile[g % 2][:].rearrange("p (h t) -> p h t", h=2)
                                             ).then_inc(dt_stored[g % 2], 16)

                def step(i, par, j, f_on, u_on, s_on):
                    f, k = i + 1, (i + 1) * TT1 + j
                    if s_on:
                        s_stores(i - 1, j, 0)
                    if f_on:
                        wait_alone(sp, x1_done, k * 2 + 2)
                        sp.dma_start(dram["x1"][bass.ds(k * P, P), :], x1[j % 2][:]).then_inc(x1_stored[j % 2], 16)
                        if not last(k + 1):
                            load_x(k + 2, j % 2, k * P + 2 * P)
                    if s_on:
                        s_stores(i - 1, j, 1)
                    if f_on and j == TT1 - 1:
                        for b in range(2):
                            wait_alone(sp, tr_split[b], k * 2 + 2)
                        for a in range(2):
                            sp.dma_start(dram["xz"][bass.ds(f * 2, 2), a].rearrange("h p n -> p h n"),
                                         xz[1 - par][:, a].rearrange("p h k t -> p h (k t)")
                                         ).then_inc(xz_stored[1 - par], 16)

                drive(sp, step)
                for b in range(2):
                    sp.wait_ge(x1_stored[b], 16 * (L // P) // 2)
                    sp.wait_ge(xz_stored[b], 32 * C1 // 2)
                    sp.wait_ge(y0_stored[b], 16 * C1 * 2)
                    sp.wait_ge(dt_stored[b], 32 * C1 * G // 2)
                sp.wait_ge(b_stored, 16 * C1)
                sp.wait_ge(ct_stored, 16 * C1)

            @block.gpsimd
            def _(pool):
                def prologue():
                    row_scale(pool, nc, vn[0], minus_half, sn[0], stats_ready[0], pow_done[0], scale_ready[0],
                              xn_done[0], 0)

                def s_work(d, dpar, j, part):
                    for v, kind, g in s_units(j, part):
                        if kind != "d":
                            continue
                        q = d * G + g
                        wait(pool, dt_done, q + 1)
                        wait(pool, dt_stored[g % 2], (d * (G // 2) + g // 2) * 32)
                        nc.gpsimd.tensor_tensor(dtu[g % 2][:], dt[g % 2][:], u[dpar][:, g, :], ALU.mult).then_inc(dtu_done, 1)

                def step(i, par, j, f_on, u_on, s_on):
                    k = (i + 1) * TT1 + j
                    if s_on:
                        s_work(i - 1, 1 - par, j, 0)
                    if f_on:
                        wait(pool, x_loaded[j % 2], ((i + 1) * 2 + j // 2 + 1) * 16)
                        wait(pool, x1_stored[j % 2], ((i + 1) * 2 + j // 2) * 16)
                        wait(pool, xn_done[1], k - 1)
                        if isinstance(k, int) and k == 0:
                            pool.wait_ge(const_done, 1)
                        nc.gpsimd.tensor_tensor(x1[j % 2][:], xin[j % 2][:], half_bias[:], ALU.add).then_inc(xb_done, 1)
                        if not last(k):
                            row_scale(pool, nc, vn[0], minus_half, sn[0], stats_ready[0], pow_done[0],
                                      scale_ready[0], xn_done[0], k + 1)
                        row_scale(pool, nc, vn[1], minus_half, sn[1], stats_ready[1], pow_done[1],
                                  scale_ready[1], xn_done[1], k)
                    if s_on:
                        s_work(i - 1, 1 - par, j, 1)

                drive(pool, step, prologue)

            @block.scalar
            def _(act):
                def normalise(n, src, k):
                    wait(act, scale_ready[n], k + 1)
                    wait(act, tr_full[1], k * 2 - 1 + n)
                    nc.scalar.activation(xn[n][:], src, ACT.Identity, bias=sn[n][:, 1:2],
                                         scale=sn[n][:, 0:1]).then_inc(xn_done[n], 1)

                def high(n, k, dst, b):
                    wait(act, tr_full[b], k * 2 + n + 1)
                    nc.scalar.activation(dst, p_tr[b][:].rearrange("p (g t) -> p g t", g=4), ACT.Copy).then_inc(hi_done[b], 1)

                def u_work(i, g):
                    q = i * G + g
                    wait(act, u_full, q + 1)
                    wait(act, conv_done, q - 1)
                    nc.scalar.activation(up[g % 2][:, 3:3 + T1], p_u[g % 2][:], ACT.Copy,
                                         scale=consts["u_scale"]).then_inc(up_done, 1)

                def silu(i, par, g):
                    q = i * G + g
                    wait(act, conv_done, q + 1)
                    if g == 0:
                        wait(act, dtu_done, (i - 1) * G)
                        wait(act, ud_done, (i - 1) * G)
                    nc.scalar.activation(u[par][:, g, :], acc[g % 2][:], ACT.Silu).then_inc(silu_done, 1)

                def s_work(d, j, part):
                    for v, kind, g in s_units(j, part):
                        if kind == "x":
                            wait(act, s_full[v % 2], d * NU + v // 2 + 1)
                            wait(act, b_stored, d * 16)
                            wait(act, s_full[1], (d - 1) * NU + NU)
                            nc.scalar.activation(xdbl[:], p_s[v % 2][0:R + 2 * NS, :], ACT.Copy).then_inc(s_free[v % 2], 1)
                        if kind == "d":
                            q = d * G + g
                            wait(act, s_full[v % 2], d * NU + v // 2 + 1)
                            wait(act, dt_done, q - 1)
                            nc.scalar.activation(rel[g % 2][:], p_s[v % 2][:], ACT.Relu, bias=dt_b[:, g:g + 1])
                            nc.scalar.activation(ex[g % 2][:], p_s[v % 2][:], ACT.Abs, bias=dt_b[:, g:g + 1]
                                                 ).then_inc(s_free[v % 2], 1)
                            wait(act, s_free[v % 2], d * NU + v // 2 + 1)
                            nc.scalar.activation(ex[g % 2][:], ex[g % 2][:], ACT.Exp, scale=-1.0).then_inc(exp_done, 1)
                            wait(act, exp_done, q + 1)
                            nc.scalar.activation(lg[g % 2][:], ex[g % 2][:], ACT.Ln, bias=1.0).then_inc(ln_done, 1)

                def prologue():
                    act.wait_ge(x_loaded[0], 16)
                    act.wait_ge(const_loaded, 16 * 7)
                    nc.scalar.mul(half_bias[:], half_bias[:], 0.5).then_inc(const_done, 1)
                    normalise(0, xin[0][:], 0)

                def step(i, par, j, f_on, u_on, s_on):
                    f = i + 1
                    k = f * TT1 + j
                    if f_on:
                        wait(act, ffn_full, k * 2)
                        for b in range(2):
                            high(0, k, xt[:, 0, 4 * b:4 * b + 4, :], b)
                    if s_on:
                        s_work(i - 1, j, 0)
                    if u_on:
                        u_work(i, 2 * j)
                    if f_on and not last(k):
                        normalise(0, xin[(j + 1) % 2][:], k + 1)
                    if u_on:
                        silu(i, par, 2 * j)
                    if s_on:
                        s_work(i - 1, j, 1)
                    if f_on:
                        normalise(1, x1[j % 2][:], k)
                    if u_on:
                        u_work(i, 2 * j + 1)
                    if f_on:
                        if j == 0:
                            wait(act, u_full, (f - 1) * G)
                            wait(act, xz_stored[1 - par], (f - (1 - par)) * 16)
                        for b in range(2):
                            high(1, k, xz[1 - par][:, 0, j // 2, 4 * b:4 * b + 4, (j % 2) * P:(j % 2 + 1) * P], b)
                    if u_on:
                        silu(i, par, 2 * j + 1)

                drive(act, step, prologue)

            @block.vector
            def _(dve):
                def low(n, k, src_hi, dst, b):
                    wait(dve, hi_done[b], k * 2 + n + 1)
                    nc.vector.tensor_tensor(dst, p_tr[b][:].rearrange("p (g t) -> p g t", g=4), src_hi,
                                            ALU.subtract).then_inc(tr_split[b], 1)

                def conv(i, g):
                    q = i * G + g
                    src, dst = up[g % 2], acc[g % 2]
                    nc.vector.tensor_copy(src[:, 0:3], halo[:, g, :]).then_inc(conv_chain, 1)
                    wait(dve, conv_chain, q * 4 + 1)
                    wait(dve, up_done, q + 1)
                    wait(dve, silu_done, q - 1)
                    nc.vector.tensor_scalar(dst[:], src[:, 0:T1], conv_w[:, g, 0:1], conv_b[:, g:g + 1],
                                            ALU.mult, ALU.add).then_inc(conv_chain, 1)
                    for tap in (1, 2):
                        wait(dve, conv_chain, q * 4 + 1 + tap)
                        nc.vector.scalar_tensor_tensor(out=dst[:], in0=src[:, tap:tap + T1], scalar=conv_w[:, g, tap:tap + 1],
                                                       in1=dst[:], op0=ALU.mult, op1=ALU.add).then_inc(conv_chain, 1)
                    nc.vector.tensor_copy(halo[:, g, :], src[:, T1:T1 + 3])
                    wait(dve, conv_chain, q * 4 + 4)
                    nc.vector.scalar_tensor_tensor(out=dst[:], in0=src[:, 3:3 + T1], scalar=conv_w[:, g, 3:4],
                                                   in1=dst[:], op0=ALU.mult, op1=ALU.add).then_inc(conv_done, 1)

                def s_work(d, dpar, j, part):
                    for v, kind, g in s_units(j, part):
                        q = d * G + g
                        if kind == "c":
                            wait(dve, s_full[v % 2], d * NU + v // 2 + 1)
                            wait(dve, ct_stored, d * 16)
                            nc.vector.tensor_copy(ct[:], p_s[v % 2][:, 0:TT1 * P].rearrange(
                                "p (t n) -> p t n", t=TT1)[:, :, R + NS:R + 2 * NS]).then_inc(s_free[v % 2], 1)
                        if kind == "y":
                            wait(dve, s_full[v % 2], d * NU + v // 2 + 1)
                            wait(dve, y0_stored[g // 2 % 2], (d * 2 + g // 4) * 16)
                            nc.vector.tensor_copy(y0[g // 2 % 2][:, :, (g % 2) * P:(g % 2 + 1) * P],
                                                  p_s[v % 2][:].rearrange("p (t n) -> p t n", t=TT1)).then_inc(s_free[v % 2], 1)
                            if g + 2 < G:
                                times_dskip(d, dpar, g + 2)
                        if kind == "d":
                            wait(dve, dt_done, q)
                            wait(dve, exp_done, q + 1)
                            nc.vector.tensor_scalar(res[:], ex[g % 2][:], 1.0, -1.0, ALU.add, ALU.add).then_inc(sp_chain, 1)
                            wait(dve, sp_chain, q * 3 + 1)
                            nc.vector.tensor_tensor(res[:], ex[g % 2][:], res[:], ALU.subtract).then_inc(sp_chain, 1)
                            wait(dve, ln_done, q + 1)
                            wait(dve, sp_chain, q * 3 + 2)
                            nc.vector.tensor_tensor(res[:], lg[g % 2][:], res[:], ALU.add).then_inc(sp_chain, 1)
                            wait(dve, sp_chain, q * 3 + 3)
                            wait(dve, dtu_done, q - 1)
                            wait(dve, dt_stored[g % 2], (d * (G // 2) + g // 2) * 32)
                            nc.vector.tensor_tensor(dt[g % 2][:], res[:], rel[g % 2][:], ALU.add).then_inc(dt_done, 1)

                def times_dskip(d, dpar, g):
                    v = units.index(("y", g - 2)) if g >= 2 else units.index(("y", g + 6))
                    wait(dve, s_full[v % 2], (d if g >= 2 else d - 1) * NU + v // 2 + 1)
                    nc.vector.tensor_scalar(ud[g % 2][:], u[dpar][:, g, :], dskip[:, g:g + 1], None,
                                            ALU.mult).then_inc(ud_done, 1)

                def prologue():
                    nc.vector.memset(halo[:], 0.0)
                    dve.wait_ge(x_loaded[0], 16)
                    row_stats(dve, nc, xin[0], stats[0], mv[0], vn[0], small[:, 40:41], ln_chain[0], stats_ready[0], scale_ready[0], 0)
                    dve.wait_ge(const_loaded, 16 * 7)

                def step(i, par, j, f_on, u_on, s_on):
                    f, d = i + 1, i - 1
                    k = f * TT1 + j
                    if s_on and j == 0:
                        wait(dve, silu_done, d * G + G)
                        times_dskip(d, 1 - par, 0)
                        times_dskip(d, 1 - par, 1)
                    if f_on:
                        for b in range(2):
                            low(0, k, xt[:, 0, 4 * b:4 * b + 4, :], xt[:, 1, 4 * b:4 * b + 4, :], b)
                    if s_on:
                        s_work(d, 1 - par, j, 0)
                    if u_on:
                        conv(i, 2 * j)
                    if f_on:
                        if not last(k):
                            wait(dve, x_loaded[(j + 1) % 2], (f * 2 + (j + 1) // 2 + 1) * 16)
                            row_stats(dve, nc, xin[(j + 1) % 2], stats[0], mv[0], vn[0], small[:, 40:41], ln_chain[0],
                                      stats_ready[0], scale_ready[0], k + 1)
                        wait(dve, xb_done, k + 1)
                        for h in range(2):
                            wait(dve, ffn_full, k * 2 + h + 1)
                            nc.vector.scalar_tensor_tensor(out=x1[j % 2][:, h * HALF:(h + 1) * HALF], in0=p_ffn[h][:],
                                                           scalar=consts["ffn_scale"],
                                                           in1=x1[j % 2][:, h * HALF:(h + 1) * HALF],
                                                           op0=ALU.mult, op1=ALU.add).then_inc(x1_done, 1)
                        wait(dve, x1_done, k * 2 + 2)
                        row_stats(dve, nc, x1[j % 2], stats[1], mv[1], vn[1], small[:, 41:42], ln_chain[1], stats_ready[1],
                                  scale_ready[1], k)
                    if s_on:
                        s_work(d, 1 - par, j, 1)
                    if f_on:
                        for b in range(2):
                            hi, lo = (xz[1 - par][:, a, j // 2, 4 * b:4 * b + 4, (j % 2) * P:(j % 2 + 1) * P] for a in range(2))
                            low(1, k, hi, lo, b)
                    if u_on:
                        conv(i, 2 * j + 1)

                drive(dve, step, prologue)

            @block.tensor
            def _(pe):
                def turn(n, k):
                    wait(pe, xn_done[n], k + 1)
                    for b in range(2):
                        wait(pe, tr_split[b], k * 2 + n)
                        for q in range(4):
                            g = 4 * b + q
                            mm = nc.tensor.transpose(p_tr[b][:, q * P:(q + 1) * P], xn[n][:, g * P:(g + 1) * P], ident[:])
                        mm.then_inc(tr_full[b], 1)

                def ffn(k):
                    for b in range(2):
                        wait(pe, tr_split[b], k * 2 + 1)
                    wait(pe, x1_done, k * 2)
                    for h in range(2):
                        for g in range(G):
                            for a in range(2):
                                mm = nc.tensor.matmul(p_ffn[h][:], xt[:, a, g, :], tern[:, g, h * HALF:(h + 1) * HALF],
                                                      start=(g == 0 and a == 0), stop=(g == G - 1 and a == 1))
                        mm.then_inc(ffn_full, 1)

                def u_product(i, par, g):
                    wait(pe, up_done, i * G + g - 1)
                    n = 0
                    for kk in range(G):
                        for wa, xa in ((0, 0), (0, 1), (1, 0)):
                            mm = nc.tensor.matmul(p_u[g % 2][:].rearrange("p (h t) -> p h t", h=2),
                                                  wu[wa][:, kk, g * P:(g + 1) * P], xz[par][:, xa, :, kk, :],
                                                  start=(n == 0), stop=(n == 3 * G - 1))
                            n += 1
                    mm.then_inc(u_full, 1)

                def s_work(d, dpar, j, part):
                    for v, kind, g in s_units(j, part):
                        wait(pe, s_free[v % 2], d * NU + v // 2)
                        ps = p_s[v % 2]
                        if kind == "x":
                            wait(pe, silu_done, d * G + G)
                            for q in range(G):
                                mm = nc.tensor.matmul(ps[0:R + 2 * NS, :], wx[:, q, :], u[dpar][:, q, :],
                                                      start=(q == 0), stop=(q == G - 1))
                        if kind == "y":
                            wait(pe, ud_done, d * G + g + 1)
                            for t in range(TT1):
                                mm = nc.tensor.transpose(ps[:, t * P:(t + 1) * P], ud[g % 2][:, t * P:(t + 1) * P], ident[:])
                        if kind == "c":
                            wait(pe, s_free[0], d * NU + 1)
                            for t in range(TT1):
                                mm = nc.tensor.transpose(ps[:, t * P:t * P + R + 2 * NS], xdbl[:, t * P:(t + 1) * P],
                                                         ident[0:R + 2 * NS, 0:R + 2 * NS])
                        if kind == "d":
                            wait(pe, s_free[0], d * NU + 1)
                            mm = nc.tensor.matmul(ps[:], wdt[:, g * P:(g + 1) * P], xdbl[0:R, :], start=True, stop=True)
                        mm.then_inc(s_full[v % 2], 1)

                def prologue():
                    pe.wait_ge(const_loaded, 16 * 7)

                def step(i, par, j, f_on, u_on, s_on):
                    k = (i + 1) * TT1 + j
                    if s_on:
                        s_work(i - 1, 1 - par, j, 0)
                    if f_on:
                        turn(0, k)
                    if u_on:
                        if j == 0:
                            for b in range(2):
                                wait(pe, tr_split[b], (i * TT1 + TT1) * 2)
                        u_product(i, par, 2 * j)
                    if f_on:
                        ffn(k)
                    if s_on:
                        s_work(i - 1, 1 - par, j, 1)
                    if u_on:
                        u_product(i, par, 2 * j + 1)
                    if f_on:
                        turn(1, k)

                drive(pe, step, prologue)


def second_pass(nc, sem, ins, tern, consts, ident, ident16, split_dram, dram, out):
    with ExitStack() as ctx:
        def sb(name, shape, dt=F32):
            return ctx.enter_context(nc.sbuf_tensor(name, shape, dt))

        wz = sb("wz", [P, 2, G, D], F16)
        wo = sb("wo", [P, 2, G, D], F16)
        half_bias = sb("half_bias2", [P, D])
        neg_a = sb("neg_a", [P, G, NS])
        carry = sb("carry", [P, NS, G])
        dt = [sb(f"dt_{i}", [P, G, T2]) for i in range(2)]
        dtu = [sb(f"dtu_{i}", [P, G, T2]) for i in range(2)]
        ct = [sb(f"ct_{i}", [P, TT2, NS]) for i in range(2)]
        NB = 2
        bb = [sb(f"bb{i}", [P, NB, T2]) for i in range(2)]
        dbu = [sb(f"dbu{i}", [P, G // 2, T2]) for i in range(2)]
        h = [sb(f"h{i}", [P, G, T2]) for i in range(2)]
        y = [[sb(f"y{i}{t}", [P, D]) for t in range(TT2)] for i in range(2)]
        xz = sb("xz_2", [P, 2, G, T2], F16)
        x1 = [sb(f"x1_2{t}", [P, D]) for t in range(TT2)]
        th = [sb(f"th{i}", [P, HALF]) for i in range(2)]
        q = [sb(f"q{i}", [P, HALF]) for i in range(2 * TT2)]
        tok = sb("tok", [P, 2, D], F16)
        tokt = sb("tokt", [P, 2, G, P], F16)
        xn = sb("xn_2", [P, D])
        o = [sb(f"o{i}", [P, HALF]) for i in range(2)]
        small = sb("small2", [P, 48])
        stats, mv, vn, sn = small[:, 0:12], small[:, 12:14], small[:, 14:16], small[:, 16:18]
        gs = [small[:, 20 + 8 * t:28 + 8 * t] for t in range(TT2)]

        def banks(name, n, shape=(P, HALF)):
            return [ctx.enter_context(nc.psum_tensor(f"{name}{i}", list(shape), F32)) for i in range(n)]

        p_da = banks("p_da", 2)
        p_ht = banks("p_ht", TT2, (P, D))
        p_g = banks("p_g", 2)

        const_loaded, w_loaded, a_done, bias_done = (sem(n) for n in ("const_loaded2", "w2_loaded", "a_done", "bias2_done"))
        carry_set = sem("carry_set")
        dt_loaded = [sem(f"dt2_loaded{i}") for i in range(2)]
        y_loaded = [sem(f"y2_loaded{i}") for i in range(2)]
        b_loaded = [sem(f"b2_loaded{i}") for i in range(2)]
        xz_loaded = sem("xz2_loaded")
        x1_loaded = [sem(f"x1_2_loaded{t}") for t in range(TT2)]
        da_done, dbu_done, scan_done, carry_done = (sem(n) for n in ("da_done", "dbu_done", "scan_done", "carry_done"))
        ht_full = [sem(f"ht_full{t}") for t in range(TT2)]
        y_added = [sem(f"y_added{t}") for t in range(TT2)]
        g_full = [sem(f"g_full{i}") for i in range(2)]
        g_free = [sem(f"g_free{i}") for i in range(2)]
        th_done, gate_done = sem("th_done"), sem("gate_done")
        tok_chain, tok_scale, gs_done, tok_hi, tok_lo = (sem(n) for n in ("tok_chain", "tok_scale", "gs_done", "tok_hi", "tok_lo"))
        x2_done, ln_chain, stats_ready, pow_done, scale_ready, xn_done = (
            sem(n) for n in ("x2_done", "ln2_chain", "stats2_ready", "pow2_done", "scale2_ready", "xn2_done"))
        hi3_done, lo3_done, xb_done, fin_done = sem("hi3_done"), sem("lo3_done"), sem("xb2_done"), sem("fin_done")
        o_stored = [sem(f"o_stored{i}") for i in range(2)]

        FFN = {0: [("f", 0, 0)], 1: [("f", 0, 1)], 2: [("n", 1, 0), ("n", 1, 1)], 3: [("f", 1, 0)], 4: [("f", 1, 1)]}
        OUT = {5: [("t", 0, 0), ("t", 0, 1)], 6: [("o", 0, 0)], 7: [("o", 0, 1)], 8: [("t", 1, 0), ("t", 1, 1)],
               9: [("o", 1, 0)], 10: [("o", 1, 1)], 14: [("n", 0, 0), ("n", 0, 1)]}
        ZED = {11: [("z", 0, 0)], 12: [("z", 0, 1)], 13: [("z", 1, 0)], 14: [("z", 1, 1)]}

        def flags(i):
            if isinstance(i, int):
                return 2 <= i, 1 <= i <= C2, i < C2
            return True, True, True

        def sequence(i):
            return [(n, *unit) for n in range(NS) for on, table in zip(flags(i), (FFN, OUT, ZED)) if on
                    for unit in table.get(n, [])]

        def base(i):
            if isinstance(i, int) and i < 2:
                return i * 2
            if isinstance(i, int) and i == C2 + 1:
                return base(C2) + 8
            return (i - 2) * 10 + 9

        def place(i, kind, t, x):
            at = [u[1:] for u in sequence(i)].index((kind, t, x))
            return at % 2, base(i) + at // 2

        def more(i):
            return not (isinstance(i, int) and i >= C2 - 1)

        def drive(eng, body, prologue):
            prologue()
            body(0, 0)
            body(1, 1)
            with eng.Fori(0, (C2 - 4) // 2) as turn:
                body(turn * 2 + 2, 0)
                body(turn * 2 + 3, 1)
            for i in range(C2 - 2, C2 + 2):
                body(i, i % 2)

        with nc.Block() as block:
            @block.sync
            def _(sp):
                def load_scan(c, par):
                    wait_alone(sp, da_done, (c - 1) * NS * 4)
                    wait_alone(sp, dbu_done, (c - 1) * NS * 2)
                    wait_alone(sp, y_added[1], (c - 1) * NS)
                    for name, tile in (("dt", dt), ("dtu", dtu)):
                        sp.dma_start(tile[par][:], dram[name][bass.ds(c, 1)].rearrange("c p g t -> p (c g) t")
                                     ).then_inc(dt_loaded[par], 16)
                    with nc.allow_non_contiguous_dma(reason="64 bytes a token"):
                        sp.dma_start(ct[par][:], dram["ct"][bass.ds(c * T2, T2), :].rearrange("(t p) n -> p t n", p=P)
                                     ).then_inc(dt_loaded[par], 16)

                def load_y(c, par):
                    wait_alone(sp, tok_lo, (c - 1) * TT2)
                    for t in range(TT2):
                        sp.dma_start(y[par][t][:], dram["y0"][bass.ds(c * T2 + t * P, P), :]).then_inc(y_loaded[par], 16)

                def load_b(c, n):
                    wait_alone(sp, dbu_done, (c * NS + n - NB) * 2)
                    s = n // NB % 2
                    sp.dma_start(bb[s][:].rearrange("p n t -> p (n t)"),
                                 dram["b"].rearrange("c n t -> c (n t)")[bass.ds(c, 1), n * T2:(n + NB) * T2]
                                 .to_broadcast([P, NB * T2])).then_inc(b_loaded[s], 16)

                def load_xz(c):
                    if not (isinstance(c, int) and c == 0):
                        b, m = place(c - 1, "z", 1, 1)
                        wait_alone(sp, g_full[b], m + 1)
                    for a in range(2):
                        sp.dma_start(xz[:, a].rearrange("p k t -> p (k t)"),
                                     dram["xz"][bass.ds(c, 1), a].rearrange("c p n -> p (c n)")).then_inc(xz_loaded, 16)

                def load_x1(c, t):
                    wait_alone(sp, fin_done, ((c - 1) * TT2 + t + 1) * 2)
                    sp.dma_start(x1[t][:], dram["x1"][bass.ds(c * T2 + t * P, P), :]).then_inc(x1_loaded[t], 16)

                def prologue():
                    with nc.allow_non_contiguous_dma(reason="constants"):
                        sp.dma_start(neg_a[:], ins["A_log"].rearrange("(g p) n -> p g n", p=P)).then_inc(const_loaded, 16)
                    sp.dma_start(half_bias[:], ins["bias"].partition_broadcast(P)).then_inc(const_loaded, 16)
                    load_scan(0, 0)
                    load_b(0, 0)
                    load_y(0, 0)
                    load_xz(0)
                    for dst, src in ((wz, split_dram[0]), (wo, split_dram[1])):
                        sp.dma_start(dst[:].rearrange("p a k m -> p (a k m)"), src).then_inc(w_loaded, 16)
                    load_scan(1, 1)

                def store(c, t, x):
                    wait_alone(sp, fin_done, (c * TT2 + t) * 2 + x + 1)
                    sp.dma_start(out[bass.ds(c * T2 + t * P, P), x * HALF:(x + 1) * HALF], o[x][:]).then_inc(o_stored[x], 16)

                def body(i, par):
                    e_on, c_on, z_on = flags(i)
                    for n in range(NS):
                        if z_on and n % NB == 0:
                            if n + NB < NS:
                                load_b(i, n + NB)
                            elif more(i):
                                load_b(i + 1, 0)
                        if z_on and more(i) and n == 2 and not (isinstance(i, int) and i == 0):
                            load_scan(i + 1, 1 - par)
                        if e_on and n in (3, 4, 6, 7):
                            store(i - 2, *{3: (0, 0), 4: (0, 1), 6: (1, 0), 7: (1, 1)}[n])
                        if c_on and n in (4, 7):
                            load_x1(i - 1, n // 7)
                        if z_on and more(i) and n == 9:
                            load_y(i + 1, 1 - par)
                        if z_on and more(i) and n == NS - 1:
                            load_xz(i + 1)

                drive(sp, body, prologue)
                for x in range(2):
                    sp.wait_ge(o_stored[x], 16 * C2 * TT2)

            @block.gpsimd
            def _(pool):
                def prologue():
                    nc.gpsimd.memset(carry[:], 0.0).then_inc(carry_set, 1)

                def times_b(i, par, n):
                    if n == 0:
                        wait(pool, dt_loaded[par], (i - par) * 24 + 48)
                    if n % NB == 0:
                        wait(pool, b_loaded[n // NB % 2], (i * (NS // NB // 2) + n // NB // 2 + 1) * 16)
                    for f in range(2):
                        wait(pool, scan_done, i * (NS * 4) + (n - 1) * 4 + 2 * f + 2)
                        nc.gpsimd.tensor_tensor(dbu[f][:], dtu[par][:, 4 * f:4 * f + 4, :],
                                                bb[n // NB % 2][:, n % NB:n % NB + 1, :].to_broadcast([P, G // 2, T2]),
                                                ALU.mult).then_inc(dbu_done, 1)

                def keep(c, n):
                    wait(pool, scan_done, c * (NS * 4) + n * 4 + 4)
                    nc.gpsimd.tensor_tensor(carry[:, n, :], h[n % 2][:, :, T2 - 1], consts["one"].to_broadcast([P, G]),
                                            ALU.mult).then_inc(carry_done, 1)

                def gate(c, cpar, t):
                    wait(pool, y_added[t], c * NS + NS)
                    for x in range(2):
                        b, m = place(c, "z", t, x)
                        wait(pool, g_free[b], m + 1)
                        half = y[cpar][t][:, x * HALF:(x + 1) * HALF]
                        nc.gpsimd.tensor_tensor(half, q[2 * t + x][:], half, ALU.mult).then_inc(gate_done, 1)

                def low(c, cpar, t):
                    wait(pool, tok_hi, c * TT2 + t + 1)
                    nc.gpsimd.tensor_tensor(tok[:, 1, :], y[cpar][t][:], tok[:, 0, :], ALU.subtract).then_inc(tok_lo, 1)

                def add_x1(i, t, x):
                    c = i - 1
                    b, m = place(i, "o", t, x)
                    wait(pool, g_free[b], m + 1)
                    if x == 0:
                        wait(pool, x1_loaded[t], c * 16 + 16)
                    half = x1[t][:, x * HALF:(x + 1) * HALF]
                    nc.gpsimd.tensor_tensor(half, o[x][:], half, ALU.add).then_inc(x2_done, 1)

                def low3(c, t):
                    wait(pool, hi3_done, c * TT2 + t + 1)
                    nc.gpsimd.tensor_tensor(tok[:, 1, :], xn[:], tok[:, 0, :], ALU.subtract).then_inc(lo3_done, 1)
                    nc.gpsimd.tensor_tensor(x1[t][:], x1[t][:], half_bias[:], ALU.add).then_inc(xb_done, 1)

                def finish(i, t, x):
                    b, m = place(i, "f", t, x)
                    wait(pool, g_free[b], m + 1)
                    wait(pool, xb_done, (i - 2) * TT2 + t + 1)
                    nc.gpsimd.tensor_tensor(o[x][:], o[x][:], x1[t][:, x * HALF:(x + 1) * HALF], ALU.add).then_inc(fin_done, 1)

                def body(i, par):
                    e_on, c_on, z_on = flags(i)
                    for n in range(NS):
                        if z_on:
                            times_b(i, par, n)
                            if n:
                                keep(i, n - 1)
                            elif c_on:
                                keep(i - 1, NS - 1)
                        if e_on:
                            if n == 0:
                                low3(i - 2, 1)
                            if n in (2, 3, 5, 6):
                                finish(i, *{2: (0, 0), 3: (0, 1), 5: (1, 0), 6: (1, 1)}[n])
                        if c_on:
                            if n in (1, 2):
                                gate(i - 1, 1 - par, n - 1)
                            if n in (4, 7):
                                low(i - 1, 1 - par, n // 7)
                            if n in (8, 9, 11, 12):
                                add_x1(i, *{8: (0, 0), 9: (0, 1), 11: (1, 0), 12: (1, 1)}[n])
                            if n in (11, 14):
                                row_scale(pool, nc, vn, consts["minus_half"], sn, stats_ready, pow_done, scale_ready,
                                          xn_done, (i - 1) * TT2 + n // 14)
                            if n == 13:
                                if isinstance(i, int) and i == 1:
                                    pool.wait_ge(bias_done, 1)
                                low3(i - 1, 0)

                drive(pool, body, prologue)

            @block.scalar
            def _(act):
                def prologue():
                    act.wait_ge(const_loaded, 32)
                    nc.scalar.activation(neg_a[:], neg_a[:], ACT.Exp).then_inc(a_done, 1)
                    act.wait_ge(a_done, 1)
                    nc.scalar.mul(neg_a[:], neg_a[:], -1.0).then_inc(a_done, 1)
                    nc.scalar.mul(half_bias[:], half_bias[:], 0.5).then_inc(bias_done, 1)
                    act.wait_ge(a_done, 2)

                def decays(i, par, n):
                    if n == 0:
                        wait(act, dt_loaded[par], (i - par) * 24 + 48)
                    for p in range(4):
                        wait(act, scan_done, i * (NS * 4) + n * 4 + p - 1)
                        for k in range(2):
                            g = 2 * p + k
                            ins_ = nc.scalar.activation(p_da[p % 2][:, k * T2:(k + 1) * T2], dt[par][:, g, :], ACT.Exp,
                                                        scale=neg_a[:, g, n:n + 1])
                        ins_.then_inc(da_done, 1)

                def tanh(i, t, x):
                    b, m = place(i, "z", t, x)
                    wait(act, g_full[b], m + 1)
                    nc.scalar.activation(th[x][:], p_g[b][:], ACT.Tanh, scale=consts["half_z"]).then_inc(th_done, 1)

                def transposed(i, kind, t):
                    for a in range(2):
                        b, m = place(i, kind, t, a)
                        wait(act, g_full[b], m + 1)
                        nc.scalar.activation(tokt[:, a].rearrange("p g t -> p (g t)"), p_g[b][:].bitcast(F16),
                                             ACT.Copy).then_inc(g_free[b], 1)

                def high(i, c, cpar, t):
                    wait(act, tok_scale, c * TT2 + t + 1)
                    nc.scalar.activation(y[cpar][t][:], y[cpar][t][:], ACT.Copy, scale=gs[t][:, 3:4]).then_inc(gs_done, 1)
                    wait(act, gs_done, c * TT2 + t + 1)
                    if t == 0 and flags(i)[0]:
                        b, m = place(i, "n", 1, 1)
                        wait(act, g_full[b], m + 1)
                    nc.scalar.activation(tok[:, 0, :], y[cpar][t][:], ACT.Copy).then_inc(tok_hi, 1)

                def product(i, kind, t, x, scale):
                    b, m = place(i, kind, t, x)
                    wait(act, g_full[b], m + 1)
                    nc.scalar.activation(o[x][:], p_g[b][:], ACT.Copy, scale=scale).then_inc(g_free[b], 1)

                def normalise(c, t):
                    k = c * TT2 + t
                    wait(act, scale_ready, k + 1)
                    wait(act, lo3_done, k)
                    nc.scalar.activation(xn[:], x1[t][:], ACT.Identity, bias=sn[:, 1:2], scale=sn[:, 0:1]).then_inc(xn_done, 1)
                    wait(act, xn_done, k + 1)
                    nc.scalar.activation(tok[:, 0, :], xn[:], ACT.Copy).then_inc(hi3_done, 1)

                def body(i, par):
                    e_on, c_on, z_on = flags(i)
                    c, e = i - 1, i - 2
                    for n in range(NS):
                        if z_on:
                            decays(i, par, n)
                        if e_on:
                            if n in (1, 2):
                                wait(act, x2_done, e * 4 + 2 + n)
                                product(i, "f", 0, n - 1, consts["ffn_scale"])
                            if n == 3:
                                transposed(i, "n", 1)
                            if n in (4, 5):
                                wait(act, o_stored[n - 4], e * 32 + 16)
                                product(i, "f", 1, n - 4, consts["ffn_scale"])
                        if c_on:
                            if n == 3:
                                high(i, c, 1 - par, 0)
                            if n == 6:
                                transposed(i, "t", 0)
                                high(i, c, 1 - par, 1)
                            if n in (7, 8):
                                wait(act, o_stored[n - 7], c * 32)
                                product(i, "o", 0, n - 7, gs[0][:, 4:5])
                            if n == 9:
                                transposed(i, "t", 1)
                            if n in (10, 11):
                                wait(act, x2_done, c * 4 + n - 9)
                                product(i, "o", 1, n - 10, gs[1][:, 4:5])
                            if n == 12:
                                normalise(c, 0)
                            if n == 15:
                                transposed(i, "n", 0)
                                normalise(c, 1)
                        if z_on and n >= 12:
                            tanh(i, (n - 12) // 2, n % 2)

                drive(act, body, prologue)

            @block.vector
            def _(dve):
                def prologue():
                    dve.wait_ge(carry_set, 1)

                def scans(i, n):
                    for g in range(G):
                        if g % 2 == 0:
                            wait(dve, da_done, i * (NS * 4) + n * 4 + g // 2 + 1)
                        if g % 4 == 0:
                            wait(dve, dbu_done, i * (NS * 2) + n * 2 + g // 4 + 1)
                        if g == 0:
                            wait(dve, carry_done, i * NS + n - 1)
                        ins_ = nc.vector.tensor_tensor_scan(h[n % 2][:, g, :], p_da[g // 2 % 2][:, (g % 2) * T2:(g % 2 + 1) * T2],
                                                            dbu[g // 4][:, g % 4, :], carry[:, n, g:g + 1], ALU.mult, ALU.add)
                        if g % 2:
                            ins_.then_inc(scan_done, 1)

                def add_state(c, par, n):
                    for t in range(TT2):
                        if n == 0:
                            wait(dve, y_loaded[par], (c - par) * 16 + 32)
                        else:
                            wait(dve, y_added[t], c * NS + n)
                        wait(dve, ht_full[t], c * NS + n + 1)
                        nc.vector.scalar_tensor_tensor(out=y[par][t][:], in0=p_ht[t][:], scalar=ct[par][:, t, n:n + 1],
                                                       in1=y[par][t][:], op0=ALU.mult, op1=ALU.add).then_inc(y_added[t], 1)

                def silu_part(i, t, x):
                    b, m = place(i, "z", t, x)
                    wait(dve, th_done, i * 4 + 2 * t + x + 1)
                    wait(dve, gate_done, i * 4)
                    nc.vector.scalar_tensor_tensor(out=q[2 * t + x][:], in0=th[x][:], scalar=1.0, in1=p_g[b][:],
                                                   op0=ALU.add, op1=ALU.mult).then_inc(g_free[b], 1)

                def token_scale(c, cpar, t):
                    k = (c * TT2 + t) * 4
                    wait(dve, gate_done, c * 4 + 2 * t + 2)
                    nc.vector.tensor_reduce(gs[t][:, 0:1], y[cpar][t][:], AX_X, ALU.max,
                                            apply_absolute_value=True).then_inc(tok_chain, 1)
                    wait(dve, tok_chain, k + 1)
                    nc.vector.tensor_scalar(gs[t][:, 0:1], gs[t][:, 0:1], TINY, None, ALU.max).then_inc(tok_chain, 1)
                    wait(dve, tok_chain, k + 2)
                    nc.vector.tensor_scalar(gs[t][:, 1:2].bitcast(I32), gs[t][:, 0:1].bitcast(I32), EXPONENT, None,
                                            ALU.bitwise_and).then_inc(tok_chain, 1)
                    wait(dve, tok_chain, k + 3)
                    nc.vector.reciprocal(gs[t][:, 2:3], gs[t][:, 1:2]).then_inc(tok_chain, 1)
                    nc.vector.tensor_scalar(gs[t][:, 4:5], gs[t][:, 1:2], consts["out_scale"], 1.0 / WS, ALU.mult, ALU.mult)
                    wait(dve, tok_chain, k + 4)
                    nc.vector.tensor_scalar(gs[t][:, 3:4], gs[t][:, 2:3], WS, None, ALU.mult).then_inc(tok_scale, 1)

                def body(i, par):
                    e_on, c_on, z_on = flags(i)
                    for n in range(NS):
                        if z_on:
                            scans(i, n)
                        if n and z_on:
                            add_state(i, par, n - 1)
                        if n == 0 and c_on:
                            add_state(i - 1, 1 - par, NS - 1)
                        if c_on:
                            if n in (2, 3):
                                token_scale(i - 1, 1 - par, n - 2)
                            if n in (10, 13):
                                k = (i - 1) * TT2 + n // 13
                                wait(dve, x2_done, (i - 1) * 4 + 2 * (n // 13) + 2)
                                row_stats(dve, nc, x1[n // 13], stats, mv, vn, small[:, 40:41], ln_chain, stats_ready, scale_ready, k)
                        if z_on and n >= 12:
                            silu_part(i, (n - 12) // 2, n % 2)

                drive(dve, body, prologue)

            @block.tensor
            def _(pe):
                def turn_state(c, n):
                    wait(pe, scan_done, c * (NS * 4) + n * 4 + 4)
                    for t in range(TT2):
                        wait(pe, y_added[t], c * NS + n)
                        for g in range(G):
                            mm = nc.tensor.transpose(p_ht[t][:, g * P:(g + 1) * P], h[n % 2][:, g, t * P:(t + 1) * P], ident[:])
                        mm.then_inc(ht_full[t], 1)

                def unit(i, kind, t, x):
                    b, m = place(i, kind, t, x)
                    wait(pe, g_free[b], m)
                    cols = slice(x * HALF, (x + 1) * HALF)
                    n = 0
                    if kind in "tn":
                        if kind == "t":
                            wait(pe, tok_lo, (i - 1) * TT2 + t + 1)
                        else:
                            wait(pe, lo3_done, (i - 1 - t) * TT2 + t + 1)
                        for g in range(G):
                            mm = nc.tensor.transpose(p_g[b][:].bitcast(F16)[:, g * P:(g + 1) * P],
                                                     tok[:, x, g * P:(g + 1) * P], ident16[:])
                    if kind == "f":
                        for a in range(2):
                            wait_evac(i - 1 if t == 0 else i, "n", t, a)
                        for g in range(G):
                            for a in range(2):
                                mm = nc.tensor.matmul(p_g[b][:], tokt[:, a, g, :], tern[:, g, cols],
                                                      start=(n == 0), stop=(n == 2 * G - 1))
                                n += 1
                    if kind == "o":
                        for a in range(2):
                            wait_evac(i, "t", t, a)
                        if isinstance(i, int) and i == 1:
                            pe.wait_ge(w_loaded, 32)
                        for g in range(G):
                            for ta, wa in ((0, 0), (0, 1), (1, 0)):
                                mm = nc.tensor.matmul(p_g[b][:], tokt[:, ta, g, :], wo[:, wa, g, cols],
                                                      start=(n == 0), stop=(n == 3 * G - 1))
                                n += 1
                    if kind == "z":
                        wait(pe, xz_loaded, i * 32 + 32)
                        if isinstance(i, int) and i == 0:
                            pe.wait_ge(w_loaded, 32)
                        for g in range(G):
                            for xa, wa in ((0, 0), (0, 1), (1, 0)):
                                mm = nc.tensor.matmul(p_g[b][:], xz[:, xa, g, t * P:(t + 1) * P], wz[:, wa, g, cols],
                                                      start=(n == 0), stop=(n == 3 * G - 1))
                                n += 1
                    mm.then_inc(g_full[b], 1)

                def wait_evac(i, kind, t, a):
                    b, m = place(i, kind, t, a)
                    wait(pe, g_free[b], m + 1)

                def body(i, par):
                    e_on, c_on, z_on = flags(i)
                    seq = sequence(i)
                    for n in range(NS):
                        if n and z_on:
                            turn_state(i, n - 1)
                        if n == 0 and c_on:
                            turn_state(i - 1, NS - 1)
                        for slot, kind, t, x in seq:
                            if slot == n:
                                unit(i, kind, t, x)

                drive(pe, body, lambda: None)


def macaron_block(nc, ins, out):
    dram = {
        "x1": nc.dram_tensor("x1_scratch", [L, D], F32, kind="Internal").ap(),
        "xz": nc.dram_tensor("xz_scratch", [C2, 2, P, G * T2], F16, kind="Internal").ap(),
        "y0": nc.dram_tensor("y0_scratch", [L, D], F32, kind="Internal").ap(),
        "dt": nc.dram_tensor("dt_scratch", [C2, P, G, T2], F32, kind="Internal").ap(),
        "dtu": nc.dram_tensor("dtu_scratch", [C2, P, G, T2], F32, kind="Internal").ap(),
        "b": nc.dram_tensor("b_scratch", [C2, NS, T2], F32, kind="Internal").ap(),
        "ct": nc.dram_tensor("ct_scratch", [L, NS], F32, kind="Internal").ap(),
    }
    split = [nc.dram_tensor(f"{n}_split", [P, 2 * G * D], F16, kind="Internal").ap() for n in ("wz", "wo")]
    with ExitStack() as ctx:
        def sem(name):
            return ctx.enter_context(nc.semaphore(name))

        tern = ctx.enter_context(nc.sbuf_tensor("tern", [P, G, D], F16))
        ident = ctx.enter_context(nc.sbuf_tensor("ident", [P, P], F32))
        ident16 = ctx.enter_context(nc.sbuf_tensor("ident16", [P, P], F16))
        c = ctx.enter_context(nc.sbuf_tensor("consts", [P, 8], F32))
        consts = {n: c[:, k:k + 1] for k, n in enumerate(("ffn_scale", "u_scale", "half_z", "out_scale", "minus_half", "one"))}
        with nc.sbuf_tensor("wu", [P, 2, G, D], F16) as wu_t:
            wu = [wu_t[:, 0], wu_t[:, 1]]
            prepare_weights(nc, sem, ins["W_ffn"], ins["W_in"], ins["W_out"], tern, wu, consts, ident, ident16, split)
            first_pass(nc, sem, ins, tern, wu, consts, ident, dram)
        second_pass(nc, sem, ins, tern, consts, ident, ident16, split, dram, out)


def kernel(L0_attn_x, L0_attn_W_in, L0_attn_conv_w, L0_attn_conv_b, L0_attn_W_xproj, L0_attn_W_dt, L0_attn_b_dt,
           L0_attn_A_log, L0_attn_Dskip, L0_attn_W_out, L0_ffn_weight, L0_ffn_bias):
    import numpy as np
    import concourse.bacc as bacc
    from concourse.bass_utils import run_bass_kernel_spmd

    arrays = {"x": L0_attn_x.reshape(L, D), "W_ffn": L0_ffn_weight.T, "bias": L0_ffn_bias, "W_in": L0_attn_W_in.T,
              "W_out": L0_attn_W_out.T, "W_xproj": L0_attn_W_xproj.T, "W_dt": L0_attn_W_dt.T,
              "conv_w": L0_attn_conv_w, "conv_b": L0_attn_conv_b, "b_dt": L0_attn_b_dt, "A_log": L0_attn_A_log,
              "Dskip": L0_attn_Dskip}
    arrays = {n: np.ascontiguousarray(a) for n, a in arrays.items()}
    nc = bacc.Bacc("TRN2", target_bir_lowering=False, num_devices=1)
    ins = {n: nc.dram_tensor("in_" + n, list(a.shape), mybir.dt.from_np(a.dtype), kind="ExternalInput").ap()
           for n, a in arrays.items()}
    out = nc.dram_tensor("out", [L, D], F32, kind="ExternalOutput").ap()
    macaron_block(nc, ins, out)
    r = run_bass_kernel_spmd(nc, [{"in_" + n: a for n, a in arrays.items()}], core_ids=[0])
    return r.results[0]["out"].reshape(1, L, D)
```

```python
from contextlib import ExitStack

import concourse.bass as bass
from concourse import mybir

ALU = mybir.AluOpType
ACT = mybir.ActivationFunctionType
AX_X = mybir.AxisListType.X
F32 = mybir.dt.float32
F16 = mybir.dt.float16
I32 = mybir.dt.int32
RADD = bass.bass_isa.ReduceOp.add
RABSMAX = bass.bass_isa.ReduceOp.absmax

P = 128
L, D = 4096, 1024
NS = 16
R = 64
G = D // P
HALF = 512
T1 = 512
C1 = L // T1
TT1 = T1 // P
T2 = 256
C2 = L // T2
TT2 = T2 // P
XS = 512.0
WS = 8192.0
EXPONENT = 0x7F800000
TINY = 1e-30
EPS = 1e-5
EPS_FFN = 1e-10
ROUND = 1.5 * 2.0 ** 23


def wait(eng, sem, count):
    if isinstance(count, int) and count <= 0:
        return
    eng.wait_ge(sem, count)


def wait_alone(eng, sem, count):
    if not isinstance(count, int):
        eng.wait_ge(sem, 1)
    wait(eng, sem, count)


def prepare_weights(nc, sem, w_ffn, w_in, w_out, tern, wu, consts, ident, split_dram):
    srcs = [w_ffn.rearrange("(k p) m -> p k m", p=P),
            w_in.rearrange("(k p) m -> p k m", p=P)[:, :, 0:D],
            w_in.rearrange("(k p) m -> p k m", p=P)[:, :, D:2 * D],
            w_out.rearrange("(k p) m -> p k m", p=P)]
    with ExitStack() as ctx:
        def sb(name, shape, dt):
            return ctx.enter_context(nc.sbuf_tensor(name, shape, dt))

        stage = [sb(f"stage{i}", [P, G, D], F32) for i in range(2)]
        parts = sb("parts", [P, 2, G, D], F16)
        part = sb("part", [P, 4], F32)
        total = sb("total", [P, 4], F32)
        tmp = sb("tmp", [P, 4, 4], F32)

        w_loaded = [sem(f"w_loaded{i}") for i in range(4)]
        part_done, total_done, small = sem("w_part_done"), sem("w_total_done"), sem("w_small")
        factor_done, hi_done, lo_done = sem("w_factor_done"), sem("w_hi_done"), sem("w_lo_done")
        tern_step, parts_stored, ident_step = sem("tern_step"), sem("w_parts_stored"), sem("ident_step")

        with nc.Block() as block:
            @block.sync
            def _(sp):
                for m in range(4):
                    if m == 2:
                        sp.wait_ge(tern_step, 3)
                    if m == 3:
                        sp.wait_ge(hi_done, 1)
                        sp.wait_ge(lo_done, 1)
                    sp.dma_start(stage[m % 2][:], srcs[m]).then_inc(w_loaded[m], 16)
                for m in (2, 3):
                    sp.wait_ge(hi_done, m)
                    sp.wait_ge(lo_done, m)
                    sp.dma_start(split_dram[m - 2], parts[:].rearrange("p a k m -> p (a k m)")).then_inc(parts_stored, 16)
                sp.wait_ge(parts_stored, 32)

            @block.gpsimd
            def _(pool):
                nc.gpsimd.memset(consts["minus_half"], -0.5)
                nc.gpsimd.memset(consts["one"], 1.0)
                nc.gpsimd.memset(ident[:], 0.0).then_inc(ident_step, 1)
                pool.wait_ge(ident_step, 1)
                nc.gpsimd.affine_select(out=ident[:], in_=ident[:], compare_op=ALU.not_equal, fill=1.0, base=0,
                                        pattern=[[-1, P]], channel_multiplier=1).then_inc(ident_step, 1)
                for m in range(4):
                    pool.wait_ge(part_done, m + 1)
                    nc.gpsimd.partition_all_reduce(total[:, m:m + 1], part[:, m:m + 1], P,
                                                   RADD if m == 0 else RABSMAX).then_inc(total_done, 1)

            @block.scalar
            def _(act):
                for m in range(1, 4):
                    hi = wu[0] if m == 1 else parts[:, 0]
                    act.wait_ge(factor_done, m)
                    if m == 3:
                        act.wait_ge(parts_stored, 16)
                    nc.scalar.activation(hi, stage[m % 2][:], ACT.Copy, scale=tmp[:, m, 2:3]).then_inc(hi_done, 1)

            @block.vector
            def _(dve):
                steps = [0]

                def link(ins):
                    steps[0] += 1
                    ins.then_inc(small, 1)
                    dve.wait_ge(small, steps[0])

                def reduce(m):
                    dve.wait_ge(w_loaded[m], 16)
                    nc.vector.tensor_reduce(part[:, m:m + 1], stage[m % 2][:].rearrange("p k m -> p (k m)"), AX_X,
                                            ALU.add if m == 0 else ALU.max,
                                            apply_absolute_value=True).then_inc(part_done, 1)

                def ternary():
                    dve.wait_ge(total_done, 1)
                    link(nc.vector.tensor_scalar(tmp[:, 0, 0:1], total[:, 0:1], 1.0 / (D * D), None, ALU.mult))
                    link(nc.vector.tensor_scalar(tmp[:, 0, 1:2], tmp[:, 0, 0:1], EPS_FFN, None, ALU.add))
                    link(nc.vector.reciprocal(tmp[:, 0, 2:3], tmp[:, 0, 1:2]))
                    link(nc.vector.tensor_scalar(consts["ffn_scale"], tmp[:, 0, 0:1], 0.5 / XS, None, ALU.mult))
                    w = stage[0][:].rearrange("p k m -> p (k m)")
                    nc.vector.tensor_scalar(w, w, tmp[:, 0, 2:3], -1.0, ALU.mult, ALU.max).then_inc(tern_step, 1)
                    dve.wait_ge(tern_step, 1)
                    nc.vector.tensor_scalar(w, w, 1.0, ROUND, ALU.min, ALU.add).then_inc(tern_step, 1)
                    dve.wait_ge(tern_step, 2)
                    nc.vector.tensor_scalar(tern[:].rearrange("p k m -> p (k m)"), w, -ROUND, None,
                                            ALU.add).then_inc(tern_step, 1)

                def factor(m):
                    dve.wait_ge(total_done, m + 1)
                    link(nc.vector.tensor_scalar(tmp[:, m, 0:1], total[:, m:m + 1], TINY, None, ALU.max))
                    link(nc.vector.tensor_scalar(tmp[:, m, 1:2].bitcast(I32), tmp[:, m, 0:1].bitcast(I32),
                                                 EXPONENT, None, ALU.bitwise_and))
                    link(nc.vector.reciprocal(tmp[:, m, 3:4], tmp[:, m, 1:2]))
                    nc.vector.tensor_scalar(tmp[:, m, 2:3], tmp[:, m, 3:4], WS, None, ALU.mult).then_inc(factor_done, 1)
                    dve.wait_ge(factor_done, m)

                def low(m):
                    hi, lo = (wu[0], wu[1]) if m == 1 else (parts[:, 0], parts[:, 1])
                    dve.wait_ge(hi_done, m)
                    nc.vector.scalar_tensor_tensor(out=lo.rearrange("p k m -> p (k m)"),
                                                   in0=stage[m % 2][:].rearrange("p k m -> p (k m)"),
                                                   scalar=tmp[:, m, 2:3], in1=hi.rearrange("p k m -> p (k m)"),
                                                   op0=ALU.mult, op1=ALU.subtract).then_inc(lo_done, 1)

                reduce(0)
                reduce(1)
                ternary()
                factor(1)
                low(1)
                for m in (2, 3):
                    reduce(m)
                    factor(m)
                    if m == 3:
                        dve.wait_ge(parts_stored, 16)
                    low(m)
                link(nc.vector.tensor_scalar(consts["u_scale"], tmp[:, 1, 1:2], 1.0 / (WS * XS), None, ALU.mult))
                link(nc.vector.tensor_scalar(consts["half_z"], tmp[:, 2, 1:2], 0.5 / (WS * XS), None, ALU.mult))
                link(nc.vector.tensor_scalar(consts["out_scale"], tmp[:, 3, 1:2], consts["half_z"], 1.0 / WS,
                                             ALU.mult, ALU.mult))


def row_stats(dve, nc, row, stats, mv, vn, idle, chain, ready, read, k):
    for h in range(2):
        ins = nc.vector.bn_stats(stats[:, 6 * h:6 * h + 6], row[:, h * HALF:(h + 1) * HALF])
    ins.then_inc(chain, 1)
    wait(dve, chain, k * 2 + 1)
    nc.vector.memset(idle, 0.0)
    nc.vector.bn_aggr(mv[:, 0:2], stats[:, 0:12]).then_inc(chain, 1)
    wait(dve, chain, k * 2 + 2)
    wait(dve, read, k)
    nc.vector.tensor_scalar(vn[:, 0:1], mv[:, 1:2], EPS, 1.0 / (XS * XS), ALU.add, ALU.mult)
    nc.vector.tensor_scalar(vn[:, 1:2], mv[:, 0:1], -1.0, None, ALU.mult).then_inc(ready, 1)


def row_scale(pool, nc, vn, minus_half, sn, ready, chain, done, used, k):
    wait(pool, ready, k + 1)
    wait(pool, used, k)
    nc.gpsimd.tensor_tensor(sn[:, 0:1], vn[:, 0:1], minus_half, ALU.pow).then_inc(chain, 1)
    wait(pool, chain, k + 1)
    nc.gpsimd.tensor_tensor(sn[:, 1:2], vn[:, 1:2], sn[:, 0:1], ALU.mult).then_inc(done, 1)


def first_pass(nc, sem, ins, tern, wu, consts, ident, dram):
    with ExitStack() as ctx:
        def sb(name, shape, dt=F32):
            return ctx.enter_context(nc.sbuf_tensor(name, shape, dt))

        wx = sb("wx", [P, G, R + 2 * NS])
        wdt = sb("wdt", [R, D])
        half_bias = sb("half_bias", [P, D])
        conv_w = sb("conv_w", [P, G, 4])
        conv_b = sb("conv_b", [P, G])
        dt_b = sb("dt_b", [P, G])
        dskip = sb("dskip", [P, G])
        xin = [sb(f"xin{i}", [P, D]) for i in range(2)]
        x1 = [sb(f"x1_{i}", [P, D]) for i in range(2)]
        xn = [sb(f"xn{i}", [P, D]) for i in range(2)]
        xt = sb("xt", [P, 2, G, P], F16)
        xz = [sb(f"xz{i}", [P, 2, 2, G, T2], F16) for i in range(2)]
        up = [sb(f"up{i}", [P, T1 + 3]) for i in range(2)]
        acc = [sb(f"acc{i}", [P, T1]) for i in range(2)]
        halo = sb("halo", [P, G, 3])
        u = [sb(f"u{i}", [P, G, T1]) for i in range(2)]
        ud = [sb(f"ud{i}", [P, T1]) for i in range(2)]
        y0 = [sb(f"y0_{i}", [P, TT1, 2 * P]) for i in range(2)]
        xdbl = sb("xdbl", [R + 2 * NS, T1])
        ct = sb("ct", [P, TT1, NS])
        rel = [sb(f"rel{i}", [P, T1]) for i in range(2)]
        ex = [sb(f"ex{i}", [P, T1]) for i in range(2)]
        lg = [sb(f"lg{i}", [P, T1]) for i in range(2)]
        res = sb("res", [P, T1])
        dt = [sb(f"dt{i}", [P, T1]) for i in range(2)]
        dtu = [sb(f"dtu{i}", [P, T1]) for i in range(2)]
        small = sb("small1", [P, 64])
        stats = [small[:, 0:12], small[:, 12:24]]
        mv = [small[:, 24:26], small[:, 26:28]]
        vn = [small[:, 28:30], small[:, 30:32]]
        sn = [small[:, 32:34], small[:, 34:36]]
        minus_half = consts["minus_half"]

        def bank(name, shape=(P, HALF)):
            return ctx.enter_context(nc.psum_tensor(name, list(shape), F32))

        p_tr = [bank(f"p_tr{i}") for i in range(2)]
        p_ffn = [bank(f"p_ffn{i}") for i in range(2)]
        p_u = [bank(f"p_u{i}") for i in range(2)]
        p_s = [bank(f"p_s{i}") for i in range(2)]

        const_loaded, const_done = sem("const_loaded1"), sem("const_done1")
        x_loaded = [sem(f"x_loaded{i}") for i in range(2)]
        xb_done, x1_done = sem("xb_done"), sem("x1_done")
        x1_stored = [sem(f"x1_stored{i}") for i in range(2)]
        ln_chain = [sem(f"ln{i}_chain") for i in range(2)]
        stats_ready = [sem(f"stats{i}_ready") for i in range(2)]
        pow_done = [sem(f"pow{i}_done") for i in range(2)]
        scale_ready = [sem(f"scale{i}_ready") for i in range(2)]
        xn_done = [sem(f"xn{i}_done") for i in range(2)]
        tr_full = [sem(f"tr_full{i}") for i in range(2)]
        hi_done = [sem(f"hi_done{i}") for i in range(2)]
        tr_split = [sem(f"tr_split{i}") for i in range(2)]
        ffn_full = sem("ffn_full")
        xz_stored = [sem(f"xz_stored{i}") for i in range(2)]
        u_full, up_done, conv_chain, conv_done = sem("u_full"), sem("up_done"), sem("conv_chain"), sem("conv_done")
        silu_done = sem("silu_done")
        s_full = [sem(f"s_full{i}") for i in range(2)]
        s_free = [sem(f"s_free{i}") for i in range(2)]
        ud_done, y0_stored = sem("ud_done"), [sem(f"y0_stored{i}") for i in range(2)]
        b_stored, ct_stored = sem("b_stored"), sem("ct_stored")
        abs_done, exp_done, ln_done = sem("abs_done"), sem("exp_done"), sem("ln_done")
        sp_chain, dt_done, dtu_done = sem("softplus_chain"), sem("dt_done"), sem("dtu_done")
        dt_stored = [sem(f"dt_stored{i}") for i in range(2)]

        units = [("y", 0), ("y", 1), ("x", 0), ("c", 0), ("d", 0), ("y", 2), ("d", 1), ("d", 2), ("y", 3), ("d", 3),
                 ("y", 4), ("d", 4), ("y", 5), ("d", 5), ("d", 6), ("y", 6), ("d", 7), ("y", 7)]
        per_phase = [(1, 1, 1, 1), (1, 1, 1, 2), (1, 1, 1, 1), (1, 2, 1, 1)]
        NU = len(units) // 2

        def last(k):
            return isinstance(k, int) and k + 1 >= L // P

        def s_units(j, phase, kinds="xycd"):
            before = sum(per_phase[j][:phase]) + sum(sum(n) for n in per_phase[:j])
            return [(v, *units[v]) for v in range(before, before + per_phase[j][phase]) if units[v][0] in kinds]

        def s_units_before(j, phase):
            if phase:
                return s_units(j, phase - 1, "d")
            return s_units(j - 1, 3, "d") if j else []

        def unit_at(d, kind, g):
            v = units.index((kind, g))
            return v % 2, d * NU + v // 2 + 1

        def had_u(i, j):
            before = i if j else i - 1
            return not isinstance(i, int) or 0 <= before < C1

        def drive(eng, step, prologue=None):
            if prologue:
                prologue()
            for j in range(TT1):
                step(-1, 1, j, True, False, False)
            for j in range(TT1):
                step(0, 0, j, True, True, False)
            for j in range(TT1):
                step(1, 1, j, True, True, True)
            with eng.Fori(0, (C1 - 4) // 2) as turn:
                for o in range(2):
                    for j in range(TT1):
                        step(turn * 2 + 2 + o, o, j, True, True, True)
            for j in range(TT1):
                step(C1 - 2, C1 % 2, j, True, True, True)
            for j in range(TT1):
                step(C1 - 1, (C1 - 1) % 2, j, False, True, True)
            for j in range(TT1):
                step(C1, C1 % 2, j, False, False, True)

        with nc.Block() as block:
            @block.sync
            def _(sp):
                loads = [(wx[:], ins["W_xproj"].rearrange("(g p) m -> p g m", p=P)), (wdt[:], ins["W_dt"]),
                         (half_bias[:], ins["bias"].partition_broadcast(P)),
                         (conv_w[:], ins["conv_w"].rearrange("(g p) k -> p g k", p=P)),
                         (conv_b[:], ins["conv_b"].rearrange("(g p) -> p g", p=P)),
                         (dt_b[:], ins["b_dt"].rearrange("(g p) -> p g", p=P)),
                         (dskip[:], ins["Dskip"].rearrange("(g p) -> p g", p=P))]

                def load_x(k, b, row):
                    wait_alone(sp, xn_done[0], k - 1)
                    wait_alone(sp, xb_done, k - 1)
                    sp.dma_start(xin[b][:], ins["x"][bass.ds(row, P), :]).then_inc(x_loaded[b], 16)

                load_x(0, 0, 0)
                load_x(1, 1, P)
                with nc.allow_non_contiguous_dma(reason="small constants"):
                    for dst, src in loads:
                        sp.dma_start(dst, src).then_inc(const_loaded, 16)

                def s_stores(d, j, phase):
                    for v, kind, g in s_units(j, phase, "xcy") + s_units_before(j, phase):
                        if kind == "x":
                            wait_alone(sp, s_free[v % 2], d * NU + v // 2 + 1)
                            sp.dma_start(dram["b"][bass.ds(d * 2, 2)].rearrange("h n t -> n h t"),
                                         xdbl[R:R + NS, :].rearrange("n (h t) -> n h t", h=2)).then_inc(b_stored, 16)
                        if kind == "c":
                            wait_alone(sp, s_free[v % 2], d * NU + v // 2 + 1)
                            with nc.allow_non_contiguous_dma(reason="64 bytes a token"):
                                sp.dma_start(dram["ct"][bass.ds(d * T1, T1), :].rearrange("(t p) n -> p t n", p=P),
                                             ct[:]).then_inc(ct_stored, 16)
                        if kind == "y" and g % 2:
                            wait_alone(sp, s_free[v % 2], d * NU + v // 2 + 1)
                            sp.dma_start(dram["y0"][bass.ds(d * T1, T1), (g - 1) * P:(g + 1) * P].rearrange(
                                "(t p) n -> p t n", p=P), y0[g // 2 % 2][:]).then_inc(y0_stored[g // 2 % 2], 16)
                        if kind == "d":
                            wait_alone(sp, dt_done, d * G + g + 1)
                            wait_alone(sp, dtu_done, d * G + g + 1)
                            for name, tile in (("dt", dt), ("dtu", dtu)):
                                sp.dma_start(dram[name][bass.ds(d * 2, 2), :, g].rearrange("h p t -> p h t"),
                                             tile[g % 2][:].rearrange("p (h t) -> p h t", h=2)
                                             ).then_inc(dt_stored[g % 2], 16)

                def step(i, par, j, f_on, u_on, s_on):
                    f, k = i + 1, (i + 1) * TT1 + j
                    if s_on:
                        s_stores(i - 1, j, 0)
                        s_stores(i - 1, j, 1)
                    if f_on:
                        wait_alone(sp, x1_done, k * 2 + 2)
                        sp.dma_start(dram["x1"][bass.ds(k * P, P), :], x1[j % 2][:]).then_inc(x1_stored[j % 2], 16)
                        if not last(k + 1):
                            load_x(k + 2, j % 2, k * P + 2 * P)
                    if s_on:
                        s_stores(i - 1, j, 2)
                        s_stores(i - 1, j, 3)
                    if f_on and j == TT1 - 1:
                        for b in range(2):
                            wait_alone(sp, tr_split[b], k * 2 + 2)
                        for a in range(2):
                            sp.dma_start(dram["xz"][bass.ds(f * 2, 2), a].rearrange("h p n -> p h n"),
                                         xz[1 - par][:, a].rearrange("p h k t -> p h (k t)")
                                         ).then_inc(xz_stored[1 - par], 16)

                drive(sp, step)
                for b in range(2):
                    sp.wait_ge(x1_stored[b], 16 * (L // P) // 2)
                    sp.wait_ge(xz_stored[b], 32 * C1 // 2)
                    sp.wait_ge(y0_stored[b], 16 * C1 * 2)
                    sp.wait_ge(dt_stored[b], 32 * C1 * G // 2)
                sp.wait_ge(b_stored, 16 * C1)
                sp.wait_ge(ct_stored, 16 * C1)

            @block.gpsimd
            def _(pool):
                def prologue():
                    row_scale(pool, nc, vn[0], minus_half, sn[0], stats_ready[0], pow_done[0], scale_ready[0],
                              xn_done[0], 0)

                def s_work(d, dpar, j, phase):
                    for v, kind, g in s_units_before(j, phase):
                        q = d * G + g
                        wait(pool, dt_done, q + 1)
                        wait(pool, dt_stored[g % 2], (d * (G // 2) + g // 2) * 32)
                        nc.gpsimd.tensor_tensor(dtu[g % 2][:], dt[g % 2][:], u[dpar][:, g, :], ALU.mult).then_inc(dtu_done, 1)

                def step(i, par, j, f_on, u_on, s_on):
                    k = (i + 1) * TT1 + j
                    if f_on:
                        wait(pool, x_loaded[j % 2], ((i + 1) * 2 + j // 2 + 1) * 16)
                        wait(pool, x1_stored[j % 2], ((i + 1) * 2 + j // 2) * 16)
                        wait(pool, xn_done[1], k - 1)
                        if isinstance(k, int) and k == 0:
                            pool.wait_ge(const_done, 1)
                        nc.gpsimd.tensor_tensor(x1[j % 2][:], xin[j % 2][:], half_bias[:], ALU.add).then_inc(xb_done, 1)
                        if not last(k):
                            row_scale(pool, nc, vn[0], minus_half, sn[0], stats_ready[0], pow_done[0],
                                      scale_ready[0], xn_done[0], k + 1)
                    if s_on:
                        s_work(i - 1, 1 - par, j, 0)
                        s_work(i - 1, 1 - par, j, 1)
                    if f_on:
                        row_scale(pool, nc, vn[1], minus_half, sn[1], stats_ready[1], pow_done[1],
                                  scale_ready[1], xn_done[1], k)
                    if s_on:
                        s_work(i - 1, 1 - par, j, 2)
                        s_work(i - 1, 1 - par, j, 3)

                drive(pool, step, prologue)

            @block.scalar
            def _(act):
                def normalise(n, src, k):
                    wait(act, scale_ready[n], k + 1)
                    wait(act, tr_full[1], k * 2 - 1 + n)
                    nc.scalar.activation(xn[n][:], src, ACT.Identity, bias=sn[n][:, 1:2],
                                         scale=sn[n][:, 0:1]).then_inc(xn_done[n], 1)

                def high(n, k, dst, b):
                    wait(act, tr_full[b], k * 2 + n + 1)
                    nc.scalar.activation(dst, p_tr[b][:].rearrange("p (g t) -> p g t", g=4), ACT.Copy).then_inc(hi_done[b], 1)

                def u_work(i, g):
                    q = i * G + g
                    wait(act, u_full, q + 1)
                    wait(act, conv_done, q - 1)
                    nc.scalar.activation(up[g % 2][:, 3:3 + T1], p_u[g % 2][:], ACT.Copy,
                                         scale=consts["u_scale"]).then_inc(up_done, 1)

                def silu(i, par, g):
                    q = i * G + g
                    wait(act, conv_done, q + 1)
                    if g == 0:
                        wait(act, dtu_done, (i - 1) * G)
                        wait(act, ud_done, (i - 1) * G)
                    nc.scalar.activation(u[par][:, g, :], acc[g % 2][:], ACT.Silu).then_inc(silu_done, 1)

                def s_work(d, j, phase):
                    for v, kind, g in s_units(j, phase, "xd"):
                        if kind == "x":
                            wait(act, s_full[v % 2], d * NU + v // 2 + 1)
                            wait(act, b_stored, d * 16)
                            b, m = unit_at(d - 1, "d", G - 1)
                            wait(act, s_full[b], m)
                            nc.scalar.activation(xdbl[:], p_s[v % 2][0:R + 2 * NS, :], ACT.Copy).then_inc(s_free[v % 2], 1)
                        if kind == "d":
                            q = d * G + g
                            wait(act, s_full[v % 2], d * NU + v // 2 + 1)
                            wait(act, dt_done, q - 1)
                            nc.scalar.activation(rel[g % 2][:], p_s[v % 2][:], ACT.Relu, bias=dt_b[:, g:g + 1])
                            nc.scalar.activation(ex[g % 2][:], p_s[v % 2][:], ACT.Abs, bias=dt_b[:, g:g + 1]
                                                 ).then_inc(s_free[v % 2], 1)
                            wait(act, s_free[v % 2], d * NU + v // 2 + 1)
                            nc.scalar.activation(ex[g % 2][:], ex[g % 2][:], ACT.Exp, scale=-1.0).then_inc(exp_done, 1)
                            wait(act, exp_done, q + 1)
                            nc.scalar.activation(lg[g % 2][:], ex[g % 2][:], ACT.Ln, bias=1.0).then_inc(ln_done, 1)

                def prologue():
                    act.wait_ge(x_loaded[0], 16)
                    act.wait_ge(const_loaded, 16 * 7)
                    nc.scalar.mul(half_bias[:], half_bias[:], 0.5).then_inc(const_done, 1)
                    normalise(0, xin[0][:], 0)

                def step(i, par, j, f_on, u_on, s_on):
                    f = i + 1
                    k = f * TT1 + j
                    before = (i if j else i - 1, (2 * j - 1) % G)
                    if had_u(i, j):
                        u_work(*before)
                    if f_on:
                        wait(act, ffn_full, k * 2)
                        for b in range(2):
                            high(0, k, xt[:, 0, 4 * b:4 * b + 4, :], b)
                    if s_on:
                        s_work(i - 1, j, 0)
                        s_work(i - 1, j, 1)
                    if f_on and not last(k):
                        normalise(0, xin[(j + 1) % 2][:], k + 1)
                    if had_u(i, j):
                        silu(before[0], par if j else 1 - par, before[1])
                    if s_on and j == 0:
                        s_work(i - 1, j, 2)
                    if f_on:
                        normalise(1, x1[j % 2][:], k)
                    if u_on:
                        u_work(i, 2 * j)
                    if f_on:
                        if j == 0:
                            wait(act, u_full, (f - 1) * G)
                            wait(act, xz_stored[1 - par], (f - (1 - par)) * 16)
                        for b in range(2):
                            high(1, k, xz[1 - par][:, 0, j // 2, 4 * b:4 * b + 4, (j % 2) * P:(j % 2 + 1) * P], b)
                    if s_on and j:
                        s_work(i - 1, j, 2)
                    if s_on:
                        s_work(i - 1, j, 3)
                    if u_on:
                        silu(i, par, 2 * j)

                drive(act, step, prologue)

            @block.vector
            def _(dve):
                def low(n, k, src_hi, dst, b):
                    wait(dve, hi_done[b], k * 2 + n + 1)
                    nc.vector.tensor_tensor(dst, p_tr[b][:].rearrange("p (g t) -> p g t", g=4), src_hi,
                                            ALU.subtract).then_inc(tr_split[b], 1)

                def conv(i, g):
                    q = i * G + g
                    src, dst = up[g % 2], acc[g % 2]
                    nc.vector.tensor_copy(src[:, 0:3], halo[:, g, :]).then_inc(conv_chain, 1)
                    wait(dve, conv_chain, q * 4 + 1)
                    wait(dve, up_done, q + 1)
                    wait(dve, silu_done, q - 1)
                    nc.vector.tensor_scalar(dst[:], src[:, 0:T1], conv_w[:, g, 0:1], conv_b[:, g:g + 1],
                                            ALU.mult, ALU.add).then_inc(conv_chain, 1)
                    for tap in (1, 2):
                        wait(dve, conv_chain, q * 4 + 1 + tap)
                        nc.vector.scalar_tensor_tensor(out=dst[:], in0=src[:, tap:tap + T1], scalar=conv_w[:, g, tap:tap + 1],
                                                       in1=dst[:], op0=ALU.mult, op1=ALU.add).then_inc(conv_chain, 1)
                    nc.vector.tensor_copy(halo[:, g, :], src[:, T1:T1 + 3])
                    wait(dve, conv_chain, q * 4 + 4)
                    nc.vector.scalar_tensor_tensor(out=dst[:], in0=src[:, 3:3 + T1], scalar=conv_w[:, g, 3:4],
                                                   in1=dst[:], op0=ALU.mult, op1=ALU.add).then_inc(conv_done, 1)

                def s_work(d, dpar, j, phase):
                    for v, kind, g in s_units(j, phase, "cy") + s_units_before(j, phase):
                        q = d * G + g
                        if kind == "c":
                            wait(dve, s_full[v % 2], d * NU + v // 2 + 1)
                            wait(dve, ct_stored, d * 16)
                            nc.vector.tensor_copy(ct[:], p_s[v % 2][:, 0:TT1 * P].rearrange(
                                "p (t n) -> p t n", t=TT1)[:, :, R + NS:R + 2 * NS]).then_inc(s_free[v % 2], 1)
                        if kind == "y":
                            wait(dve, s_full[v % 2], d * NU + v // 2 + 1)
                            wait(dve, y0_stored[g // 2 % 2], (d * 2 + g // 4) * 16)
                            nc.vector.tensor_copy(y0[g // 2 % 2][:, :, (g % 2) * P:(g % 2 + 1) * P],
                                                  p_s[v % 2][:].rearrange("p (t n) -> p t n", t=TT1)).then_inc(s_free[v % 2], 1)
                            if g + 2 < G:
                                times_dskip(d, dpar, g + 2)
                        if kind == "d":
                            wait(dve, dt_done, q)
                            wait(dve, exp_done, q + 1)
                            nc.vector.tensor_scalar(res[:], ex[g % 2][:], 1.0, -1.0, ALU.add, ALU.add).then_inc(sp_chain, 1)
                            wait(dve, sp_chain, q * 3 + 1)
                            nc.vector.tensor_tensor(res[:], ex[g % 2][:], res[:], ALU.subtract).then_inc(sp_chain, 1)
                            wait(dve, ln_done, q + 1)
                            wait(dve, sp_chain, q * 3 + 2)
                            nc.vector.tensor_tensor(res[:], lg[g % 2][:], res[:], ALU.add).then_inc(sp_chain, 1)
                            wait(dve, sp_chain, q * 3 + 3)
                            wait(dve, dtu_done, q - 1)
                            wait(dve, dt_stored[g % 2], (d * (G // 2) + g // 2) * 32)
                            nc.vector.tensor_tensor(dt[g % 2][:], res[:], rel[g % 2][:], ALU.add).then_inc(dt_done, 1)

                def times_dskip(d, dpar, g):
                    b, m = unit_at(d, "y", g - 2) if g >= 2 else unit_at(d - 1, "y", g + 6)
                    wait(dve, s_full[b], m)
                    wait(dve, silu_done, d * G + g + 1)
                    nc.vector.tensor_scalar(ud[g % 2][:], u[dpar][:, g, :], dskip[:, g:g + 1], None,
                                            ALU.mult).then_inc(ud_done, 1)

                def prologue():
                    nc.vector.memset(halo[:], 0.0)
                    dve.wait_ge(x_loaded[0], 16)
                    row_stats(dve, nc, xin[0], stats[0], mv[0], vn[0], small[:, 40:41], ln_chain[0], stats_ready[0], scale_ready[0], 0)
                    dve.wait_ge(const_loaded, 16 * 7)

                def step(i, par, j, f_on, u_on, s_on):
                    f, d = i + 1, i - 1
                    k = f * TT1 + j
                    if f_on:
                        for b in range(2):
                            low(0, k, xt[:, 0, 4 * b:4 * b + 4, :], xt[:, 1, 4 * b:4 * b + 4, :], b)
                    if f_on:
                        if not last(k):
                            wait(dve, x_loaded[(j + 1) % 2], (f * 2 + (j + 1) // 2 + 1) * 16)
                            row_stats(dve, nc, xin[(j + 1) % 2], stats[0], mv[0], vn[0], small[:, 40:41], ln_chain[0],
                                      stats_ready[0], scale_ready[0], k + 1)
                    if had_u(i, j):
                        conv(i if j else i - 1, (2 * j - 1) % G)
                    if s_on:
                        s_work(d, 1 - par, j, 0)
                        s_work(d, 1 - par, j, 1)
                    if f_on:
                        wait(dve, xb_done, k + 1)
                        for h in range(2):
                            wait(dve, ffn_full, k * 2 + h + 1)
                            nc.vector.scalar_tensor_tensor(out=x1[j % 2][:, h * HALF:(h + 1) * HALF], in0=p_ffn[h][:],
                                                           scalar=consts["ffn_scale"],
                                                           in1=x1[j % 2][:, h * HALF:(h + 1) * HALF],
                                                           op0=ALU.mult, op1=ALU.add).then_inc(x1_done, 1)
                        wait(dve, x1_done, k * 2 + 2)
                        row_stats(dve, nc, x1[j % 2], stats[1], mv[1], vn[1], small[:, 41:42], ln_chain[1], stats_ready[1],
                                  scale_ready[1], k)
                    if s_on:
                        s_work(d, 1 - par, j, 2)
                    if f_on:
                        for b in range(2):
                            hi, lo = (xz[1 - par][:, a, j // 2, 4 * b:4 * b + 4, (j % 2) * P:(j % 2 + 1) * P] for a in range(2))
                            low(1, k, hi, lo, b)
                    if u_on:
                        conv(i, 2 * j)
                    if s_on:
                        s_work(d, 1 - par, j, 3)
                    if u_on and j == TT1 - 1:
                        times_dskip(i, par, 0)
                        times_dskip(i, par, 1)

                drive(dve, step, prologue)

            @block.tensor
            def _(pe):
                def turn(n, k):
                    wait(pe, xn_done[n], k + 1)
                    for b in range(2):
                        wait(pe, tr_split[b], k * 2 + n)
                        for q in range(4):
                            g = 4 * b + q
                            mm = nc.tensor.transpose(p_tr[b][:, q * P:(q + 1) * P], xn[n][:, g * P:(g + 1) * P], ident[:])
                        mm.then_inc(tr_full[b], 1)

                def ffn(k):
                    wait(pe, x1_done, k * 2)
                    for h in range(2):
                        for g in range(G):
                            if h == 0 and g % 4 == 0:
                                wait(pe, tr_split[g // 4], k * 2 + 1)
                            for a in range(2):
                                mm = nc.tensor.matmul(p_ffn[h][:], xt[:, a, g, :], tern[:, g, h * HALF:(h + 1) * HALF],
                                                      start=(g == 0 and a == 0), stop=(g == G - 1 and a == 1))
                        mm.then_inc(ffn_full, 1)

                def u_product(i, par, g):
                    wait(pe, up_done, i * G + g - 1)
                    n = 0
                    for kk in range(G):
                        for wa, xa in ((0, 0), (0, 1), (1, 0)):
                            mm = nc.tensor.matmul(p_u[g % 2][:].rearrange("p (h t) -> p h t", h=2),
                                                  wu[wa][:, kk, g * P:(g + 1) * P], xz[par][:, xa, :, kk, :],
                                                  start=(n == 0), stop=(n == 3 * G - 1))
                            n += 1
                    mm.then_inc(u_full, 1)

                def s_work(d, dpar, j, phase):
                    for v, kind, g in s_units(j, phase):
                        wait(pe, s_free[v % 2], d * NU + v // 2)
                        ps = p_s[v % 2]
                        if kind == "x":
                            wait(pe, silu_done, d * G + G)
                            for q in range(G):
                                mm = nc.tensor.matmul(ps[0:R + 2 * NS, :], wx[:, q, :], u[dpar][:, q, :],
                                                      start=(q == 0), stop=(q == G - 1))
                        if kind == "y":
                            wait(pe, ud_done, d * G + g + 1)
                            for t in range(TT1):
                                mm = nc.tensor.transpose(ps[:, t * P:(t + 1) * P], ud[g % 2][:, t * P:(t + 1) * P], ident[:])
                        if kind == "c":
                            wait(pe, s_free[x_bank], d * NU + x_nth)
                            for t in range(TT1):
                                mm = nc.tensor.transpose(ps[:, t * P:t * P + R + 2 * NS], xdbl[:, t * P:(t + 1) * P],
                                                         ident[0:R + 2 * NS, 0:R + 2 * NS])
                        if kind == "d":
                            wait(pe, s_free[x_bank], d * NU + x_nth)
                            mm = nc.tensor.matmul(ps[:], wdt[:, g * P:(g + 1) * P], xdbl[0:R, :], start=True, stop=True)
                        mm.then_inc(s_full[v % 2], 1)

                x_bank, x_nth = unit_at(0, "x", 0)

                def prologue():
                    pe.wait_ge(const_loaded, 16 * 7)

                def step(i, par, j, f_on, u_on, s_on):
                    k = (i + 1) * TT1 + j
                    if s_on:
                        s_work(i - 1, 1 - par, j, 0)
                    if f_on:
                        turn(0, k)
                    if s_on:
                        s_work(i - 1, 1 - par, j, 1)
                    if f_on:
                        ffn(k)
                    if s_on:
                        s_work(i - 1, 1 - par, j, 2)
                    if u_on:
                        if j == 0:
                            for b in range(2):
                                wait(pe, tr_split[b], (i * TT1 + TT1) * 2)
                        u_product(i, par, 2 * j)
                    if f_on:
                        turn(1, k)
                    if s_on:
                        s_work(i - 1, 1 - par, j, 3)
                    if u_on:
                        u_product(i, par, 2 * j + 1)

                drive(pe, step, prologue)


def second_pass(nc, sem, ins, tern, consts, ident, split_dram, dram, out):
    with ExitStack() as ctx:
        def sb(name, shape, dt=F32):
            return ctx.enter_context(nc.sbuf_tensor(name, shape, dt))

        wz = sb("wz", [P, 2, G, D], F16)
        wo = sb("wo", [P, 2, G, D], F16)
        half_bias = sb("half_bias2", [P, D])
        neg_a = sb("neg_a", [P, G, NS])
        carry = sb("carry", [P, NS, G])
        dt = [sb(f"dt_{i}", [P, G, T2]) for i in range(2)]
        dtu = [sb(f"dtu_{i}", [P, G, T2]) for i in range(2)]
        ct = [sb(f"ct_{i}", [P, TT2, NS]) for i in range(2)]
        NB = 2
        bb = [sb(f"bb{i}", [P, NB, T2]) for i in range(2)]
        dbu = [sb(f"dbu{i}", [P, G // 2, T2]) for i in range(4)]
        h = [sb(f"h{i}", [P, G, T2]) for i in range(2)]
        y = [[sb(f"y{i}{t}", [P, D]) for t in range(TT2)] for i in range(2)]
        xz = sb("xz_2", [P, 2, G, T2], F16)
        x1 = [sb(f"x1_2{t}", [P, D]) for t in range(TT2)]
        q = [sb(f"q{i}", [P, HALF]) for i in range(2 * TT2)]
        tokt = sb("tokt", [P, 2, G, P], F16)
        xn = sb("xn_2", [P, D])
        o = [sb(f"o{i}", [P, HALF]) for i in range(2)]
        small = sb("small2", [P, 48])
        stats, mv, vn, sn = small[:, 0:12], small[:, 12:14], small[:, 14:16], small[:, 16:18]
        gs = [small[:, 20 + 8 * t:28 + 8 * t] for t in range(TT2)]

        def banks(name, n, shape=(P, HALF)):
            return [ctx.enter_context(nc.psum_tensor(f"{name}{i}", list(shape), F32)) for i in range(n)]

        p_da = banks("p_da", 2)
        p_ht = banks("p_ht", TT2, (P, D))
        p_g = banks("p_g", 2)

        const_loaded, w_loaded, a_done, bias_done = (sem(n) for n in ("const_loaded2", "w2_loaded", "a_done", "bias2_done"))
        carry_set = sem("carry_set")
        dt_loaded = [sem(f"dt2_loaded{i}") for i in range(2)]
        y_loaded = [sem(f"y2_loaded{i}") for i in range(2)]
        b_loaded = [sem(f"b2_loaded{i}") for i in range(2)]
        xz_loaded = sem("xz2_loaded")
        x1_loaded = [sem(f"x1_2_loaded{t}") for t in range(TT2)]
        da_done, dbu_done, scan_done, carry_done = (sem(n) for n in ("da_done", "dbu_done", "scan_done", "carry_done"))
        ht_full = [sem(f"ht_full{t}") for t in range(TT2)]
        y_added = [sem(f"y_added{t}") for t in range(TT2)]
        g_full = [sem(f"g_full{i}") for i in range(2)]
        g_free = [sem(f"g_free{i}") for i in range(2)]
        th_done, gate_done = sem("th_done"), sem("gate_done")
        tok_chain, tok_scale, y_scaled, hi_done = (sem(n) for n in ("tok_chain", "tok_scale", "y_scaled", "hi2_done"))
        ln_chain, stats_ready, pow_done, scale_ready, xn_done = (
            sem(n) for n in ("ln2_chain", "stats2_ready", "pow2_done", "scale2_ready", "xn2_done"))
        xb_done, fin_done = sem("xb2_done"), sem("fin_done")
        o_stored = [sem(f"o_stored{i}") for i in range(2)]

        FFN = {0: [("f", 1, 0)], 1: [("f", 1, 1)]}
        OUT = {4: [("t", 0, 0), ("t", 0, 1)], 5: [("o", 0, 0)], 6: [("o", 0, 1)], 7: [("t", 1, 0), ("t", 1, 1)],
               10: [("o", 1, 0)], 11: [("o", 1, 1)], 12: [("n", 0, 0), ("n", 0, 1)], 13: [("f", 0, 0)],
               14: [("f", 0, 1)], 15: [("n", 1, 0), ("n", 1, 1)]}
        ZED = {2: [("z", 0, 0)], 3: [("z", 0, 1)], 8: [("z", 1, 0)], 9: [("z", 1, 1)]}

        def flags(i):
            if isinstance(i, int):
                return 2 <= i, 1 <= i <= C2, i < C2
            return True, True, True

        def sequence(i):
            return [(n, *unit) for n in range(NS) for on, table in zip(flags(i), (FFN, OUT, ZED)) if on
                    for unit in table.get(n, [])]

        def base(i):
            if isinstance(i, int) and i < 2:
                return i * 2
            if isinstance(i, int) and i == C2 + 1:
                return base(C2) + 8
            return (i - 2) * 10 + 11

        def place(i, kind, t, x):
            at = [u[1:] for u in sequence(i)].index((kind, t, x))
            return at % 2, base(i) + at // 2

        def more(i):
            return not (isinstance(i, int) and i >= C2 - 1)

        def drive(eng, body, prologue):
            prologue()
            body(0, 0)
            body(1, 1)
            with eng.Fori(0, (C2 - 4) // 2) as turn:
                body(turn * 2 + 2, 0)
                body(turn * 2 + 3, 1)
            for i in range(C2 - 2, C2 + 2):
                body(i, i % 2)

        with nc.Block() as block:
            @block.sync
            def _(sp):
                def load_scan(c, par):
                    wait_alone(sp, da_done, (c - 1) * NS * 4)
                    wait_alone(sp, dbu_done, (c - 1) * NS * 2)
                    wait_alone(sp, y_added[1], (c - 1) * NS)
                    for name, tile in (("dt", dt), ("dtu", dtu)):
                        sp.dma_start(tile[par][:], dram[name][bass.ds(c, 1)].rearrange("c p g t -> p (c g) t")
                                     ).then_inc(dt_loaded[par], 16)
                    with nc.allow_non_contiguous_dma(reason="64 bytes a token"):
                        sp.dma_start(ct[par][:], dram["ct"][bass.ds(c * T2, T2), :].rearrange("(t p) n -> p t n", p=P)
                                     ).then_inc(dt_loaded[par], 16)

                def load_y(c, par):
                    if not (isinstance(c, int) and c < 2):
                        b, m = place(c - 1, "t", 1, 1)
                        wait_alone(sp, g_full[b], m + 1)
                    for t in range(TT2):
                        sp.dma_start(y[par][t][:], dram["y0"][bass.ds(c * T2 + t * P, P), :]).then_inc(y_loaded[par], 16)

                def load_b(c, n):
                    wait_alone(sp, dbu_done, (c * NS + n - NB) * 2)
                    s = n // NB % 2
                    sp.dma_start(bb[s][:].rearrange("p n t -> p (n t)"),
                                 dram["b"].rearrange("c n t -> c (n t)")[bass.ds(c, 1), n * T2:(n + NB) * T2]
                                 .to_broadcast([P, NB * T2])).then_inc(b_loaded[s], 16)

                def load_xz(c):
                    if not (isinstance(c, int) and c == 0):
                        b, m = place(c - 1, "z", 1, 1)
                        wait_alone(sp, g_full[b], m + 1)
                    for a in range(2):
                        sp.dma_start(xz[:, a].rearrange("p k t -> p (k t)"),
                                     dram["xz"][bass.ds(c, 1), a].rearrange("c p n -> p (c n)")).then_inc(xz_loaded, 16)

                def load_x1(c, t):
                    wait_alone(sp, fin_done, ((c - 1) * TT2 + t + 1) * 2)
                    sp.dma_start(x1[t][:], dram["x1"][bass.ds(c * T2 + t * P, P), :]).then_inc(x1_loaded[t], 16)

                def prologue():
                    with nc.allow_non_contiguous_dma(reason="constants"):
                        sp.dma_start(neg_a[:], ins["A_log"].rearrange("(g p) n -> p g n", p=P)).then_inc(const_loaded, 16)
                    sp.dma_start(half_bias[:], ins["bias"].partition_broadcast(P)).then_inc(const_loaded, 16)
                    load_scan(0, 0)
                    load_b(0, 0)
                    load_y(0, 0)
                    load_xz(0)
                    for dst, src in ((wz, split_dram[0]), (wo, split_dram[1])):
                        sp.dma_start(dst[:].rearrange("p a k m -> p (a k m)"), src).then_inc(w_loaded, 16)
                    load_scan(1, 1)

                def store(c, t, x):
                    wait_alone(sp, fin_done, (c * TT2 + t) * 2 + x + 1)
                    sp.dma_start(out[bass.ds(c * T2 + t * P, P), x * HALF:(x + 1) * HALF], o[x][:]).then_inc(o_stored[x], 16)

                def body(i, par):
                    e_on, c_on, z_on = flags(i)
                    for n in range(NS):
                        if z_on and n % NB == 0:
                            if n + NB < NS:
                                load_b(i, n + NB)
                            elif more(i):
                                load_b(i + 1, 0)
                        if z_on and more(i) and n == 2 and not (isinstance(i, int) and i == 0):
                            load_scan(i + 1, 1 - par)
                        if e_on and n in (1, 4, 5):
                            store(i - 2, *{1: (0, 1), 4: (1, 0), 5: (1, 1)}[n])
                        if c_on and n in (1, 5):
                            load_x1(i - 1, n // 5)
                        if c_on and n == 15:
                            store(i - 1, 0, 0)
                        if z_on and more(i) and n == 9:
                            load_y(i + 1, 1 - par)
                        if z_on and more(i) and n == 11:
                            load_xz(i + 1)

                drive(sp, body, prologue)
                for x in range(2):
                    sp.wait_ge(o_stored[x], 16 * C2 * TT2)

            @block.gpsimd
            def _(pool):
                def prologue():
                    nc.gpsimd.memset(carry[:], 0.0).then_inc(carry_set, 1)

                def times_b(i, par, n):
                    if n == 0:
                        wait(pool, dt_loaded[par], (i - par) * 24 + 48)
                    if n % NB == 0:
                        wait(pool, b_loaded[n // NB % 2], (i * (NS // NB // 2) + n // NB // 2 + 1) * 16)
                    for f in range(2):
                        wait(pool, scan_done, i * (NS * 4) + (n - 2) * 4 + 2 * f + 2)
                        nc.gpsimd.tensor_tensor(dbu[n % 2 * 2 + f][:], dtu[par][:, 4 * f:4 * f + 4, :],
                                                bb[n // NB % 2][:, n % NB:n % NB + 1, :].to_broadcast([P, G // 2, T2]),
                                                ALU.mult).then_inc(dbu_done, 1)

                def keep(c, n):
                    wait(pool, scan_done, c * (NS * 4) + n * 4 + 4)
                    nc.gpsimd.tensor_tensor(carry[:, n, :], h[n % 2][:, :, T2 - 1], consts["one"].to_broadcast([P, G]),
                                            ALU.mult).then_inc(carry_done, 1)

                def gate(c, cpar, t):
                    wait(pool, y_added[t], c * NS + NS)
                    for x in range(2):
                        b, m = place(c, "z", t, x)
                        wait(pool, g_free[b], m + 1)
                        half = y[cpar][t][:, x * HALF:(x + 1) * HALF]
                        nc.gpsimd.tensor_tensor(half, q[2 * t + x][:], half, ALU.mult).then_inc(gate_done, 1)

                def add_bias(c, t):
                    wait(pool, xn_done, c * TT2 + t + 1)
                    nc.gpsimd.tensor_tensor(x1[t][:], x1[t][:], half_bias[:], ALU.add).then_inc(xb_done, 1)

                def finish(i, c, t, x):
                    b, m = place(i, "f", t, x)
                    wait(pool, g_free[b], m + 1)
                    wait(pool, xb_done, c * TT2 + t + 1)
                    nc.gpsimd.tensor_tensor(o[x][:], o[x][:], x1[t][:, x * HALF:(x + 1) * HALF], ALU.add).then_inc(fin_done, 1)

                def body(i, par):
                    e_on, c_on, z_on = flags(i)
                    for n in range(NS):
                        if z_on:
                            if n >= 2:
                                keep(i, n - 2)
                            elif c_on:
                                keep(i - 1, NS - 2 + n)
                            times_b(i, par, n)
                        if e_on:
                            if n == 0:
                                add_bias(i - 2, 1)
                            if n == 1:
                                finish(i - 1, i - 2, 0, 1)
                            if n in (4, 5):
                                finish(i, i - 2, 1, n - 4)
                        if c_on:
                            if n in (2, 3):
                                gate(i - 1, 1 - par, n - 2)
                            if n in (9, 14):
                                row_scale(pool, nc, vn, consts["minus_half"], sn, stats_ready, pow_done, scale_ready,
                                          xn_done, (i - 1) * TT2 + n // 14)
                            if n == 11:
                                if isinstance(i, int) and i == 1:
                                    pool.wait_ge(bias_done, 1)
                                add_bias(i - 1, 0)
                            if n == 15:
                                finish(i, i - 1, 0, 0)

                drive(pool, body, prologue)

            @block.scalar
            def _(act):
                def prologue():
                    act.wait_ge(const_loaded, 32)
                    nc.scalar.activation(neg_a[:], neg_a[:], ACT.Exp).then_inc(a_done, 1)
                    act.wait_ge(a_done, 1)
                    nc.scalar.mul(neg_a[:], neg_a[:], -1.0).then_inc(a_done, 1)
                    nc.scalar.mul(half_bias[:], half_bias[:], 0.5).then_inc(bias_done, 1)
                    act.wait_ge(a_done, 2)

                def decays(i, par, n, pairs):
                    if n == 0 and pairs[0] == 0:
                        wait(act, dt_loaded[par], (i - par) * 24 + 48)
                    for p in pairs:
                        wait(act, scan_done, i * (NS * 4) + n * 4 + p - 1)
                        for k in range(2):
                            g = 2 * p + k
                            ins_ = nc.scalar.activation(p_da[p % 2][:, k * T2:(k + 1) * T2], dt[par][:, g, :], ACT.Exp,
                                                        scale=neg_a[:, g, n:n + 1])
                        ins_.then_inc(da_done, 1)

                def tanh(i, t, x):
                    b, m = place(i, "z", t, x)
                    wait(act, g_full[b], m + 1)
                    wait(act, gate_done, (i - 1) * 4 + 2 * t + 2)
                    nc.scalar.activation(q[2 * t + x][:], p_g[b][:], ACT.Tanh, scale=consts["half_z"]).then_inc(th_done, 1)

                def high(i, kind, t):
                    for x in range(2):
                        b, m = place(i, kind, t, x)
                        wait(act, g_full[b], m + 1)
                        nc.scalar.activation(tokt[:, 0, 4 * x:4 * x + 4, :], p_g[b][:].rearrange("p (g t) -> p g t", g=4),
                                             ACT.Copy).then_inc(hi_done, 1)

                def scale_y(c, cpar, t):
                    wait(act, tok_scale, c * TT2 + t + 1)
                    nc.scalar.activation(y[cpar][t][:], y[cpar][t][:], ACT.Copy, scale=gs[t][:, 3:4]).then_inc(y_scaled, 1)

                def ffn_out(i, c, t, x):
                    b, m = place(i, "f", t, x)
                    wait(act, g_full[b], m + 1)
                    wait(act, o_stored[x], (c * TT2 + t) * 16)
                    nc.scalar.activation(o[x][:], p_g[b][:], ACT.Copy, scale=consts["ffn_scale"]).then_inc(g_free[b], 1)

                def normalise(i, c, t):
                    wait(act, scale_ready, c * TT2 + t + 1)
                    if not (isinstance(i, int) and i == 1 and t == 0):
                        b, m = place(i if t else i - 1, "n", 1 - t, 1)
                        wait(act, g_full[b], m + 1)
                    nc.scalar.activation(xn[:], x1[t][:], ACT.Identity, bias=sn[:, 1:2], scale=sn[:, 0:1]).then_inc(xn_done, 1)

                def body(i, par):
                    e_on, c_on, z_on = flags(i)
                    c = i - 1
                    for n in range(NS):
                        if z_on:
                            decays(i, par, n, (0, 1))
                        if e_on and n in (1, 2):
                            ffn_out(i, i - 2, 1, n - 1)
                        if c_on and n in (14, 15):
                            ffn_out(i, c, 0, n - 14)
                        if z_on and n in (3, 4, 9, 10):
                            tanh(i, n // 9, n - 3 if n < 9 else n - 9)
                        if z_on:
                            decays(i, par, n, (2, 3))
                        if c_on:
                            if n in (3, 4):
                                scale_y(c, 1 - par, n - 3)
                            if n in (4, 7):
                                high(i, "t", n // 7)
                            if n == 9:
                                normalise(i, c, 0)
                            if n in (12, 15):
                                high(i, "n", n // 15)
                            if n == 14:
                                normalise(i, c, 1)

                drive(act, body, prologue)

            @block.vector
            def _(dve):
                def prologue():
                    dve.wait_ge(carry_set, 1)

                def scans(i, n, half):
                    for g in range(4 * half, 4 * half + 4):
                        if g % 2 == 0:
                            wait(dve, da_done, i * (NS * 4) + n * 4 + g // 2 + 1)
                        if g % 4 == 0:
                            wait(dve, dbu_done, i * (NS * 2) + n * 2 + g // 4 + 1)
                        if g == 0:
                            wait(dve, carry_done, i * NS + n - 1)
                        ins_ = nc.vector.tensor_tensor_scan(h[n % 2][:, g, :], p_da[g // 2 % 2][:, (g % 2) * T2:(g % 2 + 1) * T2],
                                                            dbu[n % 2 * 2 + g // 4][:, g % 4, :], carry[:, n, g:g + 1], ALU.mult, ALU.add)
                        if g % 2:
                            ins_.then_inc(scan_done, 1)

                def add_state(c, par, n):
                    for t in range(TT2):
                        if n == 0:
                            wait(dve, y_loaded[par], (c - par) * 16 + 32)
                        else:
                            wait(dve, y_added[t], c * NS + n)
                        wait(dve, ht_full[t], c * NS + n + 1)
                        nc.vector.scalar_tensor_tensor(out=y[par][t][:], in0=p_ht[t][:], scalar=ct[par][:, t, n:n + 1],
                                                       in1=y[par][t][:], op0=ALU.mult, op1=ALU.add).then_inc(y_added[t], 1)

                def silu_part(i, t, x):
                    b, m = place(i, "z", t, x)
                    wait(dve, th_done, i * 4 + 2 * t + x + 1)
                    nc.vector.scalar_tensor_tensor(out=q[2 * t + x][:], in0=q[2 * t + x][:], scalar=1.0, in1=p_g[b][:],
                                                   op0=ALU.add, op1=ALU.mult).then_inc(g_free[b], 1)

                def low(i, kind, t):
                    before = {("t", 0): 0, ("t", 1): 2, ("n", 0): 4, ("n", 1): 6}[kind, t]
                    for x in range(2):
                        b, m = place(i, kind, t, x)
                        wait(dve, hi_done, (i - 1) * 8 + before + x + 1)
                        nc.vector.tensor_tensor(tokt[:, 1, 4 * x:4 * x + 4, :], p_g[b][:].rearrange("p (g t) -> p g t", g=4),
                                                tokt[:, 0, 4 * x:4 * x + 4, :], ALU.subtract).then_inc(g_free[b], 1)

                def add_product(i, t, x):
                    b, m = place(i, "o", t, x)
                    wait(dve, g_full[b], m + 1)
                    if x == 0:
                        wait(dve, x1_loaded[t], (i - 1) * 16 + 16)
                        wait(dve, tok_scale, (i - 1) * TT2 + t + 1)
                    half = x1[t][:, x * HALF:(x + 1) * HALF]
                    nc.vector.scalar_tensor_tensor(out=half, in0=p_g[b][:], scalar=gs[t][:, 4:5], in1=half,
                                                   op0=ALU.mult, op1=ALU.add).then_inc(g_free[b], 1)

                def token_scale(c, cpar, t):
                    k = (c * TT2 + t) * 4
                    wait(dve, gate_done, c * 4 + 2 * t + 2)
                    nc.vector.tensor_reduce(gs[t][:, 0:1], y[cpar][t][:], AX_X, ALU.max,
                                            apply_absolute_value=True).then_inc(tok_chain, 1)
                    wait(dve, tok_chain, k + 1)
                    nc.vector.tensor_scalar(gs[t][:, 0:1], gs[t][:, 0:1], TINY, None, ALU.max).then_inc(tok_chain, 1)
                    wait(dve, tok_chain, k + 2)
                    nc.vector.tensor_scalar(gs[t][:, 1:2].bitcast(I32), gs[t][:, 0:1].bitcast(I32), EXPONENT, None,
                                            ALU.bitwise_and).then_inc(tok_chain, 1)
                    wait(dve, tok_chain, k + 3)
                    nc.vector.reciprocal(gs[t][:, 2:3], gs[t][:, 1:2]).then_inc(tok_chain, 1)
                    nc.vector.tensor_scalar(gs[t][:, 4:5], gs[t][:, 1:2], consts["out_scale"], 1.0 / WS, ALU.mult, ALU.mult)
                    wait(dve, tok_chain, k + 4)
                    nc.vector.tensor_scalar(gs[t][:, 3:4], gs[t][:, 2:3], WS, None, ALU.mult).then_inc(tok_scale, 1)

                def body(i, par):
                    e_on, c_on, z_on = flags(i)
                    for n in range(NS):
                        if c_on and n in (6, 7, 11, 12):
                            add_product(i, n // 11, (n - 6) if n < 8 else n - 11)
                        if z_on:
                            scans(i, n, 0)
                            if n in (3, 4, 9, 10):
                                silu_part(i, n // 9, n - 3 if n < 9 else n - 9)
                            scans(i, n, 1)
                        if n and z_on:
                            add_state(i, par, n - 1)
                        if n == 0 and c_on:
                            add_state(i - 1, 1 - par, NS - 1)
                        if c_on:
                            if n in (2, 3):
                                token_scale(i - 1, 1 - par, n - 2)
                            if n in (4, 7):
                                low(i, "t", n // 7)
                            if n in (7, 12):
                                t = n // 12
                                for x in range(2):
                                    b, m = place(i, "o", t, x)
                                    wait(dve, g_free[b], m + 1)
                                row_stats(dve, nc, x1[t], stats, mv, vn, small[:, 40:41], ln_chain, stats_ready,
                                          scale_ready, (i - 1) * TT2 + t)
                            if n in (12, 15):
                                low(i, "n", n // 15)

                drive(dve, body, prologue)

            @block.tensor
            def _(pe):
                def turn_state(c, n):
                    wait(pe, scan_done, c * (NS * 4) + n * 4 + 4)
                    for t in range(TT2):
                        wait(pe, y_added[t], c * NS + n)
                        for g in range(G):
                            mm = nc.tensor.transpose(p_ht[t][:, g * P:(g + 1) * P], h[n % 2][:, g, t * P:(t + 1) * P], ident[:])
                        mm.then_inc(ht_full[t], 1)

                def unit(i, par, kind, t, x):
                    b, m = place(i, kind, t, x)
                    wait(pe, g_free[b], m)
                    cols = slice(x * HALF, (x + 1) * HALF)
                    n = 0
                    if kind in "tn":
                        if kind == "t":
                            src = y[1 - par][t]
                            wait(pe, y_scaled, (i - 1) * TT2 + t + 1)
                        else:
                            src = xn
                            wait(pe, xn_done, (i - 1) * TT2 + t + 1)
                        for k in range(4):
                            g = 4 * x + k
                            mm = nc.tensor.transpose(p_g[b][:, k * P:(k + 1) * P], src[:, g * P:(g + 1) * P], ident[:])
                    if kind == "f":
                        for a in range(2):
                            wait_evac(i - t, "n", t, a)
                        for g in range(G):
                            for a in range(2):
                                mm = nc.tensor.matmul(p_g[b][:], tokt[:, a, g, :], tern[:, g, cols],
                                                      start=(n == 0), stop=(n == 2 * G - 1))
                                n += 1
                    if kind == "o":
                        for a in range(2):
                            wait_evac(i, "t", t, a)
                        for g in range(G):
                            for ta, wa in ((0, 0), (0, 1), (1, 0)):
                                mm = nc.tensor.matmul(p_g[b][:], tokt[:, ta, g, :], wo[:, wa, g, cols],
                                                      start=(n == 0), stop=(n == 3 * G - 1))
                                n += 1
                    if kind == "z":
                        wait(pe, xz_loaded, i * 32 + 32)
                        if isinstance(i, int) and i == 0:
                            pe.wait_ge(w_loaded, 32)
                        for g in range(G):
                            for xa, wa in ((0, 0), (0, 1), (1, 0)):
                                mm = nc.tensor.matmul(p_g[b][:], xz[:, xa, g, t * P:(t + 1) * P], wz[:, wa, g, cols],
                                                      start=(n == 0), stop=(n == 3 * G - 1))
                                n += 1
                    mm.then_inc(g_full[b], 1)

                def wait_evac(i, kind, t, a):
                    b, m = place(i, kind, t, a)
                    wait(pe, g_free[b], m + 1)

                def body(i, par):
                    e_on, c_on, z_on = flags(i)
                    seq = sequence(i)
                    for n in range(NS):
                        if n and z_on:
                            turn_state(i, n - 1)
                        if n == 0 and c_on:
                            turn_state(i - 1, NS - 1)
                        for slot, kind, t, x in seq:
                            if slot == n:
                                unit(i, par, kind, t, x)

                drive(pe, body, lambda: None)


def macaron_block(nc, ins, out):
    dram = {
        "x1": nc.dram_tensor("x1_scratch", [L, D], F32, kind="Internal").ap(),
        "xz": nc.dram_tensor("xz_scratch", [C2, 2, P, G * T2], F16, kind="Internal").ap(),
        "y0": nc.dram_tensor("y0_scratch", [L, D], F32, kind="Internal").ap(),
        "dt": nc.dram_tensor("dt_scratch", [C2, P, G, T2], F32, kind="Internal").ap(),
        "dtu": nc.dram_tensor("dtu_scratch", [C2, P, G, T2], F32, kind="Internal").ap(),
        "b": nc.dram_tensor("b_scratch", [C2, NS, T2], F32, kind="Internal").ap(),
        "ct": nc.dram_tensor("ct_scratch", [L, NS], F32, kind="Internal").ap(),
    }
    split = [nc.dram_tensor(f"{n}_split", [P, 2 * G * D], F16, kind="Internal").ap() for n in ("wz", "wo")]
    with ExitStack() as ctx:
        def sem(name):
            return ctx.enter_context(nc.semaphore(name))

        tern = ctx.enter_context(nc.sbuf_tensor("tern", [P, G, D], F16))
        ident = ctx.enter_context(nc.sbuf_tensor("ident", [P, P], F32))
        c = ctx.enter_context(nc.sbuf_tensor("consts", [P, 8], F32))
        consts = {n: c[:, k:k + 1] for k, n in enumerate(("ffn_scale", "u_scale", "half_z", "out_scale", "minus_half", "one"))}
        with nc.sbuf_tensor("wu", [P, 2, G, D], F16) as wu_t:
            wu = [wu_t[:, 0], wu_t[:, 1]]
            prepare_weights(nc, sem, ins["W_ffn"], ins["W_in"], ins["W_out"], tern, wu, consts, ident, split)
            first_pass(nc, sem, ins, tern, wu, consts, ident, dram)
        second_pass(nc, sem, ins, tern, consts, ident, split, dram, out)


def kernel(L0_attn_x, L0_attn_W_in, L0_attn_conv_w, L0_attn_conv_b, L0_attn_W_xproj, L0_attn_W_dt, L0_attn_b_dt,
           L0_attn_A_log, L0_attn_Dskip, L0_attn_W_out, L0_ffn_weight, L0_ffn_bias):
    import numpy as np
    import concourse.bacc as bacc
    from concourse.bass_utils import run_bass_kernel_spmd

    arrays = {"x": L0_attn_x.reshape(L, D), "W_ffn": L0_ffn_weight.T, "bias": L0_ffn_bias, "W_in": L0_attn_W_in.T,
              "W_out": L0_attn_W_out.T, "W_xproj": L0_attn_W_xproj.T, "W_dt": L0_attn_W_dt.T,
              "conv_w": L0_attn_conv_w, "conv_b": L0_attn_conv_b, "b_dt": L0_attn_b_dt, "A_log": L0_attn_A_log,
              "Dskip": L0_attn_Dskip}
    arrays = {n: np.ascontiguousarray(a) for n, a in arrays.items()}
    nc = bacc.Bacc("TRN2", target_bir_lowering=False, num_devices=1)
    ins = {n: nc.dram_tensor("in_" + n, list(a.shape), mybir.dt.from_np(a.dtype), kind="ExternalInput").ap()
           for n, a in arrays.items()}
    out = nc.dram_tensor("out", [L, D], F32, kind="ExternalOutput").ap()
    macaron_block(nc, ins, out)
    r = run_bass_kernel_spmd(nc, [{"in_" + n: a for n, a in arrays.items()}], core_ids=[0])
    return r.results[0]["out"].reshape(1, L, D)
```

```python
from contextlib import ExitStack

import concourse.bass as bass
from concourse import mybir

ALU = mybir.AluOpType
ACT = mybir.ActivationFunctionType
AX_X = mybir.AxisListType.X
F32 = mybir.dt.float32
F16 = mybir.dt.float16
I32 = mybir.dt.int32
RADD = bass.bass_isa.ReduceOp.add
RABSMAX = bass.bass_isa.ReduceOp.absmax

P = 128
L, D = 4096, 1024
NS = 16
R = 64
G = D // P
HALF = 512
T1 = 512
C1 = L // T1
TT1 = T1 // P
T2 = 256
C2 = L // T2
TT2 = T2 // P
XS = 512.0
WS = 8192.0
EXPONENT = 0x7F800000
TINY = 1e-30
EPS = 1e-5
EPS_FFN = 1e-10
ROUND = 1.5 * 2.0 ** 23


def wait(eng, sem, count):
    if isinstance(count, int) and count <= 0:
        return
    eng.wait_ge(sem, count)


def wait_alone(eng, sem, count):
    if not isinstance(count, int):
        eng.wait_ge(sem, 1)
    wait(eng, sem, count)


def row_stats(dve, nc, row, stats, mv, vn, idle, chain, ready, read, k):
    for h in range(2):
        ins = nc.vector.bn_stats(stats[:, 6 * h:6 * h + 6], row[:, h * HALF:(h + 1) * HALF])
    ins.then_inc(chain, 1)
    wait(dve, chain, k * 2 + 1)
    nc.vector.memset(idle, 0.0)
    nc.vector.bn_aggr(mv[:, 0:2], stats[:, 0:12]).then_inc(chain, 1)
    wait(dve, chain, k * 2 + 2)
    wait(dve, read, k)
    nc.vector.tensor_scalar(vn[:, 0:1], mv[:, 1:2], EPS, 1.0 / (XS * XS), ALU.add, ALU.mult)
    nc.vector.tensor_scalar(vn[:, 1:2], mv[:, 0:1], -1.0, None, ALU.mult).then_inc(ready, 1)


def row_scale(pool, nc, vn, minus_half, sn, ready, chain, done, used, k):
    wait(pool, ready, k + 1)
    wait(pool, used, k)
    nc.gpsimd.tensor_tensor(sn[:, 0:1], vn[:, 0:1], minus_half, ALU.pow).then_inc(chain, 1)
    wait(pool, chain, k + 1)
    nc.gpsimd.tensor_tensor(sn[:, 1:2], vn[:, 1:2], sn[:, 0:1], ALU.mult).then_inc(done, 1)


def first_pass(nc, sem, ins, tern, wu_all, consts, ident, split_dram, dram):
    with ExitStack() as ctx:
        def sb(name, shape, dt=F32):
            return ctx.enter_context(nc.sbuf_tensor(name, shape, dt))

        wx = sb("wx", [P, G, R + 2 * NS])
        wdt = sb("wdt", [R, D])
        half_bias = sb("half_bias", [P, D])
        conv_w = sb("conv_w", [P, G, 4])
        conv_b = sb("conv_b", [P, G])
        dt_b = sb("dt_b", [P, G])
        dskip = sb("dskip", [P, G])
        wu = [wu_all[:, 0], wu_all[:, 1]]
        xin = [sb(f"xin{i}", [P, D]) for i in range(2)]
        x1 = [sb(f"x1_{i}", [P, D]) for i in range(2)]
        xn = [sb(f"xn{i}", [P, D]) for i in range(2)]
        xt = sb("xt", [P, 2, G, P], F16)
        xz = [sb(f"xz{i}", [P, 2, 2, G, T2], F16) for i in range(2)]
        up = [sb(f"up{i}", [P, T1 + 3]) for i in range(2)]
        acc = [sb(f"acc{i}", [P, T1]) for i in range(2)]
        halo = sb("halo", [P, G, 3])
        u = [sb(f"u{i}", [P, G, T1]) for i in range(2)]
        ud = [sb(f"ud{i}", [P, T1]) for i in range(2)]
        late = sb("late", [P, 4 * 2 * T1])
        y0 = [late[:, i * 2 * T1:(i + 1) * 2 * T1].rearrange("p (t n) -> p t n", t=TT1) for i in range(2)]
        rel = [late[:, (4 + i) * T1:(5 + i) * T1] for i in range(2)]
        ex = [late[:, (6 + i) * T1:(7 + i) * T1] for i in range(2)]
        w_parts = [late[:, i * 4 * T1:(i + 1) * 4 * T1].bitcast(F16).rearrange("p (a k m) -> p a k m", a=2, k=2)
                   for i in range(2)]
        late2 = sb("late2", [P, 4 * T1])
        lg = [late2[:, i * T1:(i + 1) * T1] for i in range(2)]
        dtu = [late2[:, (2 + i) * T1:(3 + i) * T1] for i in range(2)]
        w_stage = [u[1][:, 0:4, :].rearrange("p g t -> p (g t)"), u[1][:, 4:8, :].rearrange("p g t -> p (g t)"), late2[:]]
        ffn_stage = wu_all.rearrange("p a k m -> p (a k m)").bitcast(F32)
        xdbl = sb("xdbl", [R + 2 * NS, T1])
        ct = sb("ct", [P, TT1, NS])
        res = sb("res", [P, T1])
        dt = [sb(f"dt{i}", [P, T1]) for i in range(2)]
        small = sb("small1", [P, 64])
        part = sb("part", [P, 4, 4])
        whole = sb("whole", [P, 4, 2])
        tmp = sb("tmp", [P, 4, 4])
        stats = [small[:, 0:12], small[:, 12:24]]
        mv = [small[:, 24:26], small[:, 26:28]]
        vn = [small[:, 28:30], small[:, 30:32]]
        sn = [small[:, 32:34], small[:, 34:36]]
        minus_half = consts["minus_half"]

        def bank(name, shape=(P, HALF)):
            return ctx.enter_context(nc.psum_tensor(name, list(shape), F32))

        p_tr = [bank(f"p_tr{i}") for i in range(2)]
        p_ffn = [bank(f"p_ffn{i}") for i in range(2)]
        p_u = [bank(f"p_u{i}") for i in range(2)]
        p_s = [bank(f"p_s{i}") for i in range(2)]

        const_loaded, const_done = sem("const_loaded1"), sem("const_done1")
        ident_step, ffn_loaded = sem("ident_step"), [sem(f"w_ffn_loaded{i}") for i in range(2)]
        w_small, part_done, whole_done = sem("w_small"), sem("w_part_done"), sem("w_whole_done")
        tern_step, tern_done, factor_done = sem("tern_step"), sem("tern_done"), sem("w_factor_done")
        w_loaded = [sem(f"w_loaded{i}") for i in range(3)]
        w_hi_done, w_item_done = sem("w_hi_done"), sem("w_item_done")
        parts_stored = [sem(f"w_parts_stored{i}") for i in range(2)]
        x_loaded = [sem(f"x_loaded{i}") for i in range(2)]
        xb_done, x1_done = sem("xb_done"), sem("x1_done")
        x1_stored = [sem(f"x1_stored{i}") for i in range(2)]
        ln_chain = [sem(f"ln{i}_chain") for i in range(2)]
        stats_ready = [sem(f"stats{i}_ready") for i in range(2)]
        pow_done = [sem(f"pow{i}_done") for i in range(2)]
        scale_ready = [sem(f"scale{i}_ready") for i in range(2)]
        xn_done = [sem(f"xn{i}_done") for i in range(2)]
        tr_full = [sem(f"tr_full{i}") for i in range(2)]
        hi_done = [sem(f"hi_done{i}") for i in range(2)]
        tr_split = [sem(f"tr_split{i}") for i in range(2)]
        ffn_full = sem("ffn_full")
        xz_stored = [sem(f"xz_stored{i}") for i in range(2)]
        u_full, up_done, conv_chain, conv_done = sem("u_full"), sem("up_done"), sem("conv_chain"), sem("conv_done")
        silu_done = sem("silu_done")
        s_full = [sem(f"s_full{i}") for i in range(2)]
        s_free = [sem(f"s_free{i}") for i in range(2)]
        ud_done, y0_stored = sem("ud_done"), [sem(f"y0_stored{i}") for i in range(2)]
        b_stored, ct_stored = sem("b_stored"), sem("ct_stored")
        abs_done, exp_done, ln_done = sem("abs_done"), sem("exp_done"), sem("ln_done")
        sp_chain, dt_done, dtu_done = sem("softplus_chain"), sem("dt_done"), sem("dtu_done")
        dt_stored = [sem(f"dt_stored{i}") for i in range(2)]

        units = [("y", 0), ("y", 1), ("x", 0), ("c", 0), ("d", 0), ("y", 2), ("d", 1), ("d", 2), ("y", 3), ("d", 3),
                 ("y", 4), ("d", 4), ("y", 5), ("d", 5), ("d", 6), ("y", 6), ("d", 7), ("y", 7)]
        per_phase = [(1, 1, 1, 1), (1, 1, 1, 2), (1, 1, 1, 1), (1, 2, 1, 1)]
        NU = len(units) // 2

        def last(k):
            return isinstance(k, int) and k + 1 >= L // P

        def s_units(j, phase, kinds="xycd"):
            before = sum(per_phase[j][:phase]) + sum(sum(n) for n in per_phase[:j])
            return [(v, *units[v]) for v in range(before, before + per_phase[j][phase]) if units[v][0] in kinds]

        def s_units_before(j, phase):
            if phase:
                return s_units(j, phase - 1, "d")
            return s_units(j - 1, 3, "d") if j else []

        def unit_at(d, kind, g):
            v = units.index((kind, g))
            return v % 2, d * NU + v // 2 + 1

        def had_u(i, j):
            before = i if j else i - 1
            return not isinstance(i, int) or 0 <= before < C1

        ITEMS, PER_STEP = 24, 3

        def w_items(i, j):
            if not isinstance(i, int) or i > 0:
                return []
            first = ((i + 1) * TT1 + j) * PER_STEP
            return [(t, t // 8, t % 4, t % 8 >= 4) for t in range(first, first + PER_STEP)]

        def drive(eng, step, prologue=None):
            if prologue:
                prologue()
            for j in range(TT1):
                step(-1, 1, j, True, False, False)
            for j in range(TT1):
                step(0, 0, j, True, True, False)
            for j in range(TT1):
                step(1, 1, j, True, True, True)
            with eng.Fori(0, (C1 - 4) // 2) as turn:
                for o in range(2):
                    for j in range(TT1):
                        step(turn * 2 + 2 + o, o, j, True, True, True)
            for j in range(TT1):
                step(C1 - 2, C1 % 2, j, True, True, True)
            for j in range(TT1):
                step(C1 - 1, (C1 - 1) % 2, j, False, True, True)
            for j in range(TT1):
                step(C1, C1 % 2, j, False, False, True)

        with nc.Block() as block:
            @block.sync
            def _(sp):
                loads = [(wx[:], ins["W_xproj"].rearrange("(g p) m -> p g m", p=P)), (wdt[:], ins["W_dt"]),
                         (half_bias[:], ins["bias"].partition_broadcast(P)),
                         (conv_w[:], ins["conv_w"].rearrange("(g p) k -> p g k", p=P)),
                         (conv_b[:], ins["conv_b"].rearrange("(g p) -> p g", p=P)),
                         (dt_b[:], ins["b_dt"].rearrange("(g p) -> p g", p=P)),
                         (dskip[:], ins["Dskip"].rearrange("(g p) -> p g", p=P))]

                def load_x(k, b, row):
                    wait_alone(sp, xn_done[0], k - 1)
                    wait_alone(sp, xb_done, k - 1)
                    sp.dma_start(xin[b][:], ins["x"][bass.ds(row, P), :]).then_inc(x_loaded[b], 16)

                sources = [ins["W_in"].rearrange("(k p) m -> p k m", p=P)[:, :, 0:D],
                           ins["W_in"].rearrange("(k p) m -> p k m", p=P)[:, :, D:2 * D],
                           ins["W_out"].rearrange("(k p) m -> p k m", p=P)]

                def load_w(t):
                    if t < ITEMS:
                        wait(sp, w_item_done, t - 2)
                        sp.dma_start(w_stage[t % 3].rearrange("p (k m) -> p k m", k=2),
                                     sources[t // 8][:, 2 * (t % 4):2 * (t % 4) + 2, :]).then_inc(w_loaded[t % 3], 16)

                def store_w(t, m, q):
                    wait(sp, w_item_done, t + 1)
                    sp.dma_start(split_dram[m - 1].rearrange("p (a k m) -> p a k m", a=2, k=G)[:, :, 2 * q:2 * q + 2, :],
                                 w_parts[t % 2]).then_inc(parts_stored[t % 2], 16)

                load_x(0, 0, 0)
                for i in range(2):
                    sp.dma_start(ffn_stage[:, i * 4 * D:(i + 1) * 4 * D].rearrange("p (k m) -> p k m", k=4),
                                 ins["W_ffn"].rearrange("(k p) m -> p k m", p=P)[:, 4 * i:4 * i + 4, :]
                                 ).then_inc(ffn_loaded[i], 16)
                with nc.allow_non_contiguous_dma(reason="small constants"):
                    for dst, src in loads:
                        sp.dma_start(dst, src).then_inc(const_loaded, 16)
                load_x(1, 1, P)
                for t in range(PER_STEP):
                    load_w(t)

                def s_stores(d, j, phase):
                    for v, kind, g in s_units(j, phase, "xcy") + s_units_before(j, phase):
                        if kind == "x":
                            wait_alone(sp, s_free[v % 2], d * NU + v // 2 + 1)
                            sp.dma_start(dram["b"][bass.ds(d * 2, 2)].rearrange("h n t -> n h t"),
                                         xdbl[R:R + NS, :].rearrange("n (h t) -> n h t", h=2)).then_inc(b_stored, 16)
                        if kind == "c":
                            wait_alone(sp, s_free[v % 2], d * NU + v // 2 + 1)
                            with nc.allow_non_contiguous_dma(reason="64 bytes a token"):
                                sp.dma_start(dram["ct"][bass.ds(d * T1, T1), :].rearrange("(t p) n -> p t n", p=P),
                                             ct[:]).then_inc(ct_stored, 16)
                        if kind == "y" and g % 2:
                            wait_alone(sp, s_free[v % 2], d * NU + v // 2 + 1)
                            sp.dma_start(dram["y0"][bass.ds(d * T1, T1), (g - 1) * P:(g + 1) * P].rearrange(
                                "(t p) n -> p t n", p=P), y0[g // 2 % 2]).then_inc(y0_stored[g // 2 % 2], 16)
                        if kind == "d":
                            wait_alone(sp, dt_done, d * G + g + 1)
                            wait_alone(sp, dtu_done, d * G + g + 1)
                            for name, tile in (("dt", dt), ("dtu", dtu)):
                                sp.dma_start(dram[name][bass.ds(d * 2, 2), :, g].rearrange("h p t -> p h t"),
                                             tile[g % 2][:].rearrange("p (h t) -> p h t", h=2)
                                             ).then_inc(dt_stored[g % 2], 16)

                def step(i, par, j, f_on, u_on, s_on):
                    f, k = i + 1, (i + 1) * TT1 + j
                    if s_on:
                        s_stores(i - 1, j, 0)
                        s_stores(i - 1, j, 1)
                    for t, m, q, split in w_items(i, j):
                        if split and m:
                            store_w(t, m, q)
                        load_w(t + PER_STEP)
                    if f_on:
                        wait_alone(sp, x1_done, k * 2 + 2)
                        sp.dma_start(dram["x1"][bass.ds(k * P, P), :], x1[j % 2][:]).then_inc(x1_stored[j % 2], 16)
                        if not last(k + 1):
                            load_x(k + 2, j % 2, k * P + 2 * P)
                    if s_on:
                        s_stores(i - 1, j, 2)
                        s_stores(i - 1, j, 3)
                    if f_on and j == TT1 - 1:
                        for b in range(2):
                            wait_alone(sp, tr_split[b], k * 2 + 2)
                        for a in range(2):
                            sp.dma_start(dram["xz"][bass.ds(f * 2, 2), a].rearrange("h p n -> p h n"),
                                         xz[1 - par][:, a].rearrange("p h k t -> p h (k t)")
                                         ).then_inc(xz_stored[1 - par], 16)

                drive(sp, step)
                for b in range(2):
                    sp.wait_ge(x1_stored[b], 16 * (L // P) // 2)
                    sp.wait_ge(xz_stored[b], 32 * C1 // 2)
                    sp.wait_ge(y0_stored[b], 16 * C1 * 2)
                    sp.wait_ge(dt_stored[b], 32 * C1 * G // 2)
                    sp.wait_ge(parts_stored[b], 16 * 4)
                sp.wait_ge(b_stored, 16 * C1)
                sp.wait_ge(ct_stored, 16 * C1)

            @block.gpsimd
            def _(pool):
                def prologue():
                    nc.gpsimd.memset(minus_half, -0.5).then_inc(ident_step, 1)
                    nc.gpsimd.memset(ident[:], 0.0).then_inc(ident_step, 1)
                    pool.wait_ge(ident_step, 2)
                    nc.gpsimd.affine_select(out=ident[:], in_=ident[:], compare_op=ALU.not_equal, fill=1.0, base=0,
                                            pattern=[[-1, P]], channel_multiplier=1).then_inc(ident_step, 1)
                    row_scale(pool, nc, vn[0], minus_half, sn[0], stats_ready[0], pow_done[0], scale_ready[0],
                              xn_done[0], 0)
                    over_partitions(3, RADD)

                def over_partitions(m, op):
                    pool.wait_ge(part_done, (m + 1) % 4 + 1)
                    nc.gpsimd.partition_all_reduce(whole[:, m, 1:2], whole[:, m, 0:1], P, op).then_inc(whole_done, 1)

                def s_work(d, dpar, j, phase):
                    for v, kind, g in s_units_before(j, phase):
                        q = d * G + g
                        wait(pool, dt_done, q + 1)
                        wait(pool, dt_stored[g % 2], (d * (G // 2) + g // 2) * 32)
                        nc.gpsimd.tensor_tensor(dtu[g % 2], dt[g % 2][:], u[dpar][:, g, :], ALU.mult).then_inc(dtu_done, 1)

                def step(i, par, j, f_on, u_on, s_on):
                    k = (i + 1) * TT1 + j
                    if f_on:
                        wait(pool, x_loaded[j % 2], ((i + 1) * 2 + j // 2 + 1) * 16)
                        wait(pool, x1_stored[j % 2], ((i + 1) * 2 + j // 2) * 16)
                        wait(pool, xn_done[1], k - 1)
                        if isinstance(k, int) and k == 0:
                            pool.wait_ge(const_done, 1)
                        nc.gpsimd.tensor_tensor(x1[j % 2][:], xin[j % 2][:], half_bias[:], ALU.add).then_inc(xb_done, 1)
                        if not last(k):
                            row_scale(pool, nc, vn[0], minus_half, sn[0], stats_ready[0], pow_done[0],
                                      scale_ready[0], xn_done[0], k + 1)
                    for t, m, q, split in w_items(i, j):
                        if t % 8 == 3:
                            over_partitions(m, RABSMAX)
                    if s_on:
                        s_work(i - 1, 1 - par, j, 0)
                        s_work(i - 1, 1 - par, j, 1)
                    if f_on:
                        row_scale(pool, nc, vn[1], minus_half, sn[1], stats_ready[1], pow_done[1],
                                  scale_ready[1], xn_done[1], k)
                    if s_on:
                        s_work(i - 1, 1 - par, j, 2)
                        s_work(i - 1, 1 - par, j, 3)

                drive(pool, step, prologue)

            @block.scalar
            def _(act):
                def normalise(n, src, k):
                    wait(act, scale_ready[n], k + 1)
                    wait(act, tr_full[1], k * 2 - 1 + n)
                    nc.scalar.activation(xn[n][:], src, ACT.Identity, bias=sn[n][:, 1:2],
                                         scale=sn[n][:, 0:1]).then_inc(xn_done[n], 1)

                def high(n, k, dst, b):
                    wait(act, tr_full[b], k * 2 + n + 1)
                    nc.scalar.activation(dst, p_tr[b][:].rearrange("p (g t) -> p g t", g=4), ACT.Copy).then_inc(hi_done[b], 1)

                def u_work(i, g):
                    q = i * G + g
                    wait(act, u_full, q + 1)
                    wait(act, conv_done, q - 1)
                    nc.scalar.activation(up[g % 2][:, 3:3 + T1], p_u[g % 2][:], ACT.Copy,
                                         scale=consts["u_scale"]).then_inc(up_done, 1)

                def silu(i, par, g):
                    q = i * G + g
                    wait(act, conv_done, q + 1)
                    if g == 0:
                        wait(act, dtu_done, (i - 1) * G)
                        wait(act, ud_done, (i - 1) * G)
                    nc.scalar.activation(u[par][:, g, :], acc[g % 2][:], ACT.Silu).then_inc(silu_done, 1)

                def s_work(d, j, phase):
                    for v, kind, g in s_units(j, phase, "xd"):
                        if kind == "x":
                            wait(act, s_full[v % 2], d * NU + v // 2 + 1)
                            wait(act, b_stored, d * 16)
                            b, m = unit_at(d - 1, "d", G - 1)
                            wait(act, s_full[b], m)
                            nc.scalar.activation(xdbl[:], p_s[v % 2][0:R + 2 * NS, :], ACT.Copy).then_inc(s_free[v % 2], 1)
                        if kind == "d":
                            q = d * G + g
                            wait(act, s_full[v % 2], d * NU + v // 2 + 1)
                            wait(act, dt_done, q - 1)
                            nc.scalar.activation(rel[g % 2], p_s[v % 2][:], ACT.Relu, bias=dt_b[:, g:g + 1])
                            nc.scalar.activation(ex[g % 2], p_s[v % 2][:], ACT.Abs, bias=dt_b[:, g:g + 1]
                                                 ).then_inc(s_free[v % 2], 1)
                            wait(act, s_free[v % 2], d * NU + v // 2 + 1)
                            nc.scalar.activation(ex[g % 2], ex[g % 2], ACT.Exp, scale=-1.0).then_inc(exp_done, 1)
                            wait(act, exp_done, q + 1)
                            nc.scalar.activation(lg[g % 2], ex[g % 2], ACT.Ln, bias=1.0).then_inc(ln_done, 1)

                def prologue():
                    normalise(0, xin[0][:], 0)
                    act.wait_ge(const_loaded, 16 * 7)
                    nc.scalar.mul(half_bias[:], half_bias[:], 0.5).then_inc(const_done, 1)
                    for h in range(2):
                        act.wait_ge(tern_step, 3 + h)
                        nc.scalar.activation(tern[:, 4 * h:4 * h + 4, :].rearrange("p k m -> p (k m)"),
                                             ffn_stage[:, h * 4 * D:(h + 1) * 4 * D], ACT.Copy, bias=-ROUND
                                             ).then_inc(tern_done, 1)

                def w_high(i, j):
                    for t, m, q, split in w_items(i, j):
                        if split:
                            act.wait_ge(factor_done, m + 1)
                            act.wait_ge(w_loaded[t % 3], (t // 3 + 1) * 16)
                            if m:
                                wait(act, parts_stored[t % 2], 16 * (((m - 1) * 4 + q) // 2))
                            hi = w_parts[t % 2][:, 0] if m else wu[0][:, 2 * q:2 * q + 2, :]
                            nc.scalar.activation(hi, w_stage[t % 3].rearrange("p (k m) -> p k m", k=2), ACT.Copy,
                                                 scale=tmp[:, m, 2:3]).then_inc(w_hi_done, 1)

                def step(i, par, j, f_on, u_on, s_on):
                    f = i + 1
                    k = f * TT1 + j
                    before = (i if j else i - 1, (2 * j - 1) % G)
                    if had_u(i, j):
                        u_work(*before)
                    if f_on:
                        wait(act, ffn_full, k * 2)
                        for b in range(2):
                            high(0, k, xt[:, 0, 4 * b:4 * b + 4, :], b)
                    if s_on:
                        s_work(i - 1, j, 0)
                        s_work(i - 1, j, 1)
                    if f_on and not last(k):
                        normalise(0, xin[(j + 1) % 2][:], k + 1)
                    w_high(i, j)
                    if had_u(i, j):
                        silu(before[0], par if j else 1 - par, before[1])
                    if s_on and j == 0:
                        s_work(i - 1, j, 2)
                    if f_on:
                        normalise(1, x1[j % 2][:], k)
                    if u_on:
                        u_work(i, 2 * j)
                    if f_on:
                        if j == 0:
                            wait(act, u_full, (f - 1) * G)
                            wait(act, xz_stored[1 - par], (f - (1 - par)) * 16)
                        for b in range(2):
                            high(1, k, xz[1 - par][:, 0, j // 2, 4 * b:4 * b + 4, (j % 2) * P:(j % 2 + 1) * P], b)
                    if s_on and j:
                        s_work(i - 1, j, 2)
                    if s_on:
                        s_work(i - 1, j, 3)
                    if u_on:
                        silu(i, par, 2 * j)

                drive(act, step, prologue)

            @block.vector
            def _(dve):
                def low(n, k, src_hi, dst, b):
                    wait(dve, hi_done[b], k * 2 + n + 1)
                    nc.vector.tensor_tensor(dst, p_tr[b][:].rearrange("p (g t) -> p g t", g=4), src_hi,
                                            ALU.subtract).then_inc(tr_split[b], 1)

                def conv(i, g):
                    q = i * G + g
                    src, dst = up[g % 2], acc[g % 2]
                    nc.vector.tensor_copy(src[:, 0:3], halo[:, g, :]).then_inc(conv_chain, 1)
                    wait(dve, conv_chain, q * 4 + 1)
                    wait(dve, up_done, q + 1)
                    wait(dve, silu_done, q - 1)
                    nc.vector.tensor_scalar(dst[:], src[:, 0:T1], conv_w[:, g, 0:1], conv_b[:, g:g + 1],
                                            ALU.mult, ALU.add).then_inc(conv_chain, 1)
                    for tap in (1, 2):
                        wait(dve, conv_chain, q * 4 + 1 + tap)
                        nc.vector.scalar_tensor_tensor(out=dst[:], in0=src[:, tap:tap + T1], scalar=conv_w[:, g, tap:tap + 1],
                                                       in1=dst[:], op0=ALU.mult, op1=ALU.add).then_inc(conv_chain, 1)
                    nc.vector.tensor_copy(halo[:, g, :], src[:, T1:T1 + 3])
                    wait(dve, conv_chain, q * 4 + 4)
                    nc.vector.scalar_tensor_tensor(out=dst[:], in0=src[:, 3:3 + T1], scalar=conv_w[:, g, 3:4],
                                                   in1=dst[:], op0=ALU.mult, op1=ALU.add).then_inc(conv_done, 1)

                def s_work(d, dpar, j, phase):
                    for v, kind, g in s_units(j, phase, "cy") + s_units_before(j, phase):
                        q = d * G + g
                        if kind == "c":
                            wait(dve, s_full[v % 2], d * NU + v // 2 + 1)
                            wait(dve, ct_stored, d * 16)
                            nc.vector.tensor_copy(ct[:], p_s[v % 2][:, 0:TT1 * P].rearrange(
                                "p (t n) -> p t n", t=TT1)[:, :, R + NS:R + 2 * NS]).then_inc(s_free[v % 2], 1)
                        if kind == "y":
                            wait(dve, s_full[v % 2], d * NU + v // 2 + 1)
                            wait(dve, y0_stored[g // 2 % 2], (d * 2 + g // 4) * 16)
                            nc.vector.tensor_copy(y0[g // 2 % 2][:, :, (g % 2) * P:(g % 2 + 1) * P],
                                                  p_s[v % 2][:].rearrange("p (t n) -> p t n", t=TT1)).then_inc(s_free[v % 2], 1)
                            if g + 2 < G:
                                times_dskip(d, dpar, g + 2)
                        if kind == "d":
                            wait(dve, dt_done, q)
                            wait(dve, exp_done, q + 1)
                            nc.vector.tensor_scalar(res[:], ex[g % 2], 1.0, -1.0, ALU.add, ALU.add).then_inc(sp_chain, 1)
                            wait(dve, sp_chain, q * 3 + 1)
                            nc.vector.tensor_tensor(res[:], ex[g % 2], res[:], ALU.subtract).then_inc(sp_chain, 1)
                            wait(dve, ln_done, q + 1)
                            wait(dve, sp_chain, q * 3 + 2)
                            nc.vector.tensor_tensor(res[:], lg[g % 2], res[:], ALU.add).then_inc(sp_chain, 1)
                            wait(dve, sp_chain, q * 3 + 3)
                            wait(dve, dtu_done, q - 1)
                            wait(dve, dt_stored[g % 2], (d * (G // 2) + g // 2) * 32)
                            nc.vector.tensor_tensor(dt[g % 2][:], res[:], rel[g % 2], ALU.add).then_inc(dt_done, 1)

                def times_dskip(d, dpar, g):
                    b, m = unit_at(d, "y", g - 2) if g >= 2 else unit_at(d - 1, "y", g + 6)
                    wait(dve, s_full[b], m)
                    wait(dve, silu_done, d * G + g + 1)
                    nc.vector.tensor_scalar(ud[g % 2][:], u[dpar][:, g, :], dskip[:, g:g + 1], None,
                                            ALU.mult).then_inc(ud_done, 1)

                steps = [0]

                def link(ins_):
                    steps[0] += 1
                    ins_.then_inc(w_small, 1)
                    dve.wait_ge(w_small, steps[0])

                def over_quarters(m, n, op):
                    link(nc.vector.tensor_reduce(whole[:, m, 0:1], part[:, m, 0:n], AX_X, op))
                    nc.vector.memset(small[:, 42:43], 0.0).then_inc(part_done, 1)

                def prologue():
                    nc.vector.memset(halo[:], 0.0)
                    dve.wait_ge(x_loaded[0], 16)
                    row_stats(dve, nc, xin[0], stats[0], mv[0], vn[0], small[:, 40:41], ln_chain[0], stats_ready[0], scale_ready[0], 0)
                    for h in range(2):
                        dve.wait_ge(ffn_loaded[h], 16)
                        ins_ = nc.vector.tensor_reduce(part[:, 3, h:h + 1], ffn_stage[:, h * 4 * D:(h + 1) * 4 * D], AX_X,
                                                       ALU.add, apply_absolute_value=True)
                    link(ins_)
                    over_quarters(3, 2, ALU.add)
                    dve.wait_ge(whole_done, 1)
                    link(nc.vector.tensor_scalar(tmp[:, 3, 0:1], whole[:, 3, 1:2], 1.0 / (D * D), None, ALU.mult))
                    link(nc.vector.tensor_scalar(tmp[:, 3, 1:2], tmp[:, 3, 0:1], EPS_FFN, None, ALU.add))
                    link(nc.vector.reciprocal(tmp[:, 3, 2:3], tmp[:, 3, 1:2]))
                    nc.vector.tensor_scalar(consts["ffn_scale"], tmp[:, 3, 0:1], 0.5 / XS, None, ALU.mult)
                    for h in range(2):
                        w = ffn_stage[:, h * 4 * D:(h + 1) * 4 * D]
                        nc.vector.tensor_scalar(w, w, tmp[:, 3, 2:3], -1.0, ALU.mult, ALU.max).then_inc(tern_step, 1)
                    for h in range(2):
                        w = ffn_stage[:, h * 4 * D:(h + 1) * 4 * D]
                        dve.wait_ge(tern_step, 1 + h)
                        nc.vector.tensor_scalar(w, w, 1.0, ROUND, ALU.min, ALU.add).then_inc(tern_step, 1)
                    dve.wait_ge(const_loaded, 16 * 7)

                def factor(m):
                    dve.wait_ge(whole_done, m + 2)
                    link(nc.vector.tensor_scalar(tmp[:, m, 0:1], whole[:, m, 1:2], TINY, None, ALU.max))
                    link(nc.vector.tensor_scalar(tmp[:, m, 1:2].bitcast(I32), tmp[:, m, 0:1].bitcast(I32),
                                                 EXPONENT, None, ALU.bitwise_and))
                    link(nc.vector.reciprocal(tmp[:, m, 3:4], tmp[:, m, 1:2]))
                    if m == 0:
                        link(nc.vector.tensor_scalar(consts["u_scale"], tmp[:, 0, 1:2], 1.0 / (WS * XS), None, ALU.mult))
                    if m == 1:
                        link(nc.vector.tensor_scalar(consts["half_z"], tmp[:, 1, 1:2], 0.5 / (WS * XS), None, ALU.mult))
                    if m == 2:
                        link(nc.vector.tensor_scalar(consts["out_scale"], tmp[:, 2, 1:2], consts["half_z"], 1.0 / WS,
                                                     ALU.mult, ALU.mult))
                    nc.vector.tensor_scalar(tmp[:, m, 2:3], tmp[:, m, 3:4], WS, None, ALU.mult).then_inc(factor_done, 1)
                    dve.wait_ge(factor_done, m + 1)

                def w_work(i, j):
                    for t, m, q, split in w_items(i, j):
                        if not split:
                            dve.wait_ge(w_loaded[t % 3], (t // 3 + 1) * 16)
                            nc.vector.tensor_reduce(part[:, m, q:q + 1], w_stage[t % 3], AX_X, ALU.max,
                                                    apply_absolute_value=True).then_inc(w_item_done, 1)
                            if q == 3:
                                dve.wait_ge(w_item_done, t + 1)
                                over_quarters(m, 4, ALU.max)
                        else:
                            if q == 0:
                                factor(m)
                            hi, lo = ((w_parts[t % 2][:, a] if m else wu[a][:, 2 * q:2 * q + 2, :]) for a in range(2))
                            dve.wait_ge(w_hi_done, m * 4 + q + 1)
                            nc.vector.scalar_tensor_tensor(out=lo, in0=w_stage[t % 3].rearrange("p (k m) -> p k m", k=2),
                                                           scalar=tmp[:, m, 2:3], in1=hi,
                                                           op0=ALU.mult, op1=ALU.subtract).then_inc(w_item_done, 1)

                def step(i, par, j, f_on, u_on, s_on):
                    f, d = i + 1, i - 1
                    k = f * TT1 + j
                    if f_on:
                        for b in range(2):
                            low(0, k, xt[:, 0, 4 * b:4 * b + 4, :], xt[:, 1, 4 * b:4 * b + 4, :], b)
                    if f_on:
                        if not last(k):
                            wait(dve, x_loaded[(j + 1) % 2], (f * 2 + (j + 1) // 2 + 1) * 16)
                            row_stats(dve, nc, xin[(j + 1) % 2], stats[0], mv[0], vn[0], small[:, 40:41], ln_chain[0],
                                      stats_ready[0], scale_ready[0], k + 1)
                    if had_u(i, j):
                        conv(i if j else i - 1, (2 * j - 1) % G)
                    w_work(i, j)
                    if s_on:
                        s_work(d, 1 - par, j, 0)
                        s_work(d, 1 - par, j, 1)
                    if f_on:
                        wait(dve, xb_done, k + 1)
                        for h in range(2):
                            wait(dve, ffn_full, k * 2 + h + 1)
                            nc.vector.scalar_tensor_tensor(out=x1[j % 2][:, h * HALF:(h + 1) * HALF], in0=p_ffn[h][:],
                                                           scalar=consts["ffn_scale"],
                                                           in1=x1[j % 2][:, h * HALF:(h + 1) * HALF],
                                                           op0=ALU.mult, op1=ALU.add).then_inc(x1_done, 1)
                        wait(dve, x1_done, k * 2 + 2)
                        row_stats(dve, nc, x1[j % 2], stats[1], mv[1], vn[1], small[:, 41:42], ln_chain[1], stats_ready[1],
                                  scale_ready[1], k)
                    if s_on:
                        s_work(d, 1 - par, j, 2)
                    if f_on:
                        for b in range(2):
                            hi, lo = (xz[1 - par][:, a, j // 2, 4 * b:4 * b + 4, (j % 2) * P:(j % 2 + 1) * P] for a in range(2))
                            low(1, k, hi, lo, b)
                    if u_on:
                        conv(i, 2 * j)
                    if s_on:
                        s_work(d, 1 - par, j, 3)
                    if u_on and j == TT1 - 1:
                        times_dskip(i, par, 0)
                        times_dskip(i, par, 1)

                drive(dve, step, prologue)

            @block.tensor
            def _(pe):
                def turn(n, k):
                    wait(pe, xn_done[n], k + 1)
                    for b in range(2):
                        wait(pe, tr_split[b], k * 2 + n)
                        for q in range(4):
                            g = 4 * b + q
                            mm = nc.tensor.transpose(p_tr[b][:, q * P:(q + 1) * P], xn[n][:, g * P:(g + 1) * P], ident[:])
                        mm.then_inc(tr_full[b], 1)

                def ffn(k):
                    wait(pe, x1_done, k * 2)
                    for h in range(2):
                        for g in range(G):
                            if h == 0 and g % 4 == 0:
                                if isinstance(k, int) and k == 0:
                                    pe.wait_ge(tern_done, g // 4 + 1)
                                wait(pe, tr_split[g // 4], k * 2 + 1)
                            for a in range(2):
                                mm = nc.tensor.matmul(p_ffn[h][:], xt[:, a, g, :], tern[:, g, h * HALF:(h + 1) * HALF],
                                                      start=(g == 0 and a == 0), stop=(g == G - 1 and a == 1))
                        mm.then_inc(ffn_full, 1)

                def u_product(i, par, g):
                    wait(pe, up_done, i * G + g - 1)
                    n = 0
                    for kk in range(G):
                        for wa, xa in ((0, 0), (0, 1), (1, 0)):
                            mm = nc.tensor.matmul(p_u[g % 2][:].rearrange("p (h t) -> p h t", h=2),
                                                  wu[wa][:, kk, g * P:(g + 1) * P], xz[par][:, xa, :, kk, :],
                                                  start=(n == 0), stop=(n == 3 * G - 1))
                            n += 1
                    mm.then_inc(u_full, 1)

                def s_work(d, dpar, j, phase):
                    for v, kind, g in s_units(j, phase):
                        wait(pe, s_free[v % 2], d * NU + v // 2)
                        ps = p_s[v % 2]
                        if kind == "x":
                            if isinstance(d, int) and d == 0:
                                pe.wait_ge(const_loaded, 16 * 7)
                            wait(pe, silu_done, d * G + G)
                            for q in range(G):
                                mm = nc.tensor.matmul(ps[0:R + 2 * NS, :], wx[:, q, :], u[dpar][:, q, :],
                                                      start=(q == 0), stop=(q == G - 1))
                        if kind == "y":
                            wait(pe, ud_done, d * G + g + 1)
                            for t in range(TT1):
                                mm = nc.tensor.transpose(ps[:, t * P:(t + 1) * P], ud[g % 2][:, t * P:(t + 1) * P], ident[:])
                        if kind == "c":
                            wait(pe, s_free[x_bank], d * NU + x_nth)
                            for t in range(TT1):
                                mm = nc.tensor.transpose(ps[:, t * P:t * P + R + 2 * NS], xdbl[:, t * P:(t + 1) * P],
                                                         ident[0:R + 2 * NS, 0:R + 2 * NS])
                        if kind == "d":
                            wait(pe, s_free[x_bank], d * NU + x_nth)
                            mm = nc.tensor.matmul(ps[:], wdt[:, g * P:(g + 1) * P], xdbl[0:R, :], start=True, stop=True)
                        mm.then_inc(s_full[v % 2], 1)

                x_bank, x_nth = unit_at(0, "x", 0)

                def prologue():
                    pe.wait_ge(ident_step, 3)

                def step(i, par, j, f_on, u_on, s_on):
                    k = (i + 1) * TT1 + j
                    if s_on:
                        s_work(i - 1, 1 - par, j, 0)
                    if f_on:
                        turn(0, k)
                    if s_on:
                        s_work(i - 1, 1 - par, j, 1)
                    if f_on:
                        ffn(k)
                    if s_on:
                        s_work(i - 1, 1 - par, j, 2)
                    if u_on:
                        if j == 0:
                            for b in range(2):
                                wait(pe, tr_split[b], (i * TT1 + TT1) * 2)
                            if isinstance(i, int) and i == 0:
                                pe.wait_ge(w_item_done, 8)
                        u_product(i, par, 2 * j)
                    if f_on:
                        turn(1, k)
                    if s_on:
                        s_work(i - 1, 1 - par, j, 3)
                    if u_on:
                        u_product(i, par, 2 * j + 1)

                drive(pe, step, prologue)


def second_pass(nc, sem, ins, tern, consts, ident, split_dram, dram, out):
    with ExitStack() as ctx:
        def sb(name, shape, dt=F32):
            return ctx.enter_context(nc.sbuf_tensor(name, shape, dt))

        wz = sb("wz", [P, 2, G, D], F16)
        wo = sb("wo", [P, 2, G, D], F16)
        half_bias = sb("half_bias2", [P, D])
        neg_a = sb("neg_a", [P, G, NS])
        carry = sb("carry", [P, NS, G])
        edge_dt = sb("edge_dt", [P, 1, G // 2])
        factor = [sb(f"carry_factor{i}", [P, NS, G]) for i in range(2)]
        dt = [sb(f"dt_{i}", [P, G, T2]) for i in range(2)]
        dtu = [sb(f"dtu_{i}", [P, G, T2]) for i in range(2)]
        ct = [sb(f"ct_{i}", [P, TT2, NS]) for i in range(2)]
        NB = 2
        bb = [sb(f"bb{i}", [P, NB, T2]) for i in range(2)]
        dbu = [sb(f"dbu{i}", [P, G, T2]) for i in range(2)]
        h = [sb(f"h{i}", [P, G, T2]) for i in range(2)]
        y = [[sb(f"y{i}{t}", [P, D]) for t in range(TT2)] for i in range(2)]
        xz = sb("xz_2", [P, 2, G, T2], F16)
        x1 = [sb(f"x1_2{t}", [P, D]) for t in range(TT2)]
        q = [sb(f"q{i}", [P, HALF]) for i in range(2 * TT2)]
        tokt = sb("tokt", [P, 2, G, P], F16)
        xn = sb("xn_2", [P, D])
        o = [sb(f"o{i}", [P, HALF]) for i in range(2)]
        small = sb("small2", [P, 48])
        stats, mv, vn, sn = small[:, 0:12], small[:, 12:14], small[:, 14:16], small[:, 16:18]
        gs = [small[:, 20 + 8 * t:28 + 8 * t] for t in range(TT2)]

        def banks(name, n, shape=(P, HALF)):
            return [ctx.enter_context(nc.psum_tensor(f"{name}{i}", list(shape), F32)) for i in range(n)]

        p_da = banks("p_da", 2)
        p_ht = banks("p_ht", TT2, (P, D))
        p_g = banks("p_g", 2)

        const_loaded, a_done, bias_done = (sem(n) for n in ("const_loaded2", "a_done", "bias2_done"))
        w_loaded = [sem("wz_loaded"), sem("wo_loaded")]
        carry_set, da_zeroed, product_done = sem("carry_set"), sem("da_zeroed"), sem("product_done")
        edge_loaded, edge_arg, edge_done = sem("edge_loaded"), sem("edge_arg"), sem("edge_done")
        bias_loaded = sem("bias2_loaded")
        dt_loaded = [sem(f"dt2_loaded{i}") for i in range(2)]
        y_loaded = [sem(f"y2_loaded{i}") for i in range(2)]
        b_loaded = [sem(f"b2_loaded{i}") for i in range(2)]
        xz_loaded = sem("xz2_loaded")
        x1_loaded = [sem(f"x1_2_loaded{t}") for t in range(TT2)]
        da_done, dbu_done, scan_done, carry_done = (sem(n) for n in ("da_done", "dbu_done", "scan_done", "carry_done"))
        ht_full = [sem(f"ht_full{t}") for t in range(TT2)]
        y_added = [sem(f"y_added{t}") for t in range(TT2)]
        g_full = [sem(f"g_full{i}") for i in range(2)]
        g_free = [sem(f"g_free{i}") for i in range(2)]
        th_done, gate_done = sem("th_done"), sem("gate_done")
        tok_chain, tok_scale, y_scaled, hi_done = (sem(n) for n in ("tok_chain", "tok_scale", "y_scaled", "hi2_done"))
        ln_chain, stats_ready, pow_done, scale_ready, xn_done = (
            sem(n) for n in ("ln2_chain", "stats2_ready", "pow2_done", "scale2_ready", "xn2_done"))
        xb_done, fin_done = sem("xb2_done"), sem("fin_done")
        o_stored = [sem(f"o_stored{i}") for i in range(2)]

        FFN = {0: [("f", 1, 0)], 1: [("f", 1, 1)]}
        OUT = {4: [("t", 0, 0), ("t", 0, 1)], 5: [("o", 0, 0)], 6: [("o", 0, 1)], 7: [("t", 1, 0), ("t", 1, 1)],
               8: [("o", 1, 0)], 9: [("o", 1, 1)], 10: [("n", 0, 0), ("n", 0, 1)], 13: [("f", 0, 0)],
               14: [("f", 0, 1)], 15: [("n", 1, 0), ("n", 1, 1)]}
        ZED = {2: [("z", 0, 0)], 3: [("z", 0, 1)], 11: [("z", 1, 0)], 12: [("z", 1, 1)]}

        def flags(i):
            if isinstance(i, int):
                return 2 <= i, 1 <= i <= C2, i < C2
            return True, True, True

        def sequence(i):
            return [(n, *unit) for n in range(NS) for on, table in zip(flags(i), (FFN, OUT, ZED)) if on
                    for unit in table.get(n, [])]

        def base(i):
            if isinstance(i, int) and i < 2:
                return i * 2
            if isinstance(i, int) and i == C2 + 1:
                return base(C2) + 8
            return (i - 2) * 10 + 11

        def place(i, kind, t, x):
            at = [u[1:] for u in sequence(i)].index((kind, t, x))
            return at % 2, base(i) + at // 2

        def more(i):
            return not (isinstance(i, int) and i >= C2 - 1)

        def odd(ap):
            return ap.rearrange("p n (q two) -> p n q two", two=2)[:, :, :, 1]

        def edge(i):
            return not (isinstance(i, int) and i + 2 >= C2)

        def drive(eng, body, prologue):
            prologue()
            body(0, 0)
            body(1, 1)
            with eng.Fori(0, (C2 - 4) // 2) as turn:
                body(turn * 2 + 2, 0)
                body(turn * 2 + 3, 1)
            for i in range(C2 - 2, C2 + 2):
                body(i, i % 2)

        with nc.Block() as block:
            @block.sync
            def _(sp):
                def load_scan(c, par):
                    wait_alone(sp, y_added[1], (c - 1) * NS)
                    for name, tile in (("dt", dt), ("dtu", dtu)):
                        sp.dma_start(tile[par][:], dram[name][bass.ds(c, 1)].rearrange("c p g t -> p (c g) t")
                                     ).then_inc(dt_loaded[par], 16)
                    with nc.allow_non_contiguous_dma(reason="64 bytes a token"):
                        sp.dma_start(ct[par][:], dram["ct"][bass.ds(c * T2, T2), :].rearrange("(t p) n -> p t n", p=P)
                                     ).then_inc(dt_loaded[par], 16)

                def load_y(c, par):
                    if not (isinstance(c, int) and c < 2):
                        b, m = place(c - 1, "t", 1, 1)
                        wait_alone(sp, g_full[b], m + 1)
                    for t in range(TT2):
                        sp.dma_start(y[par][t][:], dram["y0"][bass.ds(c * T2 + t * P, P), :]).then_inc(y_loaded[par], 16)

                def load_b(c, n):
                    wait_alone(sp, dbu_done, c * NS + n - NB)
                    s = n // NB % 2
                    sp.dma_start(bb[s][:].rearrange("p n t -> p (n t)"),
                                 dram["b"].rearrange("c n t -> c (n t)")[bass.ds(c, 1), n * T2:(n + NB) * T2]
                                 .to_broadcast([P, NB * T2])).then_inc(b_loaded[s], 16)

                def load_xz(c):
                    if not (isinstance(c, int) and c == 0):
                        b, m = place(c - 1, "z", 1, 1)
                        wait_alone(sp, g_full[b], m + 1)
                    for a in range(2):
                        sp.dma_start(xz[:, a].rearrange("p k t -> p (k t)"),
                                     dram["xz"][bass.ds(c, 1), a].rearrange("c p n -> p (c n)")).then_inc(xz_loaded, 16)

                def load_x1(c, t):
                    wait_alone(sp, fin_done, ((c - 1) * TT2 + t + 1) * 2)
                    sp.dma_start(x1[t][:], dram["x1"][bass.ds(c * T2 + t * P, P), :]).then_inc(x1_loaded[t], 16)

                def load_edge(c):
                    wait_alone(sp, edge_arg, c - 1)
                    if not (isinstance(c, int) and c < 2):
                        sp.wait_ge(edge_arg, 1)
                    with nc.allow_non_contiguous_dma(reason="a column"):
                        sp.dma_start(edge_dt[:, 0, :], dram["dt"][bass.ds(c, 1)].rearrange(
                            "c p (q two) t -> p (c q) two t", two=2)[:, :, 1, 0]).then_inc(edge_loaded, 16)

                def load_w(k):
                    sp.dma_start((wz, wo)[k][:].rearrange("p a k m -> p (a k m)"), split_dram[k]).then_inc(w_loaded[k], 16)

                def prologue():
                    with nc.allow_non_contiguous_dma(reason="constants"):
                        sp.dma_start(neg_a[:], ins["A_log"].rearrange("(g p) n -> p g n", p=P)).then_inc(const_loaded, 16)
                    load_scan(0, 0)
                    load_b(0, 0)
                    load_edge(1)
                    load_y(0, 0)
                    sp.dma_start(half_bias[:], ins["bias"].partition_broadcast(P)).then_inc(bias_loaded, 16)
                    load_xz(0)

                def store(c, t, x):
                    wait_alone(sp, fin_done, (c * TT2 + t) * 2 + x + 1)
                    sp.dma_start(out[bass.ds(c * T2 + t * P, P), x * HALF:(x + 1) * HALF], o[x][:]).then_inc(o_stored[x], 16)

                def body(i, par):
                    e_on, c_on, z_on = flags(i)
                    for n in range(NS):
                        if z_on and n % NB == 0:
                            if n + NB < NS:
                                load_b(i, n + NB)
                            elif more(i):
                                load_b(i + 1, 0)
                        if isinstance(i, int) and i == 0 and n in (0, 5):
                            load_w(n // 5)
                        if z_on and more(i) and n == 2:
                            load_scan(i + 1, 1 - par)
                        if z_on and edge(i) and n == 6:
                            load_edge(i + 2)
                        if e_on and n in (1, 6, 7):
                            store(i - 2, *{1: (0, 1), 6: (1, 0), 7: (1, 1)}[n])
                        if c_on and n in (1, 7):
                            load_x1(i - 1, n // 7)
                        if c_on and n == 15:
                            store(i - 1, 0, 0)
                        if z_on and more(i) and n == 9:
                            load_y(i + 1, 1 - par)
                        if z_on and more(i) and n == 14:
                            load_xz(i + 1)

                drive(sp, body, prologue)
                for x in range(2):
                    sp.wait_ge(o_stored[x], 16 * C2 * TT2)

            @block.gpsimd
            def _(pool):
                def edge_argument(c, par):
                    wait(pool, edge_loaded, c * 16)
                    nc.gpsimd.tensor_tensor(odd(factor[par][:]), edge_dt[:].to_broadcast([P, NS, G // 2]),
                                            neg_a[:].rearrange("p (q two) n -> p n q two", two=2)[:, :, :, 1],
                                            ALU.mult).then_inc(edge_arg, 1)

                def prologue():
                    nc.gpsimd.memset(carry[:], 0.0).then_inc(carry_set, 1)
                    for f in factor:
                        nc.gpsimd.memset(f[:], 1.0).then_inc(carry_set, 1)
                    pool.wait_ge(a_done, 2)
                    pool.wait_ge(carry_set, 3)
                    edge_argument(1, 1)

                def times_b(i, par, n):
                    if n == 0:
                        wait(pool, dt_loaded[par], (i - par) * 24 + 48)
                    if n % NB == 0:
                        wait(pool, b_loaded[n // NB % 2], (i * (NS // NB // 2) + n // NB // 2 + 1) * 16)
                    state = dbu[n % 2]
                    for f in range(2):
                        wait(pool, scan_done, i * (NS * 4) + (n - 2) * 4 + 2 * f + 2)
                        nc.gpsimd.tensor_tensor(state[:, 4 * f:4 * f + 4, :], dtu[par][:, 4 * f:4 * f + 4, :],
                                                bb[n // NB % 2][:, n % NB:n % NB + 1, :].to_broadcast([P, G // 2, T2]),
                                                ALU.mult).then_inc(product_done, 1)
                    wait(pool, product_done, (i * NS + n + 1) * 2)
                    wait(pool, carry_done, (i - 1) * NS + n + 1)
                    first = state[:].rearrange("p (q two) t -> p q two t", two=2)[:, :, 1, 0]
                    nc.gpsimd.tensor_tensor(first, first, carry[:, n, :].rearrange("p (q two) -> p q two", two=2)[:, :, 1],
                                            ALU.add).then_inc(dbu_done, 1)

                def keep(c, cpar, n):
                    wait(pool, scan_done, c * (NS * 4) + n * 4 + 4)
                    if n == 0 and not (isinstance(c, int) and c == C2 - 1):
                        wait(pool, edge_done, c + 1)
                    nc.gpsimd.tensor_tensor(carry[:, n, :], h[n % 2][:, :, T2 - 1], factor[1 - cpar][:, n, :],
                                            ALU.mult).then_inc(carry_done, 1)

                def gate(c, cpar, t):
                    wait(pool, y_added[t], c * NS + NS)
                    for x in range(2):
                        b, m = place(c, "z", t, x)
                        wait(pool, g_free[b], m + 1)
                        half = y[cpar][t][:, x * HALF:(x + 1) * HALF]
                        nc.gpsimd.tensor_tensor(half, q[2 * t + x][:], half, ALU.mult).then_inc(gate_done, 1)

                def add_bias(c, t):
                    wait(pool, xn_done, c * TT2 + t + 1)
                    nc.gpsimd.tensor_tensor(x1[t][:], x1[t][:], half_bias[:], ALU.add).then_inc(xb_done, 1)

                def finish(i, c, t, x):
                    b, m = place(i, "f", t, x)
                    wait(pool, g_free[b], m + 1)
                    wait(pool, xb_done, c * TT2 + t + 1)
                    nc.gpsimd.tensor_tensor(o[x][:], o[x][:], x1[t][:, x * HALF:(x + 1) * HALF], ALU.add).then_inc(fin_done, 1)

                def body(i, par):
                    e_on, c_on, z_on = flags(i)
                    for n in range(NS):
                        if z_on:
                            if n >= 2:
                                keep(i, par, n - 2)
                            elif c_on:
                                keep(i - 1, 1 - par, NS - 2 + n)
                            times_b(i, par, n)
                            if edge(i) and n == 8:
                                edge_argument(i + 2, par)
                        if e_on:
                            if n == 1:
                                finish(i - 1, i - 2, 0, 1)
                            if n == 5:
                                add_bias(i - 2, 1)
                            if n in (6, 7):
                                finish(i, i - 2, 1, n - 6)
                        if c_on:
                            if n in (2, 3):
                                gate(i - 1, 1 - par, n - 2)
                            if n in (10, 13):
                                row_scale(pool, nc, vn, consts["minus_half"], sn, stats_ready, pow_done, scale_ready,
                                          xn_done, (i - 1) * TT2 + n // 13)
                            if n == 12:
                                if isinstance(i, int) and i == 1:
                                    pool.wait_ge(bias_done, 1)
                                add_bias(i - 1, 0)
                            if n == 15:
                                finish(i, i - 1, 0, 0)

                drive(pool, body, prologue)

            @block.scalar
            def _(act):
                def prologue():
                    act.wait_ge(const_loaded, 16)
                    nc.scalar.activation(neg_a[:], neg_a[:], ACT.Exp).then_inc(a_done, 1)
                    act.wait_ge(a_done, 1)
                    nc.scalar.mul(neg_a[:], neg_a[:], -1.0).then_inc(a_done, 1)
                    act.wait_ge(a_done, 2)
                    act.wait_ge(da_zeroed, 2)
                    edge_decays(0, 1, 1)

                def edge_decays(m, par, count):
                    wait(act, edge_arg, m + count)
                    nc.scalar.activation(odd(factor[par][:]), odd(factor[par][:]), ACT.Exp).then_inc(edge_done, 1)

                def decays(i, par, n, pairs):
                    if n == 0 and pairs[0] == 0:
                        wait(act, dt_loaded[par], (i - par) * 24 + 48)
                    for p in pairs:
                        wait(act, scan_done, i * (NS * 4) + n * 4 + p - 1)
                        for k in range(2):
                            g = 2 * p + k
                            ins_ = nc.scalar.activation(p_da[p % 2][:, k * T2 + k:(k + 1) * T2], dt[par][:, g, k:], ACT.Exp,
                                                        scale=neg_a[:, g, n:n + 1])
                        ins_.then_inc(da_done, 1)

                def tanh(i, t, x):
                    b, m = place(i, "z", t, x)
                    wait(act, g_full[b], m + 1)
                    wait(act, gate_done, (i - 1) * 4 + 2 * t + 2)
                    nc.scalar.activation(q[2 * t + x][:], p_g[b][:], ACT.Tanh, scale=consts["half_z"]).then_inc(th_done, 1)

                def high(i, kind, t):
                    for x in range(2):
                        b, m = place(i, kind, t, x)
                        wait(act, g_full[b], m + 1)
                        nc.scalar.activation(tokt[:, 0, 4 * x:4 * x + 4, :], p_g[b][:].rearrange("p (g t) -> p g t", g=4),
                                             ACT.Copy).then_inc(hi_done, 1)

                def scale_y(c, cpar, t):
                    wait(act, tok_scale, c * TT2 + t + 1)
                    nc.scalar.activation(y[cpar][t][:], y[cpar][t][:], ACT.Copy, scale=gs[t][:, 3:4]).then_inc(y_scaled, 1)

                def ffn_out(i, c, t, x):
                    b, m = place(i, "f", t, x)
                    wait(act, g_full[b], m + 1)
                    wait(act, o_stored[x], (c * TT2 + t) * 16)
                    nc.scalar.activation(o[x][:], p_g[b][:], ACT.Copy, scale=consts["ffn_scale"]).then_inc(g_free[b], 1)

                def normalise(i, c, t):
                    wait(act, scale_ready, c * TT2 + t + 1)
                    if not (isinstance(i, int) and i == 1 and t == 0):
                        b, m = place(i if t else i - 1, "n", 1 - t, 1)
                        wait(act, g_full[b], m + 1)
                    nc.scalar.activation(xn[:], x1[t][:], ACT.Identity, bias=sn[:, 1:2], scale=sn[:, 0:1]).then_inc(xn_done, 1)

                def body(i, par):
                    e_on, c_on, z_on = flags(i)
                    c = i - 1
                    for n in range(NS):
                        if z_on:
                            decays(i, par, n, (0, 1))
                        if e_on and n in (1, 2):
                            ffn_out(i, i - 2, 1, n - 1)
                        if c_on and n in (14, 15):
                            ffn_out(i, c, 0, n - 14)
                        if c_on and n == 10:
                            normalise(i, c, 0)
                        if z_on and n in (3, 4, 12, 13):
                            tanh(i, n // 12, n - 3 if n < 12 else n - 12)
                        if z_on:
                            decays(i, par, n, (2, 3))
                            if edge(i) and n == 10:
                                edge_decays(i, par, 2)
                            if isinstance(i, int) and i == 0 and n == 0:
                                act.wait_ge(bias_loaded, 16)
                                nc.scalar.mul(half_bias[:], half_bias[:], 0.5).then_inc(bias_done, 1)
                        if c_on:
                            if n in (3, 4):
                                scale_y(c, 1 - par, n - 3)
                            if n in (4, 7):
                                high(i, "t", n // 7)
                            if n in (10, 15):
                                high(i, "n", n // 15)
                            if n == 14:
                                normalise(i, c, 1)

                drive(act, body, prologue)

            @block.vector
            def _(dve):
                def prologue():
                    for b in range(2):
                        nc.vector.memset(p_da[b][:, T2:T2 + 1], 0.0).then_inc(da_zeroed, 1)
                    dve.wait_ge(carry_set, 3)
                    dve.wait_ge(da_zeroed, 2)

                def scans(i, n, half):
                    if half == 0:
                        wait(dve, dbu_done, i * NS + n + 1)
                        wait(dve, carry_done, i * NS + n - 1)
                    for p in range(2 * half, 2 * half + 2):
                        wait(dve, da_done, i * (NS * 4) + n * 4 + p + 1)
                        nc.vector.tensor_tensor_scan(h[n % 2][:, 2 * p:2 * p + 2, :].rearrange("p g t -> p (g t)"), p_da[p % 2][:],
                                                     dbu[n % 2][:, 2 * p:2 * p + 2, :].rearrange("p g t -> p (g t)"),
                                                     carry[:, n, 2 * p:2 * p + 1], ALU.mult, ALU.add).then_inc(scan_done, 1)

                def add_state(c, par, n, t):
                    if n == 0:
                        wait(dve, y_loaded[par], (c - par) * 16 + 32)
                    else:
                        wait(dve, y_added[t], c * NS + n)
                    wait(dve, ht_full[t], c * NS + n + 1)
                    nc.vector.scalar_tensor_tensor(out=y[par][t][:], in0=p_ht[t][:], scalar=ct[par][:, t, n:n + 1],
                                                   in1=y[par][t][:], op0=ALU.mult, op1=ALU.add).then_inc(y_added[t], 1)

                def add_state_before(i, par, n, t):
                    if n and flags(i)[2]:
                        add_state(i, par, n - 1, t)
                    if n == 0 and flags(i)[1]:
                        add_state(i - 1, 1 - par, NS - 1, t)

                def silu_part(i, t, x):
                    b, m = place(i, "z", t, x)
                    wait(dve, th_done, i * 4 + 2 * t + x + 1)
                    nc.vector.scalar_tensor_tensor(out=q[2 * t + x][:], in0=q[2 * t + x][:], scalar=1.0, in1=p_g[b][:],
                                                   op0=ALU.add, op1=ALU.mult).then_inc(g_free[b], 1)

                def low(i, kind, t):
                    before = {("t", 0): 0, ("t", 1): 2, ("n", 0): 4, ("n", 1): 6}[kind, t]
                    for x in range(2):
                        b, m = place(i, kind, t, x)
                        wait(dve, hi_done, (i - 1) * 8 + before + x + 1)
                        nc.vector.tensor_tensor(tokt[:, 1, 4 * x:4 * x + 4, :], p_g[b][:].rearrange("p (g t) -> p g t", g=4),
                                                tokt[:, 0, 4 * x:4 * x + 4, :], ALU.subtract).then_inc(g_free[b], 1)

                def add_product(i, t, x):
                    b, m = place(i, "o", t, x)
                    wait(dve, g_full[b], m + 1)
                    if x == 0:
                        wait(dve, x1_loaded[t], (i - 1) * 16 + 16)
                        wait(dve, tok_scale, (i - 1) * TT2 + t + 1)
                    half = x1[t][:, x * HALF:(x + 1) * HALF]
                    nc.vector.scalar_tensor_tensor(out=half, in0=p_g[b][:], scalar=gs[t][:, 4:5], in1=half,
                                                   op0=ALU.mult, op1=ALU.add).then_inc(g_free[b], 1)

                def token_scale(c, cpar, t):
                    k = (c * TT2 + t) * 4
                    wait(dve, gate_done, c * 4 + 2 * t + 2)
                    nc.vector.tensor_reduce(gs[t][:, 0:1], y[cpar][t][:], AX_X, ALU.max,
                                            apply_absolute_value=True).then_inc(tok_chain, 1)
                    wait(dve, tok_chain, k + 1)
                    nc.vector.tensor_scalar(gs[t][:, 0:1], gs[t][:, 0:1], TINY, None, ALU.max).then_inc(tok_chain, 1)
                    wait(dve, tok_chain, k + 2)
                    nc.vector.tensor_scalar(gs[t][:, 1:2].bitcast(I32), gs[t][:, 0:1].bitcast(I32), EXPONENT, None,
                                            ALU.bitwise_and).then_inc(tok_chain, 1)
                    wait(dve, tok_chain, k + 3)
                    nc.vector.reciprocal(gs[t][:, 2:3], gs[t][:, 1:2]).then_inc(tok_chain, 1)
                    nc.vector.tensor_scalar(gs[t][:, 4:5], gs[t][:, 1:2], consts["out_scale"], 1.0 / WS, ALU.mult, ALU.mult)
                    wait(dve, tok_chain, k + 4)
                    nc.vector.tensor_scalar(gs[t][:, 3:4], gs[t][:, 2:3], WS, None, ALU.mult).then_inc(tok_scale, 1)

                def body(i, par):
                    e_on, c_on, z_on = flags(i)
                    for n in range(NS):
                        if z_on:
                            scans(i, n, 0)
                            if n in (3, 4, 12, 13):
                                silu_part(i, n // 12, n - 3 if n < 12 else n - 12)
                        add_state_before(i, par, n, 0)
                        if c_on and n in (7, 10):
                            add_product(i, n // 10, 1)
                        if z_on:
                            scans(i, n, 1)
                        add_state_before(i, par, n, 1)
                        if c_on and n in (6, 9):
                            add_product(i, n // 9, 0)
                        if c_on:
                            if n in (2, 3):
                                token_scale(i - 1, 1 - par, n - 2)
                            if n in (4, 7):
                                low(i, "t", n // 7)
                            if n in (8, 11):
                                t = n // 11
                                for x in range(2):
                                    b, m = place(i, "o", t, x)
                                    wait(dve, g_free[b], m + 1)
                                row_stats(dve, nc, x1[t], stats, mv, vn, small[:, 40:41], ln_chain, stats_ready,
                                          scale_ready, (i - 1) * TT2 + t)
                            if n in (10, 15):
                                low(i, "n", n // 15)

                drive(dve, body, prologue)

            @block.tensor
            def _(pe):
                def turn_state(c, n):
                    wait(pe, scan_done, c * (NS * 4) + n * 4 + 4)
                    for t in range(TT2):
                        wait(pe, y_added[t], c * NS + n)
                        for g in range(G):
                            mm = nc.tensor.transpose(p_ht[t][:, g * P:(g + 1) * P], h[n % 2][:, g, t * P:(t + 1) * P], ident[:])
                        mm.then_inc(ht_full[t], 1)

                def unit(i, par, kind, t, x):
                    b, m = place(i, kind, t, x)
                    wait(pe, g_free[b], m)
                    cols = slice(x * HALF, (x + 1) * HALF)
                    n = 0
                    if kind in "tn":
                        if kind == "t":
                            src = y[1 - par][t]
                            wait(pe, y_scaled, (i - 1) * TT2 + t + 1)
                        else:
                            src = xn
                            wait(pe, xn_done, (i - 1) * TT2 + t + 1)
                        for k in range(4):
                            g = 4 * x + k
                            mm = nc.tensor.transpose(p_g[b][:, k * P:(k + 1) * P], src[:, g * P:(g + 1) * P], ident[:])
                    if kind == "f":
                        for a in range(2):
                            wait_evac(i - t, "n", t, a)
                        for g in range(G):
                            for a in range(2):
                                mm = nc.tensor.matmul(p_g[b][:], tokt[:, a, g, :], tern[:, g, cols],
                                                      start=(n == 0), stop=(n == 2 * G - 1))
                                n += 1
                    if kind == "o":
                        for a in range(2):
                            wait_evac(i, "t", t, a)
                        if isinstance(i, int) and i == 1:
                            pe.wait_ge(w_loaded[1], 16)
                        for g in range(G):
                            for ta, wa in ((0, 0), (0, 1), (1, 0)):
                                mm = nc.tensor.matmul(p_g[b][:], tokt[:, ta, g, :], wo[:, wa, g, cols],
                                                      start=(n == 0), stop=(n == 3 * G - 1))
                                n += 1
                    if kind == "z":
                        wait(pe, xz_loaded, i * 32 + 32)
                        if isinstance(i, int) and i == 0:
                            pe.wait_ge(w_loaded[0], 16)
                        for g in range(G):
                            for xa, wa in ((0, 0), (0, 1), (1, 0)):
                                mm = nc.tensor.matmul(p_g[b][:], xz[:, xa, g, t * P:(t + 1) * P], wz[:, wa, g, cols],
                                                      start=(n == 0), stop=(n == 3 * G - 1))
                                n += 1
                    mm.then_inc(g_full[b], 1)

                def wait_evac(i, kind, t, a):
                    b, m = place(i, kind, t, a)
                    wait(pe, g_free[b], m + 1)

                def body(i, par):
                    e_on, c_on, z_on = flags(i)
                    seq = sequence(i)
                    for n in range(NS):
                        if n and z_on:
                            turn_state(i, n - 1)
                        if n == 0 and c_on:
                            turn_state(i - 1, NS - 1)
                        for slot, kind, t, x in seq:
                            if slot == n:
                                unit(i, par, kind, t, x)

                drive(pe, body, lambda: None)


def macaron_block(nc, ins, out):
    dram = {
        "x1": nc.dram_tensor("x1_scratch", [L, D], F32, kind="Internal").ap(),
        "xz": nc.dram_tensor("xz_scratch", [C2, 2, P, G * T2], F16, kind="Internal").ap(),
        "y0": nc.dram_tensor("y0_scratch", [L, D], F32, kind="Internal").ap(),
        "dt": nc.dram_tensor("dt_scratch", [C2, P, G, T2], F32, kind="Internal").ap(),
        "dtu": nc.dram_tensor("dtu_scratch", [C2, P, G, T2], F32, kind="Internal").ap(),
        "b": nc.dram_tensor("b_scratch", [C2, NS, T2], F32, kind="Internal").ap(),
        "ct": nc.dram_tensor("ct_scratch", [L, NS], F32, kind="Internal").ap(),
    }
    split = [nc.dram_tensor(f"{n}_split", [P, 2 * G * D], F16, kind="Internal").ap() for n in ("wz", "wo")]
    with ExitStack() as ctx:
        def sem(name):
            return ctx.enter_context(nc.semaphore(name))

        tern = ctx.enter_context(nc.sbuf_tensor("tern", [P, G, D], F16))
        ident = ctx.enter_context(nc.sbuf_tensor("ident", [P, P], F32))
        c = ctx.enter_context(nc.sbuf_tensor("consts", [P, 8], F32))
        consts = {n: c[:, k:k + 1] for k, n in enumerate(("ffn_scale", "u_scale", "half_z", "out_scale", "minus_half"))}
        with nc.sbuf_tensor("wu", [P, 2, G, D], F16) as wu_t:
            first_pass(nc, sem, ins, tern, wu_t[:], consts, ident, split, dram)
        second_pass(nc, sem, ins, tern, consts, ident, split, dram, out)


def kernel(L0_attn_x, L0_attn_W_in, L0_attn_conv_w, L0_attn_conv_b, L0_attn_W_xproj, L0_attn_W_dt, L0_attn_b_dt,
           L0_attn_A_log, L0_attn_Dskip, L0_attn_W_out, L0_ffn_weight, L0_ffn_bias):
    import numpy as np
    import concourse.bacc as bacc
    from concourse.bass_utils import run_bass_kernel_spmd

    arrays = {"x": L0_attn_x.reshape(L, D), "W_ffn": L0_ffn_weight.T, "bias": L0_ffn_bias, "W_in": L0_attn_W_in.T,
              "W_out": L0_attn_W_out.T, "W_xproj": L0_attn_W_xproj.T, "W_dt": L0_attn_W_dt.T,
              "conv_w": L0_attn_conv_w, "conv_b": L0_attn_conv_b, "b_dt": L0_attn_b_dt, "A_log": L0_attn_A_log,
              "Dskip": L0_attn_Dskip}
    arrays = {n: np.ascontiguousarray(a) for n, a in arrays.items()}
    nc = bacc.Bacc("TRN2", target_bir_lowering=False, num_devices=1)
    ins = {n: nc.dram_tensor("in_" + n, list(a.shape), mybir.dt.from_np(a.dtype), kind="ExternalInput").ap()
           for n, a in arrays.items()}
    out = nc.dram_tensor("out", [L, D], F32, kind="ExternalOutput").ap()
    macaron_block(nc, ins, out)
    r = run_bass_kernel_spmd(nc, [{"in_" + n: a for n, a in arrays.items()}], core_ids=[0])
    return r.results[0]["out"].reshape(1, L, D)
```
